# Optimizing a Trainium2 kernel written in Bass

```python
import numpy as np
import jax
import jax.numpy as jnp

def _softmax(x, axis=-1):
    return jax.nn.softmax(x, axis=axis)

def _gelu(x):
    return jax.nn.gelu(x, approximate=True)

def _silu(x):
    return jax.nn.silu(x)

def _sigmoid(x):
    return jax.nn.sigmoid(x)

def _layernorm(x, axis=-1, eps=1e-05):
    m = jnp.mean(x, axis=axis, keepdims=True)
    v = jnp.var(x, axis=axis, keepdims=True)
    return (x - m) / jnp.sqrt(v + eps)

def _scatter_add(tgt, idx, src, axis=0):
    return tgt.at[idx].add(src)

def _segment_sum(src, seg, n):
    return jax.ops.segment_sum(src, seg, n)
kernel_name = 'mk_gnn_preln_d4_gnn_r32_86f18e'

def setup_inputs(seed: int=0):
    np.random.seed(seed)
    _w = jnp.asarray

    def _rec_inputs():
        import jax
        import jax.numpy as jnp
        _gk = jax.random.key(seed)
        x = -0.000202 + 1 * jax.random.normal(jax.random.fold_in(_gk, 1), (50000, 128), jnp.float32)
        src = jax.random.randint(jax.random.fold_in(_gk, 2), (25000,), 0, 50000, jnp.int32)
        dst = jax.random.randint(jax.random.fold_in(_gk, 3), (25000,), 0, 50000, jnp.int32)
        _o = jnp.argsort(dst, stable=True)
        src = src[_o]
        dst = dst[_o]
        edge_attr_8 = 0.000398945 + 1.00003 * jax.random.normal(jax.random.fold_in(_gk, 12), (25000, 8), jnp.float32)
        edge_attr_8_n2 = 0.000398945 + 1.00003 * jax.random.normal(jax.random.fold_in(_gk, 13), (25000, 8), jnp.float32)
        edge_type_8 = jax.random.randint(jax.random.fold_in(_gk, 15), (25000,), 0, 8, jnp.int32)
        edge_weight1 = jax.random.uniform(jax.random.fold_in(_gk, 16), (25000, 1), jnp.float32, 0.0, 1)
        return (x, src, dst, edge_attr_8, edge_attr_8_n2, edge_type_8, edge_weight1)
    x, src, dst, edge_attr_8, edge_attr_8_n2, edge_type_8, edge_weight1 = _rec_inputs()

    def _L0_gnn_setup():
        import jax, jax.numpy as jnp
        import numpy as np
        N_NODES = 50000
        N_EDGES = 25000
        D_MODEL = 128
        N_HEADS = 8
        HEAD_DIM = D_MODEL // N_HEADS
        EPS = 1e-05
        key = jax.random.key(seed)
        ks = jax.random.split(key, 8)
        return {'node_feature': jax.random.normal(ks[0], (N_NODES, D_MODEL), jnp.float32), 'dist_attn': jax.random.normal(ks[1], (N_EDGES, N_HEADS), jnp.float32), 'path_attn': jax.random.normal(ks[2], (N_EDGES, N_HEADS), jnp.float32), 'gamma': jnp.ones((D_MODEL,), jnp.float32), 'beta': jnp.zeros((D_MODEL,), jnp.float32), 'W_qkv': jax.random.normal(ks[3], (3 * D_MODEL, D_MODEL), jnp.float32) * D_MODEL ** (-0.5), 'b_qkv': jnp.zeros((3 * D_MODEL,), jnp.float32), 'W_out': jax.random.normal(ks[4], (D_MODEL, D_MODEL), jnp.float32) * D_MODEL ** (-0.5), 'b_out': jnp.zeros((D_MODEL,), jnp.float32), 'src': jax.random.randint(ks[5], (N_EDGES,), 0, N_NODES, jnp.int32), 'dst': jax.random.randint(ks[6], (N_EDGES,), 0, N_NODES, jnp.int32)}
    _L0_gnn_all = _L0_gnn_setup()
    _L0_gnn_in = {k: v for k, v in _L0_gnn_all.items() if k in ('gamma', 'beta', 'W_qkv', 'b_qkv', 'W_out', 'b_out')}
    del _L0_gnn_all

    def _L1_gnn_setup():
        import jax, jax.numpy as jnp
        import numpy as np
        N_NODES = 3125
        D = 128
        NUM_BLOCKS = 8
        BLOCK_SIZE = 16
        NUM_RELATIONS = 8
        N_EDGES = 15625
        key = jax.random.key(seed)
        k1, k2, k3, k4, k5 = jax.random.split(key, 5)
        x = jax.random.normal(k1, (N_NODES, D), dtype=jnp.float32)
        std = np.sqrt(2.0) / (2 * BLOCK_SIZE)
        blocks = jax.random.normal(k2, (NUM_RELATIONS + 1, NUM_BLOCKS, BLOCK_SIZE, BLOCK_SIZE), dtype=jnp.float32) * std
        source = jax.random.randint(k3, (N_EDGES,), 0, N_NODES, dtype=jnp.int32)
        target = jax.random.randint(k4, (N_EDGES,), 0, N_NODES, dtype=jnp.int32)
        edge_type = jax.random.randint(k5, (N_EDGES,), 0, NUM_RELATIONS, dtype=jnp.int32)
        return {'x': x, 'blocks': blocks, 'source': source, 'target': target, 'edge_type': edge_type}
    _L1_gnn_all = _L1_gnn_setup()
    _L1_gnn_in = {k: v for k, v in _L1_gnn_all.items() if k in ('blocks',)}
    del _L1_gnn_all

    def _L2_gnn_setup():
        import jax, jax.numpy as jnp
        import numpy as np
        N_NODES = 50000
        N_EDGES = 25000
        DIM = 128
        N_HEADS = 8
        HEAD_DIM = DIM // N_HEADS
        key = jax.random.key(seed)
        ks = jax.random.split(key, 12)
        s = 0.02
        return {'h': jax.random.normal(ks[0], (N_NODES, DIM), dtype=jnp.float32), 'src': jax.random.randint(ks[1], (N_EDGES,), 0, N_NODES), 'dst': jax.random.randint(ks[2], (N_EDGES,), 0, N_NODES), 'Wq': jax.random.normal(ks[3], (DIM, DIM), dtype=jnp.float32) * s, 'bq': jax.random.normal(ks[4], (DIM,), dtype=jnp.float32) * s, 'Wk': jax.random.normal(ks[5], (DIM, DIM), dtype=jnp.float32) * s, 'bk': jax.random.normal(ks[6], (DIM,), dtype=jnp.float32) * s, 'Wv': jax.random.normal(ks[7], (DIM, DIM), dtype=jnp.float32) * s, 'bv': jax.random.normal(ks[8], (DIM,), dtype=jnp.float32) * s, 'Wo': jax.random.normal(ks[9], (DIM, DIM), dtype=jnp.float32) * s, 'bo': jax.random.normal(ks[10], (DIM,), dtype=jnp.float32) * s}
    _L2_gnn_all = _L2_gnn_setup()
    _L2_gnn_in = {k: v for k, v in _L2_gnn_all.items() if k in ('Wq', 'bq', 'Wk', 'bk', 'Wv', 'bv', 'Wo', 'bo')}
    del _L2_gnn_all

    def _L3_gnn_setup():
        import jax, jax.numpy as jnp
        import numpy as np
        N_NODES = 50000
        N_EDGES = 18750
        D = 128
        ROUNDS = 2
        key = jax.random.key(seed)
        ks = jax.random.split(key, 6)
        x = jax.random.normal(ks[0], (N_NODES, D), dtype=jnp.float32)
        edge_index = jax.random.randint(ks[1], (2, N_EDGES), 0, N_NODES, dtype=jnp.int32)
        edge_attr = jnp.ones((N_EDGES, 1), dtype=jnp.float32)
        s_msg = 1.0 / np.sqrt(2 * D + 1)
        s_gru = 1.0 / np.sqrt(D)
        msg_W = jax.random.uniform(ks[2], (ROUNDS, D, 2 * D + 1), jnp.float32, -s_msg, s_msg)
        msg_b = jnp.zeros((ROUNDS, D), dtype=jnp.float32)
        gru_Wih = jax.random.uniform(ks[3], (ROUNDS, 3 * D, D), jnp.float32, -s_gru, s_gru)
        gru_Whh = jax.random.uniform(ks[4], (ROUNDS, 3 * D, D), jnp.float32, -s_gru, s_gru)
        gru_bih = jnp.zeros((ROUNDS, 3 * D), dtype=jnp.float32)
        gru_bhh = jnp.zeros((ROUNDS, 3 * D), dtype=jnp.float32)
        return {'x': x, 'edge_index': edge_index, 'edge_attr': edge_attr, 'msg_W': msg_W, 'msg_b': msg_b, 'gru_Wih': gru_Wih, 'gru_Whh': gru_Whh, 'gru_bih': gru_bih, 'gru_bhh': gru_bhh}
    _L3_gnn_all = _L3_gnn_setup()
    _L3_gnn_in = {k: v for k, v in _L3_gnn_all.items() if k in ('msg_W', 'msg_b', 'gru_Wih', 'gru_Whh', 'gru_bih', 'gru_bhh')}
    del _L3_gnn_all
    return {'x': x, 'src': src, 'dst': dst, 'edge_attr_8': edge_attr_8, 'edge_attr_8_n2': edge_attr_8_n2, 'edge_type_8': edge_type_8, 'edge_weight1': edge_weight1, 'L0_gnn_gamma': _L0_gnn_in['gamma'], 'L0_gnn_beta': _L0_gnn_in['beta'], 'L0_gnn_W_qkv': _L0_gnn_in['W_qkv'], 'L0_gnn_b_qkv': _L0_gnn_in['b_qkv'], 'L0_gnn_W_out': _L0_gnn_in['W_out'], 'L0_gnn_b_out': _L0_gnn_in['b_out'], 'L1_gnn_blocks': _L1_gnn_in['blocks'], 'L2_gnn_Wq': _L2_gnn_in['Wq'], 'L2_gnn_bq': _L2_gnn_in['bq'], 'L2_gnn_Wk': _L2_gnn_in['Wk'], 'L2_gnn_bk': _L2_gnn_in['bk'], 'L2_gnn_Wv': _L2_gnn_in['Wv'], 'L2_gnn_bv': _L2_gnn_in['bv'], 'L2_gnn_Wo': _L2_gnn_in['Wo'], 'L2_gnn_bo': _L2_gnn_in['bo'], 'L3_gnn_msg_W': _L3_gnn_in['msg_W'], 'L3_gnn_msg_b': _L3_gnn_in['msg_b'], 'L3_gnn_gru_Wih': _L3_gnn_in['gru_Wih'], 'L3_gnn_gru_Whh': _L3_gnn_in['gru_Whh'], 'L3_gnn_gru_bih': _L3_gnn_in['gru_bih'], 'L3_gnn_gru_bhh': _L3_gnn_in['gru_bhh']}

def reference(x, src, dst, edge_attr_8, edge_attr_8_n2, edge_type_8, edge_weight1, L0_gnn_gamma, L0_gnn_beta, L0_gnn_W_qkv, L0_gnn_b_qkv, L0_gnn_W_out, L0_gnn_b_out, L1_gnn_blocks, L2_gnn_Wq, L2_gnn_bq, L2_gnn_Wk, L2_gnn_bk, L2_gnn_Wv, L2_gnn_bv, L2_gnn_Wo, L2_gnn_bo, L3_gnn_msg_W, L3_gnn_msg_b, L3_gnn_gru_Wih, L3_gnn_gru_Whh, L3_gnn_gru_bih, L3_gnn_gru_bhh):
    import jax
    import jax.numpy as jnp

    def _L0_gnn_ref(node_feature, dist_attn, path_attn, gamma, beta, W_qkv, b_qkv, W_out, b_out, src, dst):
        import jax, jax.numpy as jnp
        import numpy as np
        N_NODES = 50000
        N_EDGES = 25000
        D_MODEL = 128
        N_HEADS = 8
        HEAD_DIM = D_MODEL // N_HEADS
        EPS = 1e-05
        res = node_feature
        mu = jnp.mean(node_feature, axis=-1, keepdims=True)
        var = jnp.var(node_feature, axis=-1, keepdims=True)
        x = (node_feature - mu) * jax.lax.rsqrt(var + EPS) * gamma + beta
        qkv = (x @ W_qkv.T + b_qkv).reshape(-1, 3, N_HEADS, HEAD_DIM)
        q = qkv[:, 0] * D_MODEL ** (-0.5)
        k = qkv[:, 1]
        v = qkv[:, 2]
        node_attn = jnp.einsum('ehd,ehd->eh', q[src], k[dst])
        a = node_attn + dist_attn + path_attn
        m = jax.ops.segment_max(a, dst, num_segments=N_NODES)
        ex = jnp.exp(a - m[dst])
        denom = jax.ops.segment_sum(ex, dst, num_segments=N_NODES)
        sa = ex / denom[dst]
        he = v[src] * sa[:, :, None]
        agg = jax.ops.segment_sum(he, dst, num_segments=N_NODES)
        agg = agg.reshape(-1, D_MODEL)
        out = res + (agg @ W_out.T + b_out)
        return out

    def _L1_gnn_ref(x, blocks, source, target, edge_type):
        import jax, jax.numpy as jnp
        import numpy as np
        N_NODES = 3125
        D = 128
        NUM_BLOCKS = 8
        BLOCK_SIZE = 16
        NUM_RELATIONS = 8
        N_EDGES = 15625
        n, d = x.shape
        r_plus_1, nb, bs, _ = blocks.shape
        num_rel = r_plus_1 - 1
        xb = x.reshape(n, nb, bs)
        out = jnp.einsum('nbi,bij->nbj', xb, blocks[-1]).reshape(n, d)
        xr = jnp.einsum('nbi,rbij->rnbj', xb, blocks[:num_rel]).reshape(num_rel, n, d)
        src2 = jnp.concatenate([source, target])
        tgt2 = jnp.concatenate([target, source])
        et2 = jnp.concatenate([edge_type, edge_type])
        m = xr[et2, src2]
        out = out + jax.ops.segment_sum(m, tgt2, num_segments=n)
        return out

    def _L2_gnn_ref(h, src, dst, Wq, bq, Wk, bk, Wv, bv, Wo, bo):
        import jax, jax.numpy as jnp
        import numpy as np
        N_NODES = 50000
        N_EDGES = 25000
        DIM = 128
        N_HEADS = 8
        HEAD_DIM = DIM // N_HEADS
        n = h.shape[0]
        q = (h @ Wq.T + bq).reshape(n, N_HEADS, HEAD_DIM)
        k = (h @ Wk.T + bk).reshape(n, N_HEADS, HEAD_DIM)
        v = (h @ Wv.T + bv).reshape(n, N_HEADS, HEAD_DIM)
        scores = jnp.einsum('ehd,ehd->eh', q[src], k[dst]) / HEAD_DIM ** 0.5
        m = jax.ops.segment_max(scores, dst, num_segments=n)
        e = jnp.exp(scores - m[dst])
        denom = jax.ops.segment_sum(e, dst, num_segments=n)
        p = e / denom[dst]
        agg = jax.ops.segment_sum(v[src] * p[:, :, None], dst, num_segments=n)
        out = agg.reshape(n, DIM) @ Wo.T + bo
        return out

    def _L3_gnn_ref(x, edge_index, edge_attr, msg_W, msg_b, gru_Wih, gru_Whh, gru_bih, gru_bhh):
        import jax, jax.numpy as jnp
        import numpy as np
        N_NODES = 50000
        N_EDGES = 18750
        D = 128
        ROUNDS = 2
        'GraphProp.forward: ROUNDS of edge message passing + GRU node update.'
        n_nodes = x.shape[0]
        row, col = (edge_index[0], edge_index[1])
        for t in range(msg_W.shape[0]):
            m_in = jnp.concatenate([x[col], x[row], edge_attr], axis=1)
            messages = m_in @ msg_W[t].T + msg_b[t]
            agg = jax.ops.segment_sum(messages, row, num_segments=n_nodes)
            gi = agg @ gru_Wih[t].T + gru_bih[t]
            gh = x @ gru_Whh[t].T + gru_bhh[t]
            ir, iz, in_ = jnp.split(gi, 3, axis=1)
            hr, hz, hn = jnp.split(gh, 3, axis=1)
            r = jax.nn.sigmoid(ir + hr)
            z = jax.nn.sigmoid(iz + hz)
            n = jnp.tanh(in_ + r * hn)
            x = (1.0 - z) * n + z * x
        return x
    edge_index = jnp.stack([src, dst])
    h = jnp.maximum(_layernorm(x, axis=-1), 0.0)
    x = x + _L0_gnn_ref(h, edge_attr_8, edge_attr_8_n2, L0_gnn_gamma, L0_gnn_beta, L0_gnn_W_qkv, L0_gnn_b_qkv, L0_gnn_W_out, L0_gnn_b_out, src, dst)
    h = jnp.maximum(_layernorm(x, axis=-1), 0.0)
    x = x + _L1_gnn_ref(h, L1_gnn_blocks, src, dst, edge_type_8)
    h = jnp.maximum(_layernorm(x, axis=-1), 0.0)
    x = x + _L2_gnn_ref(h, src, dst, L2_gnn_Wq, L2_gnn_bq, L2_gnn_Wk, L2_gnn_bk, L2_gnn_Wv, L2_gnn_bv, L2_gnn_Wo, L2_gnn_bo)
    h = jnp.maximum(_layernorm(x, axis=-1), 0.0)
    x = x + _L3_gnn_ref(h, edge_index, edge_weight1, L3_gnn_msg_W, L3_gnn_msg_b, L3_gnn_gru_Wih, L3_gnn_gru_Whh, L3_gnn_gru_bih, L3_gnn_gru_bhh)
    return x

_drawn_inputs = setup_inputs


def setup_inputs(seed=0):
    import zlib

    import numpy as np

    out = dict(_drawn_inputs(seed))
    spreads = {'L0_gnn_gamma': (1.0, 0.2),
     'L0_gnn_beta': (0.0, 0.1),
     'L0_gnn_b_qkv': (0.0, 0.1),
     'L0_gnn_b_out': (0.0, 0.1),
     'L3_gnn_msg_b': (0.0, 0.59),
     'L3_gnn_gru_bih': (0.0, 0.27),
     'L3_gnn_gru_bhh': (0.0, 0.461)}
    factors = {'edge_weight1': 48.02,
     'L2_gnn_Wq': 8.0,
     'L2_gnn_bq': 64.0,
     'L2_gnn_Wk': 8.0,
     'L2_gnn_bk': 64.0,
     'L2_gnn_Wv': 4.017,
     'L2_gnn_bv': 8.0,
     'L2_gnn_Wo': 4.22,
     'L2_gnn_bo': 4.38}
    for name, (base, spread) in spreads.items():
        noise = np.random.default_rng([zlib.crc32(name.encode()), seed]).standard_normal(out[name].shape)
        drawn = base * np.exp(spread * noise) if base else spread * noise
        out[name] = jnp.asarray(drawn.astype(out[name].dtype))
    for name, factor in factors.items():
        out[name] = (out[name] * factor).astype(out[name].dtype)
    return out
```

```python
from contextlib import ExitStack

import numpy as np
import concourse.bass as bass
from concourse import mybir
from concourse.alu_op_type import AluOpType as ALU

F32, BF16, I32 = mybir.dt.float32, mybir.dt.bfloat16, mybir.dt.int32
ACT = mybir.ActivationFunctionType
AXX = mybir.AxisListType.X

NODES, EDGES, D, HEADS = 50000, 25000, 128, 8
HD = D // HEADS
P = 128
RELS = 8
EPS = 1e-5
BIG = 1e30

C = EDGES // 125
EP = EDGES // C
REC = 4 + HEADS
KEY_SRC, KEY_DST, TYPE, WEIGHT, ATTN = 0, 1, 2, 3, 4
BUCKETS = 256

PAD_NODE = NODES
FIX = NODES + P
FIX_DUMMY = FIX + 2 * P
DUMMY = FIX_DUMMY + 2 * P
ROWS = DUMMY + P * C
SUMW = D + 2

G = 4
BLOCK = P * G
BLOCKS = -(-NODES // BLOCK)
TAIL = BLOCKS - 1
TAIL_P = (NODES - TAIL * BLOCK) // G


class Group:
    pass


def ds(i, n=1):
    return bass.ds(i, n)


def wait(eng, sem, value):
    if not isinstance(value, int) or value > 0:
        eng.wait_ge(sem, value)


def spread(ap, axis, n):
    shape = list(ap.shape)
    shape[axis] = n
    return ap.broadcast_to(shape)


class Phase:

    def __init__(self, nc, name):
        self.nc, self.name, self.stack = nc, name, ExitStack()

    def __enter__(self):
        self.stack.enter_context(self.nc.cleanup_on_exit())
        self.gate = self.sem("gate")
        return self

    def __exit__(self, *said):
        self.stack.__exit__(*said)
        self.nc.all_engine_barrier()

    def sb(self, name, shape, dt=F32):
        return self.nc.alloc_sbuf_tensor(f"{self.name}_{name}", shape, dt)

    def ps(self, name, shape):
        parts, free = shape[0], shape[1:]
        size = int(np.prod(free))
        whole = self.nc.alloc_psum_tensor(f"{self.name}_{name}", [P, -(-size // 512) * 512], F32)
        used = whole[0:parts, 0:size]
        return used if len(free) == 1 else used.rearrange("p (a b) -> p a b", b=free[-1])

    def sem(self, name):
        return self.nc.alloc_semaphore(f"{self.name}_{name}")

    def held(self, eng, sem, value):
        wait(eng, sem, value)
        if not isinstance(value, int):
            eng.sem_inc(self.gate, 1)


def pipeline(eng, n, stages, unroll, alike=None):
    last = max(lag for lag, _ in stages)
    first = -(-(last + unroll) // unroll) * unroll
    turns = ((alike or n) - first) // unroll

    def tick(t):
        for lag, stage in stages:
            if 0 <= t - lag < n:
                stage(t - lag, (t - lag) % unroll, (t - lag) // unroll)

    for t in range(first):
        tick(t)
    with eng.Fori(0, turns) as turn:
        for u in range(unroll):
            for lag, stage in stages:
                at = first + u - lag
                stage(turn * unroll + at, at % unroll, turn + at // unroll)
    for t in range(first + turns * unroll, n + last):
        tick(t)


class Chain:

    def __init__(self, eng, sem):
        self.eng, self.sem, self.n = eng, sem, 0

    def __call__(self, instruction):
        self.n += 1
        instruction.then_inc(self.sem, 1)
        self.eng.wait_ge(self.sem, self.n)


def block_rows(table, i, width=D, at=0, rows=NODES):
    if isinstance(i, int) and i == TAIL:
        return table[TAIL * BLOCK:NODES, :].rearrange("(p a g) d -> p a (g d)", g=G, a=1)
    whole = table[0:TAIL * BLOCK, :].rearrange("(i p g) d -> p i (g d)", p=P, g=G)
    return whole[:, ds(i), :]


def block_tile(tile, s, i):
    n = TAIL_P if isinstance(i, int) and i == TAIL else P
    return tile[0:n, s:s + 1, :, :].rearrange("p s g d -> p s (g d)")


def prepare(nc, k, A):
    with Phase(nc, "prep") as ph:
        NT = 24
        stage = ph.sb("stage", [P, NT, D])
        wb_col = ph.sb("wb_col", [P, 2, 2])
        iota_i = ph.sb("iota_i", [P, BUCKETS], I32)
        dummy_i = ph.sb("dummy_i", [P, C], I32)
        fix_i = ph.sb("fix_i", [P, 4], I32)
        ends = [ph.sb(f"end{j}", [P, C], I32) for j in range(3)]
        dist = ph.sb("dist", [P, C, HEADS])
        path = ph.sb("path", [P, C, HEADS])
        weight = ph.sb("weight", [P, C])
        brow = ph.sb("brow", [1, 4, 512])
        bres = ph.sb("bres", [1, 4, 512])
        bparts = ph.sb("bparts", [1, 3, 4, 512], BF16)
        zero = ph.sb("zero", [P, 41 * D])
        turned = [ph.ps(f"turned{j}", [P, D]) for j in range(4)]
        loads, cleared, made, sent = ph.sem("loads"), ph.sem("cleared"), ph.sem("made"), ph.sem("sent")
        w_in, w_turned, w_kept, v_step = ph.sem("w_in"), ph.sem("w_turned"), ph.sem("w_kept"), ph.sem("v_step")
        parts_ready, zeroed = ph.sem("parts_ready"), ph.sem("zeroed")

        tiles = [(A["L0_gnn_W_qkv"][j * D:(j + 1) * D, :], k.l0.w[:, o:o + D]) for j, o in ((0, 0), (1, 256), (2, 128))]
        tiles += [(A["L0_gnn_W_out"], k.l0.wo[:, :])]
        tiles += [(w, k.l2.w[:, o:o + D]) for w, o in ((A["L2_gnn_Wq"], 0), (A["L2_gnn_Wk"], 256), (A["L2_gnn_Wv"], 128))]
        tiles += [(A["L2_gnn_Wo"], k.l2.wo[:, :])]
        for r in range(2):
            tiles += [(A["L3_gnn_msg_W"][r, :, j * D:(j + 1) * D], k.msg[:, r, j, :]) for j in range(2)]
            tiles += [(A["L3_gnn_gru_Wih"][r, j * D:(j + 1) * D, :], k.wih[:, r, j * D:(j + 1) * D]) for j in range(3)]
            tiles += [(A["L3_gnn_gru_Whh"][r, j * D:(j + 1) * D, :], k.whh[:, r, j * D:(j + 1) * D]) for j in range(3)]
        assert len(tiles) == NT
        row = lambda a: a.rearrange("(o n) -> o n", o=1)
        n_loads = 6 + 6 + 4 + 3 + 3 + HEADS
        with nc.Block() as block:
            @block.sync
            def _(sp):
                for t, (src, _) in enumerate(tiles):
                    sp.dma_start(stage[:, t, :], src).then_inc(w_in, 16)
                with nc.allow_non_contiguous_dma(reason="columns of 128 single elements, once"):
                    for r in range(2):
                        sp.dma_start(wb_col[:, r, 0:1], A["L3_gnn_msg_W"][r, :, 2 * D:2 * D + 1]).then_inc(w_in, 16)
                        sp.dma_start(wb_col[:, r, 1:2], A["L3_gnn_msg_b"][r, :].rearrange("(n o) -> n o", o=1)).then_inc(w_in, 16)
                sp.wait_ge(cleared, 1)
                for dst, src in (
                    (brow[:, 0, 0:D], row(A["L0_gnn_b_qkv"][0:D])), (brow[:, 0, 256:384], row(A["L0_gnn_b_qkv"][D:2 * D])),
                    (brow[:, 0, D:256], row(A["L0_gnn_b_qkv"][2 * D:3 * D])),
                    (brow[:, 1, 0:D], row(A["L2_gnn_bq"])), (brow[:, 1, 256:384], row(A["L2_gnn_bk"])),
                    (brow[:, 1, D:256], row(A["L2_gnn_bv"])),
                ):
                    sp.dma_start(dst, src).then_inc(loads, 16)
                for r in range(2):
                    sp.dma_start(brow[:, 2 + r, 0:384], A["L3_gnn_gru_bih"][r:r + 1, :]).then_inc(loads, 16)
                    sp.dma_start(brow[:, 2 + r, 384:512], A["L3_gnn_gru_bhh"][r:r + 1, 2 * D:3 * D]).then_inc(loads, 16)
                    sp.dma_start(bres[:, 2 + r, 0:256], A["L3_gnn_gru_bhh"][r:r + 1, 0:2 * D]).then_inc(loads, 16)
                for dst, src in ((k.gamma, A["L0_gnn_gamma"]), (k.beta, A["L0_gnn_beta"]), (k.b_out, A["L0_gnn_b_out"]),
                                 (k.bo, A["L2_gnn_bo"])):
                    sp.dma_start(dst[:, :], spread(row(src), 0, P)).then_inc(loads, 16)
                for j, src in enumerate((A["src"], A["dst"], A["edge_type_8"])):
                    sp.dma_start(ends[j][0:EP, :], src.rearrange("(p c) -> p c", c=C)).then_inc(loads, 16)
                sp.dma_start(weight[0:EP, :], A["edge_weight1"].rearrange("(p c) o -> p (c o)", c=C)).then_inc(loads, 16)
                sp.dma_start(dist[0:EP, :, :], A["edge_attr_8"].rearrange("(p c) h -> p c h", c=C)).then_inc(loads, 16)
                sp.dma_start(path[0:EP, :, :], A["edge_attr_8_n2"].rearrange("(p c) h -> p c h", c=C)).then_inc(loads, 16)
                for b in range(HEADS):
                    sp.dma_start(k.rel[b * HD:(b + 1) * HD, :, b * HD:(b + 1) * HD],
                                 A["L1_gnn_blocks"][:, b, :, :].rearrange("r i j -> i r j")).then_inc(loads, 16)
                sp.wait_ge(parts_ready, 1)
                for j in range(3):
                    sp.dma_start(k.bias3[j:j + 1, :, :], bparts[:, j, :, :]).then_inc(sent, 16)
                sp.wait_ge(sent, 48)

            @block.gpsimd
            def _(pool):
                pool.memset(k.ident[:, :], 0.0)
                pool.memset(k.identb[:, :], 0.0)
                pool.memset(k.before[:, :], 1.0)
                pool.memset(k.below[:, :], 0.0)
                pool.memset(k.ones[:, :], 1.0)
                pool.memset(k.onesb[:, :], 1.0)
                pool.memset(zero[:, :], 0.0)
                pool.memset(k.eps[:, :], EPS)
                pool.memset(bres[:, :, :], 0.0)
                pool.memset(brow[:, :, :], 0.0)
                pool.memset(k.rel[:, :, :], 0.0)
                for e in ends:
                    pool.memset(e[:, :], PAD_NODE)
                pool.memset(weight[:, :], 0.0)
                pool.memset(dist[:, :, :], 0.0)
                pool.memset(path[:, :, :], 0.0).then_inc(cleared, 1)
                pool.wait_ge(cleared, 1)
                for m in (k.ident, k.identb):
                    pool.affine_select(out=m[:, :], in_=m[:, :], compare_op=ALU.not_equal, fill=1.0, base=0,
                                       pattern=[[-1, P]], channel_multiplier=1)
                pool.affine_select(out=k.before[:, :], in_=k.before[:, :], compare_op=ALU.is_ge, fill=0.0, base=-1,
                                   pattern=[[1, P]], channel_multiplier=-1)
                pool.affine_select(out=k.below[:, :], in_=k.below[:, :], compare_op=ALU.not_equal, fill=1.0, base=-1,
                                   pattern=[[-1, P]], channel_multiplier=1)
                pool.iota(iota_i[:, :], pattern=[[1, BUCKETS]], base=0, channel_multiplier=0)
                pool.iota(dummy_i[:, :], pattern=[[1, C]], base=DUMMY, channel_multiplier=C)
                pool.iota(fix_i[:, :], pattern=[[P, 4]], base=FIX, channel_multiplier=1).then_inc(made, 1)

            @block.scalar
            def _(act):
                act.wait_ge(cleared, 1)
                flat = lambda t, a, n: t[a:a + n, :].rearrange("(p r) d -> p (r d)", p=P)
                x_rest = flat(k.x, NODES, ROWS - NODES)
                piece = 41 * D
                for j in range((ROWS - NODES) // P // 41):
                    act.dma_start(x_rest[:, j * piece:(j + 1) * piece], zero[:, :]).then_inc(zeroed, 16)
                for t in (k.xn, k.h):
                    act.dma_start(flat(t, NODES, P), zero[:, 0:D]).then_inc(zeroed, 16)
                rows = -(-FIX_DUMMY // P)
                sums = flat(k.sums, 0, rows * P)
                n_sum = 0
                for j in range(0, rows, 40):
                    w = min(40, rows - j) * SUMW
                    act.dma_start(sums[:, j * SUMW:j * SUMW + w], zero[:, 0:w]).then_inc(zeroed, 16)
                    n_sum += 1
                for t, (_, dst) in enumerate(tiles):
                    act.wait_ge(w_turned, t + 1)
                    act.copy(dst, turned[t % 4][:, :]).then_inc(w_kept, 1)
                for r in range(2):
                    act.wait_ge(w_turned, NT + r + 1)
                    act.copy(k.wb[:, r, :], turned[(NT + r) % 4][0:2, :]).then_inc(w_kept, 1)
                act.wait_ge(zeroed, 16 * ((ROWS - NODES) // P // 41 + 2 + n_sum))

            @block.tensor
            def _(pe):
                pe.wait_ge(made, 1)
                pe.wait_ge(w_in, 16 * (NT + 4))
                for t in range(NT):
                    wait(pe, w_kept, t - 3)
                    pe.transpose(turned[t % 4][:, :], stage[:, t, :], k.ident[:, :]).then_inc(w_turned, 1)
                for r in range(2):
                    t = NT + r
                    pe.wait_ge(w_kept, t - 3)
                    pe.transpose(turned[t % 4][0:2, :], wb_col[:, r, :], k.ident[:, :]).then_inc(w_turned, 1)

            @block.vector
            def _(dve):
                link = Chain(dve, v_step)
                dve.wait_ge(loads, 16 * n_loads)
                dve.wait_ge(made, 1)
                nc.vector.tensor_copy(k.iota[:, :], iota_i[:, :])
                nc.vector.tensor_copy(k.dummy[:, :], dummy_i[:, :])
                nc.vector.tensor_copy(k.fix[:, :], fix_i[:, :])
                for j in range(3):
                    nc.vector.tensor_copy(k.rec0[:, :, j], ends[j][:, :])
                nc.vector.tensor_copy(k.rec0[:, :, WEIGHT], weight[:, :])
                nc.vector.tensor_tensor(k.rec0[:, :, ATTN:REC], dist[:, :, :], path[:, :, :], ALU.add)
                link(nc.vector.tensor_tensor(brow[:, :, :], brow[:, :, :], bres[:, :, :], ALU.add))
                for j in range(3):
                    link(nc.vector.tensor_copy(bparts[:, j, :, :], brow[:, :, :]))
                    link(nc.vector.tensor_tensor(brow[:, :, :], brow[:, :, :], bparts[:, j, :, :], ALU.subtract))
                nc.vector.tensor_copy(k.selfw[:, :], k.rel[:, RELS, :]).then_inc(parts_ready, 1)


def sort_pass(nc, k, name, rec_in, rec_table, rec_out, key, shift):
    with Phase(nc, name) as ph:
        U = 4
        key_i = ph.sb("key_i", [P, C], I32)
        digit_i = ph.sb("digit_i", [P, C], I32)
        digit = ph.sb("digit", [P, C])
        hit = ph.sb("hit", [P, U, BUCKETS], BF16)
        own = ph.sb("own", [P, BUCKETS], BF16)
        zeros = ph.sb("zeros", [P, BUCKETS])
        total = ph.sb("total", [P, BUCKETS])
        start = ph.sb("start", [P, BUCKETS])
        picked = ph.sb("picked", [P, 2, BUCKETS])
        place = ph.sb("place", [P, U, 1])
        place_i = ph.sb("place_i", [P, U, 1], I32)
        row = ph.sb("row", [P, U, REC])
        counts = ph.ps("counts", [P, BUCKETS])
        totals = ph.ps("totals", [P, BUCKETS])
        cursor = ph.ps("cursor", [P, BUCKETS])
        v_step, digits_ready = ph.sem("v_step"), ph.sem("digits_ready")
        hit_ready, counted, counts_kept = ph.sem("hit_ready"), ph.sem("counted"), ph.sem("counts_kept")
        totals_ready, start_ready = ph.sem("totals_ready"), ph.sem("start_ready")
        cursor_ready, picked_ready, place_ready = ph.sem("cursor_ready"), ph.sem("picked_ready"), ph.sem("place_ready")
        again_ready, row_ready, loaded = ph.sem("again_ready"), ph.sem("row_ready"), ph.sem("loaded")
        stored = [ph.sem(f"stored{u}") for u in range(U)]

        with nc.Block() as block:
            @block.vector
            def _(dve):
                link = Chain(dve, v_step)
                nc.vector.memset(zeros[:, :], 0.0)
                link(nc.vector.tensor_copy(key_i[:, :], rec_in[:, :, key]))
                if shift:
                    link(nc.vector.tensor_scalar(digit_i[:, :], key_i[:, :], shift, None, ALU.logical_shift_right))
                else:
                    link(nc.vector.tensor_scalar(digit_i[:, :], key_i[:, :], BUCKETS - 1, None, ALU.bitwise_and))
                link(nc.vector.tensor_copy(digit[:, :], digit_i[:, :]))

                def hits(c, u, turn):
                    wait(dve, counted, c - U + 1)
                    nc.vector.tensor_scalar(hit[:, u, :], k.iota[:, :], digit[:, ds(c)], None, ALU.is_equal)\
                        .then_inc(hit_ready, 1)

                pipeline(dve, C, [(0, hits)], U)
                dve.wait_ge(counted, C)
                nc.vector.tensor_copy(own[:, :], counts[:, :]).then_inc(counts_kept, 1)
                dve.wait_ge(totals_ready, 1)
                link(nc.vector.tensor_copy(total[:, :], totals[:, :]))
                link(nc.vector.tensor_tensor_scan(start[:, :], zeros[:, :], total[:, :], 0.0, ALU.add, ALU.add))
                nc.vector.tensor_tensor(start[:, :], start[:, :], total[:, :], ALU.subtract).then_inc(start_ready, 1)

                def hits_again(c, u, turn):
                    wait(dve, cursor_ready, c - U + 2)
                    nc.vector.tensor_scalar(hit[:, u, :], k.iota[:, :], digit[:, ds(c)], None, ALU.is_equal)\
                        .then_inc(again_ready, 1)

                def places(c, u, turn):
                    wait(dve, again_ready, c + 1)
                    wait(dve, cursor_ready, c + 1)
                    nc.vector.tensor_tensor_reduce(out=picked[:, u % 2, :], in0=cursor[:, :], in1=hit[:, u, :],
                                                   scale=1.0, scalar=0.0, op0=ALU.mult, op1=ALU.add,
                                                   accum_out=place[:, u, :]).then_inc(picked_ready, 1)

                def places_int(c, u, turn):
                    wait(dve, picked_ready, c + 1)
                    wait(dve, stored[u], 16 * turn)
                    nc.vector.tensor_copy(place_i[:, u, :], place[:, u, :]).then_inc(place_ready, 1)

                pipeline(dve, C, [(0, hits_again), (1, places), (2, places_int)], U)

            @block.tensor
            def _(pe):
                def count(c, u, turn):
                    wait(pe, hit_ready, c + 1)
                    first = isinstance(c, int) and c == 0
                    pe.matmul(counts[:, :], k.identb[:, :], hit[:, u, :], start=first, stop=False,
                              skip_group_check=True).then_inc(counted, 1)

                pipeline(pe, C, [(0, count)], U)
                pe.wait_ge(counts_kept, 1)
                pe.matmul(totals[:, :], k.onesb[:, :], own[:, :], start=True, stop=True).then_inc(totals_ready, 1)
                pe.wait_ge(start_ready, 1)
                pe.matmul(cursor[:, :], k.before[:, :], own[:, :], start=True, stop=False, skip_group_check=True)
                pe.matmul(cursor[:, :], k.ident[:, :], start[:, :], start=False, stop=False,
                          skip_group_check=True).then_inc(cursor_ready, 1)

                def advance(c, u, turn):
                    wait(pe, picked_ready, c + 1)
                    pe.matmul(cursor[:, :], k.identb[:, :], hit[:, u, :], start=False, stop=False,
                              skip_group_check=True).then_inc(cursor_ready, 1)

                pipeline(pe, C, [(0, advance)], U)

            @block.scalar
            def _(act):
                def record(c, u, turn):
                    ph.held(act, stored[u], 16 * turn)
                    act.copy(row[:, u:u + 1, :], rec_in[:, ds(c), :]).then_inc(row_ready, 1)

                pipeline(act, C, [(0, record)], U)
                for u in range(U):
                    act.wait_ge(stored[u], 16 * C // U)
                act.dma_start(rec_out[:, :, :], rec_table[:, :].rearrange("(p c) w -> p c w", c=C)).then_inc(loaded, 16)
                act.wait_ge(loaded, 16)

            @block.gpsimd
            def _(pool):
                def store(c, u, turn):
                    ph.held(pool, row_ready, c + 1)
                    ph.held(pool, place_ready, c + 1)
                    pool.indirect_dma_start(rec_table, bass.IndirectOffsetOnAxis(ap=place_i[:, u, :], axis=0),
                                            row[:, u, :], None).then_inc(stored[u], 16)

                pipeline(pool, C, [(0, store)], U)


def order_masks(nc, k, name, o):
    with Phase(nc, name) as ph:
        key = o.rec[:, :, o.key]
        f_first = ph.sb("t0", [P, C])
        t1 = ph.sb("t1", [P, C])
        t2 = ph.sb("t2", [P, C])
        kdiag = ph.sb("kdiag", [P, 2, P])
        kwide = ph.sb("kwide", [P, 2, HEADS])
        nextk = ph.sb("nextk", [P, 2])
        own = ph.sb("own", [P, 2])
        kseq = ph.sb("kseq", [HEADS, P, 2])
        ktile = ph.sb("ktile", [P, 2, 1])
        kb = ph.ps("kb", [P, 2, P])
        kn = ph.ps("kn", [P, 2])
        ks = ph.ps("ks", [HEADS, 2, P])
        v_step, keys_ready, keys_wide = ph.sem("v_step"), ph.sem("keys_ready"), ph.sem("keys_wide")

        with nc.Block() as block:
            @block.vector
            def _(dve):
                link = Chain(dve, v_step)
                k0, k1 = ktile[:, 0, :], ktile[:, 1, :]
                link(nc.vector.tensor_copy(ktile[:, 0, :], o.rec[:, 0, o.key:o.key + 1]))
                link(nc.vector.tensor_copy(ktile[:, 1, :], o.rec[:, C - 1, o.key:o.key + 1]))
                for j in range(2):
                    nc.vector.tensor_scalar(kdiag[:, j, :], k.ident[:, :], ktile[:, j, :], None, ALU.mult)
                    last = nc.vector.tensor_scalar(kwide[:, j, :], k.ones[:, 0:HEADS], ktile[:, j, :], None, ALU.mult)
                last.then_inc(keys_ready, 1)
                nc.vector.memset(o.same[:, 0:1], 0.0)
                nc.vector.memset(o.notlast[:, C - 1:C], 0.0)
                nc.vector.tensor_tensor(o.same[:, 1:C], key[:, 1:C], key[:, 0:C - 1], ALU.is_equal)
                link(nc.vector.tensor_tensor(o.notlast[:, 0:C - 1], key[:, 1:C], key[:, 0:C - 1], ALU.is_equal))
                nc.vector.tensor_scalar(o.last[:, :], o.notlast[:, :], -1.0, 1.0, ALU.mult, ALU.add)
                nc.vector.tensor_scalar(o.pen[:, :], o.same[:, :], 1.0, BIG, ALU.subtract, ALU.mult)
                nc.vector.tensor_scalar(o.first[:, :], key, k0, None, ALU.is_equal)
                link(nc.vector.tensor_scalar(t1[:, :], key, k1, None, ALU.is_equal))
                link(nc.vector.tensor_tensor(t2[:, :], t1[:, :], o.first[:, :], ALU.mult))
                link(nc.vector.tensor_tensor(o.final[:, :], t1[:, :], t2[:, :], ALU.subtract))
                link(nc.vector.tensor_tensor(t1[:, :], o.first[:, :], o.final[:, :], ALU.add))
                link(nc.vector.tensor_scalar(o.middle[:, :], t1[:, :], -1.0, 1.0, ALU.mult, ALU.add))
                link(nc.vector.tensor_tensor(t1[:, :], key, o.middle[:, :], ALU.mult))
                link(nc.vector.scalar_tensor_tensor(t2[:, :], o.first[:, :], k.fix[:, 0:1], t1[:, :], ALU.mult, ALU.add))
                link(nc.vector.scalar_tensor_tensor(t1[:, :], o.final[:, :], k.fix[:, 1:2], t2[:, :], ALU.mult, ALU.add))
                link(nc.vector.tensor_tensor(t2[:, :], t1[:, :], o.last[:, :], ALU.mult))
                link(nc.vector.tensor_tensor(t1[:, :], k.dummy[:, :], o.notlast[:, :], ALU.mult))
                link(nc.vector.tensor_tensor(o.target[:, :], t1[:, :], t2[:, :], ALU.add))
                dve.wait_ge(keys_wide, 1)
                for a in range(2):
                    for b in range(2):
                        nc.vector.tensor_scalar(o.join[:, a, b, :], kb[:, b, :], ktile[:, a, :], None, ALU.is_equal)
                nc.vector.tensor_copy(nextk[:, 0:1], k1)
                link(nc.vector.tensor_copy(nextk[:, 1:2], kn[:, 0:1]))
                nc.vector.tensor_tensor(o.split[:, :], k0, k1, ALU.not_equal)
                nc.vector.tensor_tensor(own[:, 0:1], k0, k1, ALU.not_equal)
                link(nc.vector.tensor_tensor(own[:, 1:2], k1, nextk[:, 1:2], ALU.not_equal))
                link(nc.vector.tensor_tensor(t1[:, 0:2], ktile[:, :, 0], k.fix[:, 2:4], ALU.subtract))
                link(nc.vector.tensor_tensor(t2[:, 0:2], t1[:, 0:2], own[:, :], ALU.mult))
                link(nc.vector.tensor_tensor(o.fix_target[:, :], t2[:, 0:2], k.fix[:, 2:4], ALU.add))
                for j in range(2):
                    last = nc.vector.tensor_copy(kseq[:, :, j], ks[:, j, :])
                link(last)
                seq = kseq[:, :, :].rearrange("h p j -> h (p j)")
                nc.vector.memset(o.seq_same[:, 0:1], 0.0)
                nc.vector.memset(o.seq_notlast[:, 2 * P - 1:2 * P], 0.0)
                nc.vector.tensor_tensor(o.seq_same[:, 1:2 * P], seq[:, 1:2 * P], seq[:, 0:2 * P - 1], ALU.is_equal)
                link(nc.vector.tensor_tensor(o.seq_notlast[:, 0:2 * P - 1], seq[:, 1:2 * P], seq[:, 0:2 * P - 1],
                                             ALU.is_equal))
                nc.vector.tensor_scalar(o.seq_last[:, :], o.seq_notlast[:, :], -1.0, 1.0, ALU.mult, ALU.add)
                link(nc.vector.tensor_scalar(o.seq_pen[:, :], o.seq_same[:, :], 1.0, BIG, ALU.subtract, ALU.mult))
                nc.vector.tensor_copy(o.tail[:, :, 0], o.rec[:, :, WEIGHT])
                nc.vector.memset(o.tail[:, :, 1], 1.0)
                link(nc.vector.tensor_copy(o.ends[:, :, :], o.rec[:, :, KEY_SRC:KEY_DST + 1]))

            @block.tensor
            def _(pe):
                pe.wait_ge(keys_ready, 1)
                for j in range(2):
                    pe.matmul(kb[:, j, :], k.ones[:, :], kdiag[:, j, :], start=True, stop=True)
                    pe.matmul(ks[:, j, :], kwide[:, j, :], k.ident[:, :], start=True, stop=True)
                pe.matmul(kn[:, 0:1], k.below[:, :], ktile[:, 0, :], start=True, stop=True).then_inc(keys_wide, 1)


def dense_stats(nc, ph, dve, m, s, i, rows):
    for g in range(G):
        last = nc.vector.bn_stats(m.stats[:, s, g, :], rows[:, g, :])
    last.then_inc(m.stats_done, 1)
    ph.held(dve, m.stats_done, i + 1)
    for g in range(G):
        last = nc.vector.bn_aggr(m.moments[:, s, g, :], m.stats[:, s, g, :])
    last.then_inc(m.moments_done, 1)


def row_roots(act, k, m, s, i):
    wait(act, m.moments_done, i + 1)
    act.activation(m.root[:, s, :], m.moments[:, s, :, 1], ACT.Sqrt, bias=k.eps[:, :]).then_inc(m.root_done, 1)


def row_scales(nc, dve, m, s, i):
    wait(dve, m.root_done, i + 1)
    nc.vector.reciprocal(m.scale[:, s, :], m.root[:, s, :]).then_inc(m.scale_done, 1)
    wait(dve, m.scale_done, i + 1)
    nc.vector.scalar_tensor_tensor(m.shift[:, s, :], m.moments[:, s, :, 0], -1.0, m.scale[:, s, :],
                                   ALU.mult, ALU.mult).then_inc(m.ready, 1)


def moments_of(ph, name, slots, g=G):
    m = Group()
    m.stats, m.moments = ph.sb(name + "_stats", [P, slots, g, 6]), ph.sb(name + "_moments", [P, slots, g, 2])
    m.root, m.scale = ph.sb(name + "_root", [P, slots, g]), ph.sb(name + "_scale", [P, slots, g])
    m.shift = ph.sb(name + "_shift", [P, slots, g])
    m.stats_done, m.moments_done = ph.sem(name + "_stats_done"), ph.sem(name + "_moments_done")
    m.root_done, m.scale_done, m.ready = ph.sem(name + "_root_done"), ph.sem(name + "_scale_done"), ph.sem(name + "_ready")
    return m


def first_norm(nc, k, A):
    with Phase(nc, "norm0") as ph:
        U = 2
        x = ph.sb("x", [P, U, G, D])
        h = ph.sb("h", [P, U, G, D])
        xn = ph.sb("xn", [P, U, G, D])
        xo = ph.sb("xo", [P, U, G, D])
        mx, mh = moments_of(ph, "mx", U), moments_of(ph, "mh", U)
        x_in = [ph.sem(f"x_in{u}") for u in range(U)]
        out_x = [ph.sem(f"out_x{u}") for u in range(U)]
        out_n = [ph.sem(f"out_n{u}") for u in range(U)]
        h_done, n_done, scaled, xn_ready = ph.sem("h_done"), ph.sem("n_done"), ph.sem("scaled"), ph.sem("xn_ready")
        summed, xo_ready = ph.sem("summed"), ph.sem("xo_ready")
        wide = lambda row: spread(row[:, :].rearrange("p (g d) -> p g d", g=1), 1, G)

        with nc.Block() as block:
            @block.sync
            def _(sp):
                def load(i, s, turn):
                    wait(sp, summed, i - U + 1)
                    sp.dma_start(block_tile(x, s, i), block_rows(A["x"], i)).then_inc(x_in[s], 16)

                def store(i, s, turn):
                    wait(sp, xo_ready, i + 1)
                    sp.dma_start(block_rows(k.x, i), block_tile(xo, s, i)).then_inc(out_x[s], 16)

                pipeline(sp, BLOCKS, [(0, load), (2, store)], U, TAIL)
                for s in range(U):
                    sp.wait_ge(out_x[s], 16 * (BLOCKS // U))

            @block.vector
            def _(dve):
                def x_stats(i, s, turn):
                    wait(dve, x_in[s], 16 * (turn + 1))
                    dense_stats(nc, ph, dve, mx, s, i, x[:, s])

                def x_scales(i, s, turn):
                    row_scales(nc, dve, mx, s, i)

                def h_scales(i, s, turn):
                    row_scales(nc, dve, mh, s, i)

                def h_stats(i, s, turn):
                    wait(dve, h_done, i + 1)
                    wait(dve, out_x[s], 16 * turn)
                    nc.vector.tensor_tensor(xo[:, s], x[:, s], h[:, s], ALU.add).then_inc(summed, 1)
                    dense_stats(nc, ph, dve, mh, s, i, h[:, s])
                    wait(dve, summed, i + 1)
                    nc.vector.tensor_tensor(xo[:, s], xo[:, s], wide(k.b_out), ALU.add).then_inc(xo_ready, 1)

                def affine(i, s, turn):
                    wait(dve, n_done, i + 1)
                    nc.vector.tensor_tensor(xn[:, s], xn[:, s], wide(k.gamma), ALU.mult).then_inc(scaled, 1)
                    wait(dve, scaled, i + 1)
                    nc.vector.tensor_tensor(xn[:, s], xn[:, s], wide(k.beta), ALU.add).then_inc(xn_ready, 1)

                pipeline(dve, BLOCKS, [(0, x_stats), (0, x_scales), (1, h_stats), (1, h_scales), (2, affine)], U, TAIL)

            @block.scalar
            def _(act):
                def relu(i, s, turn):
                    wait(act, n_done, i - U + 1)
                    wait(act, xo_ready, i - U + 1)
                    wait(act, mx.ready, i + 1)
                    for g in range(G):
                        last = act.activation(h[:, s, g, :], x[:, s, g, :], ACT.Relu,
                                              bias=mx.shift[:, s, g:g + 1], scale=mx.scale[:, s, g:g + 1])
                    last.then_inc(h_done, 1)

                def norm(i, s, turn):
                    wait(act, out_n[s], 16 * turn)
                    wait(act, mh.ready, i + 1)
                    for g in range(G):
                        last = act.activation(xn[:, s, g, :], h[:, s, g, :], ACT.Identity,
                                              bias=mh.shift[:, s, g:g + 1], scale=mh.scale[:, s, g:g + 1])
                    last.then_inc(n_done, 1)

                def x_roots(i, s, turn):
                    row_roots(act, k, mx, s, i)

                def h_roots(i, s, turn):
                    row_roots(act, k, mh, s, i)

                pipeline(act, BLOCKS, [(0, x_roots), (0, relu), (1, h_roots), (1, norm)], U, TAIL)

            @block.gpsimd
            def _(pool):
                def store(i, s, turn):
                    wait(pool, xn_ready, i + 1)
                    pool.sem_inc(ph.gate, 1)
                    pool.dma_start(block_rows(k.xn, i), block_tile(xn, s, i)).then_inc(out_n[s], 16)

                pipeline(pool, BLOCKS, [(0, store)], U, TAIL)
                for s in range(U):
                    pool.wait_ge(out_n[s], 16 * (BLOCKS // U))


def edge_scores(nc, k, name, o, table, L, normed):
    with Phase(nc, name) as ph:
        U = 4
        idx = ph.sb("idx", [P, U, 2], I32)
        rows = [[ph.sb(f"rows{u}{j}", [P, D]) for j in range(2)] for u in range(U)]
        act_rows = ph.sb("act_rows", [P, 2, 2, D]) if normed else None
        turned_sb = ph.sb("turned_sb", [P, 2, 2, D])
        k_sb = ph.sb("k_sb", [P, 2, D])
        prod = ph.sb("prod", [P, 2, D])
        turned = [ph.ps(f"turned{j}", [P, 2, D]) for j in range(2)]
        qvk = [ph.ps(f"qvk{j}", [P, 512]) for j in range(2)]
        idx_ready, turned_ready, turned_kept = ph.sem("idx_ready"), ph.sem("turned_ready"), ph.sem("turned_kept")
        qvk_ready, kv_kept, prod_ready, scores_done = ph.sem("qvk_ready"), ph.sem("kv_kept"), ph.sem("prod_ready"), ph.sem("scores_done")
        gathered = [ph.sem(f"gathered{u}") for u in range(U)]
        relu_done = ph.sem("relu_done")
        m = moments_of(ph, "m", 2, 2) if normed else None

        with nc.Block() as block:
            @block.gpsimd
            def _(pool):
                def gather(c, u, turn):
                    ph.held(pool, idx_ready, c + 1)
                    ph.held(pool, relu_done if normed else turned_ready, c - U + 1)
                    for j in range(2):
                        pool.indirect_dma_start(rows[u][j][:, :], None, table,
                                                bass.IndirectOffsetOnAxis(ap=idx[:, u, j:j + 1], axis=0))\
                            .then_inc(gathered[u], 16)

                pipeline(pool, C, [(0, gather)], U)

            @block.vector
            def _(dve):
                def index(c, u, turn):
                    ph.held(dve, gathered[u], 32 * turn)
                    nc.vector.tensor_copy(idx[:, u:u + 1, :], o.ends[:, ds(c), :]).then_inc(idx_ready, 1)

                def moments(c, u, turn):
                    s = u % 2
                    wait(dve, gathered[u], 32 * (turn + 1))
                    for j in range(2):
                        last = nc.vector.bn_stats(m.stats[:, s, j, :], rows[u][j][:, :])
                    last.then_inc(m.stats_done, 1)
                    ph.held(dve, m.stats_done, c + 1)
                    for j in range(2):
                        last = nc.vector.bn_aggr(m.moments[:, s, j, :], m.stats[:, s, j, :])
                    last.then_inc(m.moments_done, 1)

                def scales(c, u, turn):
                    wait(dve, relu_done, c - 1)
                    row_scales(nc, dve, m, u % 2, c)

                def product(c, u, turn):
                    s = u % 2
                    wait(dve, kv_kept, c + 1)
                    wait(dve, scores_done, c - 1)
                    nc.vector.tensor_tensor(prod[:, s, :], qvk[s][:, 0:D], k_sb[:, s, :], ALU.mult)\
                        .then_inc(prod_ready, 1)

                def head_sums(c, u, turn):
                    s = u % 2
                    ph.held(dve, prod_ready, c + 1)
                    nc.vector.tensor_reduce(k.att[:, :, ds(c)], prod[:, s, :].rearrange("p (h e) -> p h e", e=HD),
                                            axis=AXX, op=ALU.add).then_inc(scores_done, 1)

                stages = [(0, index)] + ([(1, moments), (2, scales)] if normed else [])
                stages += [(5, product), (6, head_sums)] if normed else [(3, product), (4, head_sums)]
                pipeline(dve, C, stages, U)

            @block.tensor
            def _(pe):
                def turn_rows(c, u, turn):
                    s = u % 2
                    wait(pe, turned_kept, c - 1)
                    if normed:
                        wait(pe, relu_done, c + 1)
                    else:
                        wait(pe, gathered[u], 32 * (turn + 1))
                    for j in range(2):
                        src = act_rows[:, s, j, :] if normed else rows[u][j][:, :]
                        last = pe.transpose(turned[s][:, j, :], src, k.ident[:, :])
                    last.then_inc(turned_ready, 1)

                def project(c, u, turn):
                    s = u % 2
                    wait(pe, turned_kept, c + 1)
                    wait(pe, prod_ready, c - 1)
                    pe.matmul(qvk[s][:, 0:384], k.onesb[0:3, :], k.bias3[:, L.bias, 0:384], start=True, stop=False)
                    pe.matmul(qvk[s][:, 0:256], turned_sb[:, s, 0, :], L.w[:, 0:256], start=False, stop=False)
                    pe.matmul(qvk[s][:, 256:384], turned_sb[:, s, 1, :], L.w[:, 256:384], start=False, stop=True)\
                        .then_inc(qvk_ready, 1)

                pipeline(pe, C, [(0, turn_rows), (1, project)], U)

            @block.scalar
            def _(act):
                def relu(c, u, turn):
                    s = u % 2
                    wait(act, turned_ready, c - 1)
                    wait(act, m.ready, c + 1)
                    for j in range(2):
                        last = act.activation(act_rows[:, s, j, :], rows[u][j][:, :], ACT.Relu,
                                              bias=m.shift[:, s, j:j + 1], scale=m.scale[:, s, j:j + 1])
                    last.then_inc(relu_done, 1)

                def keep_turned(c, u, turn):
                    s = u % 2
                    wait(act, turned_ready, c + 1)
                    wait(act, qvk_ready, c - 1)
                    act.copy(turned_sb[:, s, :, :], turned[s][:, :, :]).then_inc(turned_kept, 1)

                def keep_kv(c, u, turn):
                    s = u % 2
                    ph.held(act, qvk_ready, c + 1)
                    ph.held(act, prod_ready, c - 1)
                    act.copy(k_sb[:, s, :], qvk[s][:, 256:384])
                    act.copy(k.edge_v[:, ds(c), :], qvk[s][:, 128:256].rearrange("p (o d) -> p o d", o=1))\
                        .then_inc(kv_kept, 1)

                def roots(c, u, turn):
                    row_roots(act, k, m, u % 2, c)

                stages = [(0, roots), (1, relu), (2, keep_turned), (3, keep_kv)] if normed else \
                    [(1, keep_turned), (2, keep_kv)]
                pipeline(act, C, stages, U)


def segment_softmax(nc, k, name, o, scale, biased):
    with Phase(nc, name) as ph:
        a = k.att
        run = ph.sb("run", [P, HEADS, C])
        tmp = ph.sb("tmp", [P, HEADS, C])
        low = ph.sb("low", [P, 1])
        part = ph.sb("part", [P, 2, HEADS])
        total = ph.sb("total", [P, 2, HEADS])
        seq = ph.sb("seq", [HEADS, P, 2])
        seq_run = ph.sb("seq_run", [HEADS, 2 * P])
        seq_end = ph.sb("seq_end", [HEADS, 2 * P])
        seq_tot = ph.sb("seq_tot", [HEADS, 2 * P])
        seq_half = ph.sb("seq_half", [HEADS, 2, P])
        wide = ph.ps("wide", [HEADS, 2, P])
        tall = ph.ps("tall", [P, 2, HEADS])
        v_step, part_ready, wide_ready = ph.sem("v_step"), ph.sem("part_ready"), ph.sem("wide_ready")
        seq_ready, tall_ready, shifted, exps = ph.sem("seq_ready"), ph.sem("tall_ready"), ph.sem("shifted"), ph.sem("exps")
        per_head = lambda mask: spread(mask[:, :].rearrange("p (h c) -> p h c", h=1), 1, HEADS)
        V = nc.vector

        with nc.Block() as block:
            @block.vector
            def _(dve):
                link = Chain(dve, v_step)
                if biased:
                    attn = o.rec[:, :, ATTN:REC].rearrange("p c h -> p h c")
                    link(V.tensor_scalar(tmp[:, :, :], a[:, :, :], scale, None, ALU.mult))
                    link(V.tensor_tensor(a[:, :, :], tmp[:, :, :], attn, ALU.add))
                else:
                    link(V.tensor_scalar(a[:, :, :], a[:, :, :], scale, None, ALU.mult))

                def over_segments(step, state_in, state_op, value_op, start):
                    for h in range(HEADS):
                        last = V.tensor_tensor_scan(run[:, h, :], state_in[:, :], a[:, h, :], start, state_op, value_op)
                    link(last)
                    link(V.tensor_tensor(tmp[:, :, :], run[:, :, :], per_head(o.last), ALU.mult))
                    for h in range(HEADS):
                        last = V.tensor_tensor_scan(run[:, h, ::-1], o.notlast[:, ::-1], tmp[:, h, ::-1], 0.0,
                                                    ALU.mult, ALU.add)
                    link(last)
                    V.tensor_copy(part[:, 0, :], run[:, :, 0])
                    if state_op == ALU.mult:
                        last = V.tensor_scalar(part[:, 1, :], run[:, :, C - 1], o.split[:, :], None, ALU.mult)
                    else:
                        last = V.tensor_copy(part[:, 1, :], run[:, :, C - 1])
                    last.then_inc(part_ready, 1)
                    dve.wait_ge(wide_ready, step)
                    for j in range(2):
                        last = V.tensor_copy(seq[:, :, j], wide[:, j, :])
                    link(last)
                    seq_in = o.seq_pen if state_op == ALU.add else o.seq_same
                    link(V.tensor_tensor_scan(seq_run[:, :], seq_in[:, :], seq[:, :, :].rearrange("h p j -> h (p j)"),
                                              start, state_op, value_op))
                    link(V.tensor_tensor(seq_end[:, :], seq_run[:, :], o.seq_last[:, :], ALU.mult))
                    link(V.tensor_tensor_scan(seq_tot[:, ::-1], o.seq_notlast[:, ::-1], seq_end[:, ::-1], 0.0,
                                              ALU.mult, ALU.add))
                    V.tensor_copy(seq_half[:, :, :], seq_tot[:, :].rearrange("h (p j) -> h j p", j=2)).then_inc(seq_ready, 1)
                    dve.wait_ge(tall_ready, step)
                    link(V.tensor_copy(total[:, :, :], tall[:, :, :]))
                    link(V.tensor_tensor(run[:, :, :], run[:, :, :], per_head(o.middle), ALU.mult))
                    for mask, j in ((o.first, 0), (o.final, 1)):
                        for h in range(HEADS):
                            last = V.scalar_tensor_tensor(run[:, h, :], mask[:, :], total[:, j, h:h + 1], run[:, h, :],
                                                          ALU.mult, ALU.add)
                        link(last)

                over_segments(1, o.pen, ALU.add, ALU.max, -BIG)
                V.tensor_tensor(a[:, :, :], a[:, :, :], run[:, :, :], ALU.subtract).then_inc(shifted, 1)
                dve.wait_ge(exps, 1)
                over_segments(2, o.same, ALU.mult, ALU.add, 0.0)
                link(V.reciprocal(tmp[:, :, :], run[:, :, :]))
                link(V.tensor_tensor(a[:, :, :], a[:, :, :], tmp[:, :, :], ALU.mult))

            @block.scalar
            def _(act):
                act.wait_ge(shifted, 1)
                act.activation(a[:, :, :], a[:, :, :], ACT.Exp).then_inc(exps, 1)

            @block.tensor
            def _(pe):
                for step in (1, 2):
                    pe.wait_ge(part_ready, step)
                    for j in range(2):
                        last = pe.transpose(wide[:, j, :], part[:, j, :], k.ident[:, :])
                    last.then_inc(wide_ready, 1)
                    pe.wait_ge(seq_ready, step)
                    for j in range(2):
                        last = pe.transpose(tall[:, j, :], seq_half[:, j, :], k.ident[0:HEADS, 0:HEADS])
                    last.then_inc(tall_ready, 1)


def add_attention(nc, k, name, o, wo):
    with Phase(nc, name) as ph:
        U = 4
        idx = ph.sb("idx", [P, U, 1], I32)
        value = ph.sb("value", [P, U, D])
        state = ph.sb("state", [P, U, D])
        turned_sb = ph.sb("turned_sb", [P, 2, D])
        out = ph.sb("out", [P, U, D])
        turned = [ph.ps(f"turned{j}", [P, D]) for j in range(2)]
        mixed = [ph.ps(f"mixed{j}", [P, D]) for j in range(2)]
        idx_ready, value_ready, state_ready = ph.sem("idx_ready"), ph.sem("value_ready"), ph.sem("state_ready")
        turned_ready, turned_kept, mixed_ready, out_ready = ph.sem("turned_ready"), ph.sem("turned_kept"), ph.sem("mixed_ready"), ph.sem("out_ready")
        added = [ph.sem(f"added{u}") for u in range(U)]
        state_init = ph.sem("state_init")

        with nc.Block() as block:
            @block.vector
            def _(dve):
                nc.vector.memset(state[:, U - 1, :], 0.0).then_inc(state_init, 1)
                dve.wait_ge(state_init, 1)

                def weigh(c, u, turn):
                    ph.held(dve, added[u], 16 * turn)
                    nc.vector.tensor_copy(idx[:, u:u + 1, :], o.target[:, ds(c)].rearrange("p (a c) -> p a c", a=1))\
                        .then_inc(idx_ready, 1)
                    v = k.edge_v[:, ds(c), :].rearrange("p c (h e) -> p (c h) e", e=HD)
                    nc.vector.tensor_tensor(value[:, u, :].rearrange("p (h e) -> p h e", e=HD), v,
                                            spread(k.att[:, :, ds(c)], 2, HD), ALU.mult).then_inc(value_ready, 1)

                def accumulate(c, u, turn):
                    wait(dve, value_ready, c + 1)
                    wait(dve, turned_ready, c - U + 1)
                    wait(dve, state_ready, c)
                    nc.vector.scalar_tensor_tensor(state[:, u, :], state[:, (u - 1) % U, :], o.same[:, ds(c)],
                                                   value[:, u, :], ALU.mult, ALU.add).then_inc(state_ready, 1)

                pipeline(dve, C, [(0, weigh), (1, accumulate)], U)

            @block.tensor
            def _(pe):
                def turn_sums(c, u, turn):
                    wait(pe, state_ready, c + 1)
                    wait(pe, turned_kept, c - 1)
                    pe.transpose(turned[u % 2][:, :], state[:, u, :], k.ident[:, :]).then_inc(turned_ready, 1)

                def mix(c, u, turn):
                    wait(pe, turned_kept, c + 1)
                    wait(pe, out_ready, c - 1)
                    pe.matmul(mixed[u % 2][:, :], turned_sb[:, u % 2, :], wo[:, :], start=True, stop=True)\
                        .then_inc(mixed_ready, 1)

                pipeline(pe, C, [(0, turn_sums), (1, mix)], U)

            @block.scalar
            def _(act):
                def keep_turned(c, u, turn):
                    wait(act, turned_ready, c + 1)
                    wait(act, mixed_ready, c - 1)
                    act.copy(turned_sb[:, u % 2, :], turned[u % 2][:, :]).then_inc(turned_kept, 1)

                def keep_out(c, u, turn):
                    wait(act, mixed_ready, c + 1)
                    wait(act, added[u], 16 * turn)
                    act.copy(out[:, u, :], mixed[u % 2][:, :]).then_inc(out_ready, 1)

                pipeline(act, C, [(0, keep_turned), (1, keep_out)], U)

            @block.gpsimd
            def _(pool):
                def add(c, u, turn):
                    ph.held(pool, idx_ready, c + 1)
                    ph.held(pool, out_ready, c + 1)
                    pool.indirect_dma_start(k.x, bass.IndirectOffsetOnAxis(ap=idx[:, u, :], axis=0), out[:, u, :],
                                            None, compute_op=ALU.add).then_inc(added[u], 16)

                pipeline(pool, C, [(0, add)], U)
                for u in range(U):
                    pool.wait_ge(added[u], 16 * C // U)


def join_parts(nc, k, name, o, table, width, adding):
    with Phase(nc, name) as ph:
        part = ph.sb("part", [P, 2, width])
        out = [ph.sb(f"out{j}", [P, width]) for j in range(2)]
        zero = ph.sb("zero", [P, 2 * width])
        idx = ph.sb("idx", [P, 2], I32)
        total = ph.ps("total", [P, 2, 256])
        loaded, totals, ready, stored, cleared = ph.sem("loaded"), ph.sem("totals"), ph.sem("ready"), ph.sem("stored"), ph.sem("cleared")
        parts = table[FIX:FIX + 2 * P, :].rearrange("(j p) d -> p j d", p=P)

        with nc.Block() as block:
            @block.sync
            def _(sp):
                sp.dma_start(part[:, :, :], parts).then_inc(loaded, 16)
                if adding:
                    sp.wait_ge(loaded, 16)
                    sp.wait_ge(ready, 1)
                    sp.dma_start(parts, zero[:, :].rearrange("p (j d) -> p j d", j=2)).then_inc(cleared, 16)
                    sp.wait_ge(cleared, 16)

            @block.tensor
            def _(pe):
                pe.wait_ge(loaded, 16)
                for b in range(2):
                    for a in range(2):
                        last = pe.matmul(total[:, b, 0:width], o.join[:, a, b, :], part[:, a, :],
                                         start=(a == 0), stop=(a == 1))
                last.then_inc(totals, 1)

            @block.vector
            def _(dve):
                nc.vector.memset(zero[:, :], 0.0)
                nc.vector.tensor_copy(idx[:, :], o.fix_target[:, :]).then_inc(ready, 1)
                dve.wait_ge(totals, 1)
                for j in range(2):
                    nc.vector.tensor_copy(out[j][:, :], total[:, j, 0:width]).then_inc(ready, 1)

            @block.gpsimd
            def _(pool):
                pool.wait_ge(ready, 3)
                for j in range(2):
                    op = dict(compute_op=ALU.add) if adding else {}
                    pool.indirect_dma_start(table, bass.IndirectOffsetOnAxis(ap=idx[:, j:j + 1], axis=0),
                                            out[j][:, :], None, **op).then_inc(stored, 16)
                pool.wait_ge(stored, 32)


def self_relation(nc, k):
    with Phase(nc, "self") as ph:
        U = 2
        x = ph.sb("x", [P, U, G, D])
        h = ph.sb("h", [P, U, G, D])
        xo = ph.sb("xo", [P, U, G, D])
        h_t = ph.sb("h_t", [P, U, G, D])
        m = moments_of(ph, "m", U)
        turned = [ph.ps(f"turned{j}", [P, G, D]) for j in range(U)]
        own = [ph.ps(f"own{j}", [P, G, D]) for j in range(U)]
        x_in = [ph.sem(f"x_in{u}") for u in range(U)]
        out_x = [ph.sem(f"out_x{u}") for u in range(U)]
        out_h = [ph.sem(f"out_h{u}") for u in range(U)]
        h_done, turned_ready, turned_kept, own_ready, xo_ready = (ph.sem(n) for n in ("h_done", "turned_ready", "turned_kept", "own_ready", "xo_ready"))

        with nc.Block() as block:
            @block.sync
            def _(sp):
                def load(i, s, turn):
                    wait(sp, xo_ready, i - U + 1)
                    sp.dma_start(block_tile(x, s, i), block_rows(k.x, i)).then_inc(x_in[s], 16)

                def store(i, s, turn):
                    wait(sp, h_done, i + 1)
                    sp.dma_start(block_rows(k.h, i), block_tile(h, s, i)).then_inc(out_h[s], 16)
                    wait(sp, xo_ready, i + 1)
                    sp.dma_start(block_rows(k.x, i), block_tile(xo, s, i)).then_inc(out_x[s], 16)

                pipeline(sp, BLOCKS, [(0, load), (1, store)], U, TAIL)
                for s in range(U):
                    sp.wait_ge(out_x[s], 16 * (BLOCKS // U))
                    sp.wait_ge(out_h[s], 16 * (BLOCKS // U))

            @block.vector
            def _(dve):
                def moments(i, s, turn):
                    wait(dve, x_in[s], 16 * (turn + 1))
                    wait(dve, h_done, i - U + 1)
                    dense_stats(nc, ph, dve, m, s, i, x[:, s])
                    row_scales(nc, dve, m, s, i)

                def add(i, s, turn):
                    wait(dve, own_ready, i + 1)
                    wait(dve, out_x[s], 16 * turn)
                    nc.vector.tensor_tensor(xo[:, s], x[:, s], own[s][:, :, :], ALU.add).then_inc(xo_ready, 1)

                pipeline(dve, BLOCKS, [(0, moments), (1, add)], U, TAIL)

            @block.scalar
            def _(act):
                def relu(i, s, turn):
                    row_roots(act, k, m, s, i)
                    wait(act, turned_ready, i - U + 1)
                    wait(act, out_h[s], 16 * turn)
                    wait(act, m.ready, i + 1)
                    for g in range(G):
                        last = act.activation(h[:, s, g, :], x[:, s, g, :], ACT.Relu,
                                              bias=m.shift[:, s, g:g + 1], scale=m.scale[:, s, g:g + 1])
                    last.then_inc(h_done, 1)

                def keep(i, s, turn):
                    wait(act, turned_ready, i + 1)
                    wait(act, own_ready, i - U + 1)
                    act.copy(h_t[:, s], turned[s][:, :, :]).then_inc(turned_kept, 1)

                pipeline(act, BLOCKS, [(0, relu), (1, keep)], U, TAIL)

            @block.tensor
            def _(pe):
                def turn_rows(i, s, turn):
                    wait(pe, h_done, i + 1)
                    wait(pe, turned_kept, i - U + 1)
                    for g in range(G):
                        last = pe.transpose(turned[s][:, g, :], h[:, s, g, :], k.ident[:, :])
                    last.then_inc(turned_ready, 1)

                def multiply(i, s, turn):
                    wait(pe, turned_kept, i + 1)
                    wait(pe, xo_ready, i - U + 1)
                    for g in range(G):
                        last = pe.matmul(own[s][:, g, :], h_t[:, s, g, :], k.selfw[:, :], start=True, stop=True)
                    last.then_inc(own_ready, 1)

                pipeline(pe, BLOCKS, [(0, turn_rows), (1, multiply)], U, TAIL)


def add_relations(nc, k, name, o, other):
    with Phase(nc, name) as ph:
        U = 4
        idx = ph.sb("idx", [P, U, 1], I32)
        idx_to = ph.sb("idx_to", [P, U, 1], I32)
        rows = [ph.sb(f"rows{u}", [P, D]) for u in range(U)]
        rel = ph.sb("rel", [P, C, RELS])
        turned_sb = ph.sb("turned_sb", [P, 2, D])
        state = ph.sb("state", [P, U, D])
        turned = [ph.ps(f"turned{j}", [P, D]) for j in range(2)]
        each = [ph.ps(f"each{j}", [P, RELS, D]) for j in range(2)]
        idx_ready, to_ready, turned_ready, turned_kept, each_ready = (ph.sem(n) for n in ("idx_ready", "to_ready", "turned_ready", "turned_kept", "each_ready"))
        carried, picked, v_step = ph.sem("carried"), ph.sem("picked"), ph.sem("v_step")
        gathered = [ph.sem(f"gathered{u}") for u in range(U)]
        added = [ph.sem(f"added{u}") for u in range(U)]

        with nc.Block() as block:
            @block.gpsimd
            def _(pool):
                def gather(c, u, turn):
                    ph.held(pool, idx_ready, c + 1)
                    ph.held(pool, turned_ready, c - U + 1)
                    pool.indirect_dma_start(rows[u][:, :], None, k.h,
                                            bass.IndirectOffsetOnAxis(ap=idx[:, u, :], axis=0)).then_inc(gathered[u], 16)

                def add(c, u, turn):
                    ph.held(pool, picked, RELS * (c + 1))
                    ph.held(pool, to_ready, c + 1)
                    pool.indirect_dma_start(k.x, bass.IndirectOffsetOnAxis(ap=idx_to[:, u, :], axis=0), state[:, u, :],
                                            None, compute_op=ALU.add).then_inc(added[u], 16)

                pipeline(pool, C, [(0, gather), (3, add)], U)
                for u in range(U):
                    pool.wait_ge(added[u], 16 * C // U)

            @block.vector
            def _(dve):
                for r in range(RELS):
                    last = nc.vector.tensor_scalar(rel[:, :, r], o.rec[:, :, TYPE], float(r), None, ALU.is_equal)
                nc.vector.memset(state[:, U - 1, :], 0.0).then_inc(v_step, 1)
                dve.wait_ge(v_step, 1)

                def index(c, u, turn):
                    ph.held(dve, gathered[u], 16 * turn)
                    nc.vector.tensor_copy(idx[:, u:u + 1, :], o.ends[:, ds(c), other:other + 1]).then_inc(idx_ready, 1)

                def pick(c, u, turn):
                    s = u % 2
                    wait(dve, added[u], 16 * turn)
                    wait(dve, picked, RELS * c)
                    nc.vector.tensor_scalar(state[:, u, :], state[:, (u - 1) % U, :], o.same[:, ds(c)], None, ALU.mult)\
                        .then_inc(carried, 1)
                    ph.held(dve, carried, c + 1)
                    nc.vector.tensor_copy(idx_to[:, u:u + 1, :], o.target[:, ds(c)].rearrange("p (a c) -> p a c", a=1))\
                        .then_inc(to_ready, 1)
                    wait(dve, each_ready, c + 1)
                    for r in range(RELS):
                        if r:
                            wait(dve, picked, RELS * c + r)
                        nc.vector.scalar_tensor_tensor(state[:, u, :], each[s][:, r, :],
                                                       rel[:, ds(c), r:r + 1].rearrange("p a b -> p (a b)"),
                                                       state[:, u, :], ALU.mult, ALU.add).then_inc(picked, 1)

                pipeline(dve, C, [(0, index), (3, pick)], U)

            @block.scalar
            def _(act):
                def keep(c, u, turn):
                    wait(act, turned_ready, c + 1)
                    wait(act, each_ready, c - 1)
                    act.copy(turned_sb[:, u % 2, :], turned[u % 2][:, :]).then_inc(turned_kept, 1)

                pipeline(act, C, [(0, keep)], U)

            @block.tensor
            def _(pe):
                def turn_rows(c, u, turn):
                    wait(pe, gathered[u], 16 * (turn + 1))
                    wait(pe, turned_kept, c - 1)
                    pe.transpose(turned[u % 2][:, :], rows[u][:, :], k.ident[:, :]).then_inc(turned_ready, 1)

                def multiply(c, u, turn):
                    s = u % 2
                    wait(pe, turned_kept, c + 1)
                    wait(pe, picked, RELS * (c - 1))
                    for j in range(2):
                        last = pe.matmul(each[s][:, 4 * j:4 * j + 4, :], turned_sb[:, s, :],
                                         k.rel[:, 4 * j:4 * j + 4, :], start=True, stop=True)
                    last.then_inc(each_ready, 1)

                pipeline(pe, C, [(0, turn_rows), (1, multiply)], U)


def last_norm(nc, k):
    with Phase(nc, "norm3") as ph:
        U = 2
        x = ph.sb("x", [P, U, G, D])
        h = ph.sb("h", [P, U, G, D])
        xb = ph.sb("xb", [P, U, G, D])
        m = moments_of(ph, "m", U)
        x_in = [ph.sem(f"x_in{u}") for u in range(U)]
        out_h = [ph.sem(f"out_h{u}") for u in range(U)]
        h_done, biased = ph.sem("h_done"), ph.sem("biased")
        bo = spread(k.bo[:, :].rearrange("p (g d) -> p g d", g=1), 1, G)

        with nc.Block() as block:
            @block.sync
            def _(sp):
                def load(i, s, turn):
                    wait(sp, biased, i - U + 1)
                    sp.dma_start(block_tile(x, s, i), block_rows(k.x, i)).then_inc(x_in[s], 16)

                def store(i, s, turn):
                    wait(sp, h_done, i + 1)
                    sp.dma_start(block_rows(k.h, i), block_tile(h, s, i)).then_inc(out_h[s], 16)

                pipeline(sp, BLOCKS, [(0, load), (1, store)], U, TAIL)
                for s in range(U):
                    sp.wait_ge(out_h[s], 16 * (BLOCKS // U))

            @block.vector
            def _(dve):
                def moments(i, s, turn):
                    wait(dve, x_in[s], 16 * (turn + 1))
                    wait(dve, h_done, i - U + 1)
                    nc.vector.tensor_tensor(xb[:, s], x[:, s], bo, ALU.add).then_inc(biased, 1)
                    wait(dve, biased, i + 1)
                    dense_stats(nc, ph, dve, m, s, i, xb[:, s])
                    row_scales(nc, dve, m, s, i)

                pipeline(dve, BLOCKS, [(0, moments)], U, TAIL)

            @block.scalar
            def _(act):
                def relu(i, s, turn):
                    row_roots(act, k, m, s, i)
                    wait(act, out_h[s], 16 * turn)
                    wait(act, m.ready, i + 1)
                    for g in range(G):
                        last = act.activation(h[:, s, g, :], xb[:, s, g, :], ACT.Relu,
                                              bias=m.shift[:, s, g:g + 1], scale=m.scale[:, s, g:g + 1])
                    last.then_inc(h_done, 1)

                pipeline(act, BLOCKS, [(0, relu)], U, TAIL)


def sum_neighbours(nc, k, name, o):
    with Phase(nc, name) as ph:
        U = 4
        idx = ph.sb("idx", [P, U, 1], I32)
        idx_to = ph.sb("idx_to", [P, U, 1], I32)
        rows = [ph.sb(f"rows{u}", [P, D]) for u in range(U)]
        state = ph.sb("state", [P, U, SUMW])
        idx_ready, to_ready, tails, summed, v_step = (ph.sem(n) for n in ("idx_ready", "to_ready", "tails", "summed", "v_step"))
        gathered = [ph.sem(f"gathered{u}") for u in range(U)]
        stored = [ph.sem(f"stored{u}") for u in range(U)]

        with nc.Block() as block:
            @block.gpsimd
            def _(pool):
                def gather(c, u, turn):
                    ph.held(pool, idx_ready, c + 1)
                    ph.held(pool, summed, c - U + 1)
                    pool.indirect_dma_start(rows[u][:, :], None, k.h,
                                            bass.IndirectOffsetOnAxis(ap=idx[:, u, :], axis=0)).then_inc(gathered[u], 16)

                def store(c, u, turn):
                    ph.held(pool, summed, c + 1)
                    ph.held(pool, to_ready, c + 1)
                    pool.indirect_dma_start(k.sums, bass.IndirectOffsetOnAxis(ap=idx_to[:, u, :], axis=0),
                                            state[:, u, :], None).then_inc(stored[u], 16)

                pipeline(pool, C, [(0, gather), (3, store)], U)
                for u in range(U):
                    pool.wait_ge(stored[u], 16 * C // U)

            @block.vector
            def _(dve):
                nc.vector.memset(state[:, U - 1, :], 0.0).then_inc(v_step, 1)
                dve.wait_ge(v_step, 1)

                def index(c, u, turn):
                    ph.held(dve, gathered[u], 16 * turn)
                    nc.vector.tensor_copy(idx[:, u:u + 1, :], o.ends[:, ds(c), 1:2]).then_inc(idx_ready, 1)

                def add(c, u, turn):
                    ph.held(dve, stored[u], 16 * turn)
                    nc.vector.tensor_copy(idx_to[:, u:u + 1, :], o.target[:, ds(c)].rearrange("p (a c) -> p a c", a=1))\
                        .then_inc(to_ready, 1)
                    ph.held(dve, summed, c)
                    same = o.same[:, ds(c)]
                    nc.vector.scalar_tensor_tensor(state[:, u, D:SUMW], state[:, (u - 1) % U, D:SUMW], same,
                                                   o.tail[:, ds(c), :].rearrange("p a b -> p (a b)"),
                                                   ALU.mult, ALU.add)
                    wait(dve, gathered[u], 16 * (turn + 1))
                    nc.vector.scalar_tensor_tensor(state[:, u, 0:D], state[:, (u - 1) % U, 0:D], same, rows[u][:, :],
                                                   ALU.mult, ALU.add).then_inc(summed, 1)

                pipeline(dve, C, [(0, index), (3, add)], U)


def update_nodes(nc, k, A, out, r):
    final = r == 1
    with Phase(nc, f"gru{r}") as ph:
        U = 2
        h = ph.sb("h", [P, U, G, D])
        su = ph.sb("su", [P, U, G, SUMW])
        x = ph.sb("x", [P, U, G, D])
        dh = ph.sb("dh", [P, U, G, D])
        t_sb = ph.sb("t_sb", [P, U, 3, G, D])
        wd_sb = ph.sb("wd_sb", [2, U, G, P])
        agg_sb = ph.sb("agg_sb", [P, U, G, P])
        rz = ph.sb("rz", [P, 2, 2 * D])
        t1 = ph.sb("t1", [P, 2, D])
        t2 = ph.sb("t2", [P, 2, D])
        n = ph.sb("n", [P, 2, D])
        u1 = ph.sb("u1", [P, 2, D])
        u2 = ph.sb("u2", [P, 2, D])
        ho = ph.sb("ho", [P, U, G, D])
        turned = [ph.ps(f"turned{j}", [P, G, P]) for j in range(3)]
        wd = ph.ps("wd", [2, G, P])
        agg = ph.ps("agg", [P, G, P])
        gate = [ph.ps(f"gate{j}", [P, 512]) for j in range(2)]
        h_in = [ph.sem(f"h_in{u}") for u in range(U)]
        h_out = [ph.sem(f"h_out{u}") for u in range(U)]
        scaled, turned_ready, turned_kept, agg_ready, agg_kept, block_done, left = (ph.sem(s) for s in ("scaled", "turned_ready", "turned_kept", "agg_ready", "agg_kept", "block_done", "left"))
        gate_ready, rz_ready, gated, cand_in, cand, diff, weighed, x_sum = (ph.sem(s) for s in ("gate_ready", "rz_ready", "gated", "cand_in", "cand", "diff", "weighed", "x_sum"))
        bo = spread(k.bo[:, :].rearrange("p (g d) -> p g d", g=1), 1, G)
        loads = 3 if final else 2

        with nc.Block() as block:
            @block.sync
            def _(sp):
                def load(i, s, turn):
                    wait(sp, block_done, i - U + 1)
                    sp.dma_start(block_tile(h, s, i), block_rows(k.h, i)).then_inc(h_in[s], 16)
                    sp.dma_start(block_tile(su, s, i), block_rows(k.sums, i, SUMW)).then_inc(h_in[s], 16)
                    if final:
                        sp.dma_start(block_tile(x, s, i), block_rows(k.x, i)).then_inc(h_in[s], 16)

                def store(i, s, turn):
                    wait(sp, block_done, i + 1)
                    sp.dma_start(block_rows(out if final else k.h, i), block_tile(ho, s, i)).then_inc(h_out[s], 16)

                pipeline(sp, BLOCKS, [(0, load), (1, store)], U, TAIL)
                for s in range(U):
                    sp.wait_ge(h_out[s], 16 * (BLOCKS // U))

            @block.vector
            def _(dve):
                def degree(i, s, turn):
                    wait(dve, h_in[s], 16 * loads * (turn + 1))
                    wait(dve, turned_ready, i - U + 1)
                    nc.vector.tensor_tensor(dh[:, s], h[:, s], spread(su[:, s, :, D + 1:D + 2], 2, D), ALU.mult)\
                        .then_inc(scaled, 1)
                    if final:
                        nc.vector.tensor_tensor(x[:, s], x[:, s], bo, ALU.add).then_inc(x_sum, 1)

                def mix(i, s, turn):
                    wait(dve, h_out[s], 16 * turn)
                    for g in range(G):
                        j, q = g % 2, i * G + g
                        wait(dve, rz_ready, q + 1)
                        nc.vector.tensor_tensor(t1[:, j, :], gate[j][:, 384:512], rz[:, j, 0:D], ALU.mult)\
                            .then_inc(gated, 1)
                        wait(dve, gated, q + 1)
                        nc.vector.tensor_tensor(t2[:, j, :], gate[j][:, 256:384], t1[:, j, :], ALU.add)\
                            .then_inc(cand_in, 1)
                        if g:
                            blend(i, s, g - 1)
                    blend(i, s, G - 1)
                    if final:
                        wait(dve, left, G * (i + 1))
                        wait(dve, x_sum, i + 1)
                        nc.vector.tensor_tensor(ho[:, s], ho[:, s], x[:, s], ALU.add).then_inc(block_done, 1)

                def blend(i, s, g):
                    j, q = g % 2, i * G + g
                    wait(dve, cand, q + 1)
                    nc.vector.tensor_tensor(u1[:, j, :], h[:, s, g, :], n[:, j, :], ALU.subtract).then_inc(diff, 1)
                    wait(dve, diff, q + 1)
                    nc.vector.tensor_tensor(u2[:, j, :], u1[:, j, :], rz[:, j, D:2 * D], ALU.mult).then_inc(weighed, 1)
                    wait(dve, weighed, q + 1)
                    last = nc.vector.tensor_tensor(ho[:, s, g, :], u2[:, j, :], n[:, j, :], ALU.add).then_inc(left, 1)
                    if g == G - 1 and not final:
                        wait(dve, left, q + 1)
                        nc.vector.sem_inc(block_done, 1)

                pipeline(dve, BLOCKS, [(0, degree), (1, mix)], U, TAIL)

            @block.tensor
            def _(pe):
                def turn_rows(i, s, turn):
                    wait(pe, scaled, i + 1)
                    wait(pe, turned_kept, 2 * i)
                    for g in range(G):
                        pe.transpose(turned[0][:, g, :], su[:, s, g, 0:D], k.ident[:, :])
                        pe.transpose(turned[1][:, g, :], dh[:, s, g, :], k.ident[:, :])
                        pe.transpose(turned[2][:, g, :], h[:, s, g, :], k.ident[:, :])
                        last = pe.transpose(wd[:, g, :], su[:, s, g, D:SUMW], k.ident[:, :])
                    last.then_inc(turned_ready, 1)

                def aggregate(i, s, turn):
                    wait(pe, turned_kept, 2 * i + 2)
                    wait(pe, agg_kept, i)
                    pe.matmul(agg[:, :, :], k.msg[:, r, 0, :], t_sb[:, s, 0, :, :], start=True, stop=False)
                    pe.matmul(agg[:, :, :], k.msg[:, r, 1, :], t_sb[:, s, 1, :, :], start=False, stop=False)
                    pe.matmul(agg[:, :, :], k.wb[:, r, :], wd_sb[:, s, :, :], start=False, stop=True)\
                        .then_inc(agg_ready, 1)

                def gates(i, s, turn):
                    wait(pe, agg_kept, i + 1)
                    for g in range(G):
                        j, q = g % 2, i * G + g
                        wait(pe, rz_ready, q - 1)
                        wait(pe, cand_in, q - 1)
                        pe.matmul(gate[j][:, :], k.onesb[0:3, :], k.bias3[:, 2 + r, :], start=True, stop=False)
                        pe.matmul(gate[j][:, 0:384], agg_sb[:, s, g, :], k.wih[:, r, :], start=False, stop=False)
                        pe.matmul(gate[j][:, 0:256], t_sb[:, s, 2, g, :], k.whh[:, r, 0:256], start=False, stop=False)
                        pe.matmul(gate[j][:, 384:512], t_sb[:, s, 2, g, :], k.whh[:, r, 256:384], start=False,
                                  stop=True).then_inc(gate_ready, 1)

                pipeline(pe, BLOCKS, [(0, turn_rows), (0, aggregate), (1, gates)], U, TAIL)

            @block.scalar
            def _(act):
                def keep(i, s, turn):
                    wait(act, turned_ready, i + 1)
                    wait(act, gate_ready, G * (i - U + 1))
                    act.copy(t_sb[:, s, 0], turned[0][:, :, :])
                    act.copy(t_sb[:, s, 1], turned[1][:, :, :]).then_inc(turned_kept, 1)
                    act.copy(wd_sb[:, s], wd[:, :, :])
                    act.copy(t_sb[:, s, 2], turned[2][:, :, :]).then_inc(turned_kept, 1)
                    wait(act, agg_ready, i + 1)
                    act.copy(agg_sb[:, s], agg[:, :, :]).then_inc(agg_kept, 1)

                def gates(i, s, turn):
                    for g in range(G):
                        j, q = g % 2, i * G + g
                        wait(act, gate_ready, q + 1)
                        wait(act, weighed, q - 1)
                        act.activation(rz[:, j, :], gate[j][:, 0:256], ACT.Sigmoid).then_inc(rz_ready, 1)
                        if g:
                            candidate(i, g - 1)
                    candidate(i, G - 1)

                def candidate(i, g):
                    j, q = g % 2, i * G + g
                    wait(act, cand_in, q + 1)
                    wait(act, left, q - 1)
                    act.activation(n[:, j, :], t2[:, j, :], ACT.Tanh).then_inc(cand, 1)

                pipeline(act, BLOCKS, [(0, keep), (1, gates)], U, TAIL)


def build(nc, A, out):
    k = Group()
    sb = lambda name, shape, dt=F32: nc.alloc_sbuf_tensor(name, shape, dt)
    table = lambda name, rows, width: nc.dram_tensor(name, (rows, width), F32, kind="Internal").ap()
    k.x, k.h, k.xn = table("x_rows", ROWS, D), table("h_rows", NODES + P, D), table("xn_rows", NODES + P, D)
    k.sums = table("sum_rows", ROWS, SUMW)
    k.edge_table = [table(f"edge_rows{j}", P * C, REC) for j in range(4)]
    k.ident, k.identb = sb("ident", [P, P]), sb("identb", [P, P], BF16)
    k.before, k.below = sb("before", [P, P], BF16), sb("below", [P, P])
    k.ones, k.onesb = sb("ones", [P, P]), sb("onesb", [P, P], BF16)
    k.iota, k.dummy, k.fix = sb("iota", [P, BUCKETS], BF16), sb("dummy_rows", [P, C]), sb("fix", [P, 4])
    k.l0, k.l2 = Group(), Group()
    k.l0.w, k.l0.wo, k.l0.bias = sb("w0", [P, 384]), sb("wo0", [P, D]), 0
    k.l2.w, k.l2.wo, k.l2.bias = sb("w2", [P, 384]), sb("wo2", [P, D]), 1
    k.rel, k.selfw = sb("rel", [P, RELS + 1, D]), sb("selfw", [P, D])
    k.msg, k.wb = sb("msg", [P, 2, 2, D]), sb("wb", [2, 2, D])
    k.wih, k.whh = sb("wih", [P, 2, 384]), sb("whh", [P, 2, 384])
    k.bias3 = sb("bias3", [3, 4, 512], BF16)
    k.gamma, k.beta, k.b_out, k.bo = (sb(n, [P, D]) for n in ("gamma", "beta", "b_out", "bo"))
    k.eps = sb("eps", [P, 1])

    def order(name, key):
        mask = lambda n: sb(f"{name}_{n}", [P, C])
        seq = lambda n: sb(f"{name}_{n}", [HEADS, 2 * P])
        o = Group()
        o.key, o.rec = key, sb(f"{name}_rec", [P, C, REC])
        o.ends, o.tail = sb(f"{name}_ends", [P, C, 2], I32), sb(f"{name}_tail", [P, C, 2])
        o.target, o.fix_target = sb(f"{name}_target", [P, C], I32), sb(f"{name}_fix", [P, 2], I32)
        o.split, o.join = sb(f"{name}_split", [P, 1]), sb(f"{name}_join", [P, 2, 2, P])
        o.same, o.notlast, o.last, o.pen = mask("same"), mask("notlast"), mask("last"), mask("pen")
        o.first, o.final, o.middle = mask("first"), mask("final"), mask("middle")
        o.seq_same, o.seq_pen = seq("seq_same"), seq("seq_pen")
        o.seq_last, o.seq_notlast = seq("seq_last"), seq("seq_notlast")
        return o

    by_src, by_dst = order("src", KEY_SRC), order("dst", KEY_DST)

    with nc.sbuf_tensor("rec0", [P, C, REC], F32) as k.rec0, nc.sbuf_tensor("rec_mid", [P, C, REC], F32) as rec_mid:
        prepare(nc, k, A)
        for j, (name, o) in enumerate((("sort_src", by_src), ("sort_dst", by_dst))):
            sort_pass(nc, k, name + "_low", k.rec0, k.edge_table[2 * j], rec_mid, o.key, 0)
            sort_pass(nc, k, name + "_high", rec_mid, k.edge_table[2 * j + 1], o.rec, o.key, 8)
            order_masks(nc, k, name + "_masks", o)
    first_norm(nc, k, A)

    k.att = sb("att", [P, HEADS, C])
    with nc.sbuf_tensor("edge_v0", [P, C, D], F32) as k.edge_v:
        edge_scores(nc, k, "score0", by_dst, k.xn, k.l0, False)
        segment_softmax(nc, k, "soft0", by_dst, float(D) ** -0.5, True)
        add_attention(nc, k, "att0", by_dst, k.l0.wo)
    join_parts(nc, k, "join0", by_dst, k.x, D, True)
    self_relation(nc, k)
    add_relations(nc, k, "rel_dst", by_dst, 0)
    join_parts(nc, k, "join1", by_dst, k.x, D, True)
    add_relations(nc, k, "rel_src", by_src, 1)
    join_parts(nc, k, "join2", by_src, k.x, D, True)
    with nc.sbuf_tensor("edge_v2", [P, C, D], F32) as k.edge_v:
        edge_scores(nc, k, "score2", by_dst, k.x, k.l2, True)
        segment_softmax(nc, k, "soft2", by_dst, float(HD) ** -0.5, False)
        add_attention(nc, k, "att2", by_dst, k.l2.wo)
    join_parts(nc, k, "join3", by_dst, k.x, D, True)
    last_norm(nc, k)
    for r in range(2):
        sum_neighbours(nc, k, f"sum{r}", by_src)
        join_parts(nc, k, f"joins{r}", by_src, k.sums, SUMW, False)
        update_nodes(nc, k, A, out, r)


INPUTS = ["x", "src", "dst", "edge_attr_8", "edge_attr_8_n2", "edge_type_8", "edge_weight1", "L0_gnn_gamma",
          "L0_gnn_beta", "L0_gnn_W_qkv", "L0_gnn_b_qkv", "L0_gnn_W_out", "L0_gnn_b_out", "L1_gnn_blocks",
          "L2_gnn_Wq", "L2_gnn_bq", "L2_gnn_Wk", "L2_gnn_bk", "L2_gnn_Wv", "L2_gnn_bv", "L2_gnn_Wo", "L2_gnn_bo",
          "L3_gnn_msg_W", "L3_gnn_msg_b", "L3_gnn_gru_Wih", "L3_gnn_gru_Whh", "L3_gnn_gru_bih", "L3_gnn_gru_bhh"]


def kernel(**inputs):
    import concourse.bacc as bacc
    from concourse.bass_utils import run_bass_kernel_spmd

    nc = bacc.Bacc("TRN2", target_bir_lowering=False, num_devices=1)
    arrays, args = {}, {}
    for name in INPUTS:
        a = np.ascontiguousarray(inputs[name])
        arrays[f"in_{name}"] = a
        args[name] = nc.dram_tensor(f"in_{name}", a.shape, mybir.dt.from_np(a.dtype), kind="ExternalInput").ap()
    out = nc.dram_tensor("out_x", (NODES, D), F32, kind="ExternalOutput").ap()
    build(nc, args, out)
    r = run_bass_kernel_spmd(nc, [arrays], core_ids=[0])
    return r.results[0]["out_x"]
```

```python
from contextlib import ExitStack

import numpy as np
import concourse.bass as bass
from concourse import mybir
from concourse.alu_op_type import AluOpType as ALU

F32, BF16, I32 = mybir.dt.float32, mybir.dt.bfloat16, mybir.dt.int32
ACT = mybir.ActivationFunctionType
AXX = mybir.AxisListType.X

NODES, EDGES, D, HEADS = 50000, 25000, 128, 8
HD = D // HEADS
P = 128
RELS = 8
EPS = 1e-5
BIG = 1e30

C = EDGES // 125
EP = EDGES // C
REC = 4 + HEADS
KEY_SRC, KEY_DST, TYPE, WEIGHT, ATTN = 0, 1, 2, 3, 4
BUCKETS = 256

PAD_NODE = NODES
FIX = NODES + P
FIX_DUMMY = FIX + 2 * P
DUMMY = FIX_DUMMY + 2 * P
STEPS = 8
ROWS = DUMMY + P * STEPS
SUMW = D + 2

G = 4
BLOCK = P * G
BLOCKS = -(-NODES // BLOCK)
TAIL = BLOCKS - 1
TAIL_P = (NODES - TAIL * BLOCK) // G


class Group:
    pass


def ds(i, n=1):
    return bass.ds(i, n)


def wait(eng, sem, value):
    if not isinstance(value, int) or value > 0:
        eng.wait_ge(sem, value)


def spread(ap, axis, n):
    shape = list(ap.shape)
    shape[axis] = n
    return ap.broadcast_to(shape)


class Phase:

    def __init__(self, nc, name):
        self.nc, self.name, self.stack = nc, name, ExitStack()

    def __enter__(self):
        self.stack.enter_context(self.nc.cleanup_on_exit())
        self.gate = self.sem("gate")
        return self

    def __exit__(self, *said):
        self.stack.__exit__(*said)
        self.nc.all_engine_barrier()

    def sb(self, name, shape, dt=F32):
        return self.nc.alloc_sbuf_tensor(f"{self.name}_{name}", shape, dt)

    def ps(self, name, shape):
        parts, free = shape[0], shape[1:]
        size = int(np.prod(free))
        whole = self.nc.alloc_psum_tensor(f"{self.name}_{name}", [P, -(-size // 512) * 512], F32)
        used = whole[0:parts, 0:size]
        return used if len(free) == 1 else used.rearrange("p (a b) -> p a b", b=free[-1])

    def sem(self, name):
        return self.nc.alloc_semaphore(f"{self.name}_{name}")

    def held(self, eng, sem, value):
        wait(eng, sem, value)
        if not isinstance(value, int):
            eng.sem_inc(self.gate, 1)


def pipeline(eng, n, stages, unroll, alike=None):
    last = max(lag for lag, _ in stages)
    first = -(-(last + unroll) // unroll) * unroll
    turns = ((alike or n) - first) // unroll

    def tick(t):
        for lag, stage in stages:
            if 0 <= t - lag < n:
                stage(t - lag, (t - lag) % unroll, (t - lag) // unroll)

    for t in range(first):
        tick(t)
    with eng.Fori(0, turns) as turn:
        for u in range(unroll):
            for lag, stage in stages:
                at = first + u - lag
                stage(turn * unroll + at, at % unroll, turn + at // unroll)
    for t in range(first + turns * unroll, n + last):
        tick(t)


class Chain:

    def __init__(self, eng, sem):
        self.eng, self.sem, self.n = eng, sem, 0

    def __call__(self, instruction):
        self.n += 1
        instruction.then_inc(self.sem, 1)
        self.eng.wait_ge(self.sem, self.n)


def block_rows(table, i, width=D, at=0, rows=NODES):
    if isinstance(i, int) and i == TAIL:
        return table[TAIL * BLOCK:NODES, :].rearrange("(p a g) d -> p a (g d)", g=G, a=1)
    whole = table[0:TAIL * BLOCK, :].rearrange("(i p g) d -> p i (g d)", p=P, g=G)
    return whole[:, ds(i), :]


def block_tile(tile, s, i):
    n = TAIL_P if isinstance(i, int) and i == TAIL else P
    return tile[0:n, s:s + 1, :, :].rearrange("p s g d -> p s (g d)")


def prepare(nc, k, A):
    with Phase(nc, "prep") as ph:
        NT = 24
        stage = ph.sb("stage", [P, NT, D])
        wb_col = ph.sb("wb_col", [P, 2, 2])
        iota_i = ph.sb("iota_i", [P, BUCKETS], I32)
        dummy_i = ph.sb("dummy_i", [P, C], I32)
        fix_i = ph.sb("fix_i", [P, 4], I32)
        ends = [ph.sb(f"end{j}", [P, C], I32) for j in range(3)]
        dist = ph.sb("dist", [P, C, HEADS])
        path = ph.sb("path", [P, C, HEADS])
        weight = ph.sb("weight", [P, C])
        wb_row = ph.sb("wb_row", [2, 2, D])
        brow = ph.sb("brow", [1, 4, 512])
        bres = ph.sb("bres", [1, 4, 512])
        bparts = ph.sb("bparts", [1, 3, 4, 512], BF16)
        zero = ph.sb("zero", [P, 41 * D])
        turned = [ph.ps(f"turned{j}", [P, D]) for j in range(4)]
        loads, cleared, made, sent = ph.sem("loads"), ph.sem("cleared"), ph.sem("made"), ph.sem("sent")
        w_in, w_turned, w_kept, v_step = ph.sem("w_in"), ph.sem("w_turned"), ph.sem("w_kept"), ph.sem("v_step")
        parts_ready, zeroed = ph.sem("parts_ready"), ph.sem("zeroed")

        tiles = [(A["L0_gnn_W_qkv"][j * D:(j + 1) * D, :], k.l0.w[:, o:o + D]) for j, o in ((0, 0), (1, 256), (2, 128))]
        tiles += [(A["L0_gnn_W_out"], k.l0.wo[:, :])]
        tiles += [(w, k.l2.w[:, o:o + D]) for w, o in ((A["L2_gnn_Wq"], 0), (A["L2_gnn_Wk"], 256), (A["L2_gnn_Wv"], 128))]
        tiles += [(A["L2_gnn_Wo"], k.l2.wo[:, :])]
        for r in range(2):
            tiles += [(A["L3_gnn_msg_W"][r, :, j * D:(j + 1) * D], k.msg[:, r, j, :]) for j in range(2)]
            tiles += [(A["L3_gnn_gru_Wih"][r, j * D:(j + 1) * D, :], k.wih[:, r, j * D:(j + 1) * D]) for j in range(3)]
            tiles += [(A["L3_gnn_gru_Whh"][r, j * D:(j + 1) * D, :], k.whh[:, r, j * D:(j + 1) * D]) for j in range(3)]
        assert len(tiles) == NT
        row = lambda a: a.rearrange("(o n) -> o n", o=1)
        n_loads = 6 + 6 + 4 + 3 + 3 + HEADS
        with nc.Block() as block:
            @block.sync
            def _(sp):
                for t, (src, _) in enumerate(tiles):
                    sp.dma_start(stage[:, t, :], src).then_inc(w_in, 16)
                with nc.allow_non_contiguous_dma(reason="columns of 128 single elements, once"):
                    for r in range(2):
                        sp.dma_start(wb_col[:, r, 0:1], A["L3_gnn_msg_W"][r, :, 2 * D:2 * D + 1]).then_inc(w_in, 16)
                        sp.dma_start(wb_col[:, r, 1:2], A["L3_gnn_msg_b"][r, :].rearrange("(n o) -> n o", o=1)).then_inc(w_in, 16)
                sp.wait_ge(cleared, 1)
                for dst, src in (
                    (brow[:, 0, 0:D], row(A["L0_gnn_b_qkv"][0:D])), (brow[:, 0, 256:384], row(A["L0_gnn_b_qkv"][D:2 * D])),
                    (brow[:, 0, D:256], row(A["L0_gnn_b_qkv"][2 * D:3 * D])),
                    (brow[:, 1, 0:D], row(A["L2_gnn_bq"])), (brow[:, 1, 256:384], row(A["L2_gnn_bk"])),
                    (brow[:, 1, D:256], row(A["L2_gnn_bv"])),
                ):
                    sp.dma_start(dst, src).then_inc(loads, 16)
                for r in range(2):
                    sp.dma_start(brow[:, 2 + r, 0:384], A["L3_gnn_gru_bih"][r:r + 1, :]).then_inc(loads, 16)
                    sp.dma_start(brow[:, 2 + r, 384:512], A["L3_gnn_gru_bhh"][r:r + 1, 2 * D:3 * D]).then_inc(loads, 16)
                    sp.dma_start(bres[:, 2 + r, 0:256], A["L3_gnn_gru_bhh"][r:r + 1, 0:2 * D]).then_inc(loads, 16)
                for dst, src in ((k.gamma, A["L0_gnn_gamma"]), (k.beta, A["L0_gnn_beta"]), (k.b_out, A["L0_gnn_b_out"]),
                                 (k.bo, A["L2_gnn_bo"])):
                    sp.dma_start(dst[:, :], spread(row(src), 0, P)).then_inc(loads, 16)
                for j, src in enumerate((A["src"], A["dst"], A["edge_type_8"])):
                    sp.dma_start(ends[j][0:EP, :], src.rearrange("(p c) -> p c", c=C)).then_inc(loads, 16)
                sp.dma_start(weight[0:EP, :], A["edge_weight1"].rearrange("(p c) o -> p (c o)", c=C)).then_inc(loads, 16)
                sp.dma_start(dist[0:EP, :, :], A["edge_attr_8"].rearrange("(p c) h -> p c h", c=C)).then_inc(loads, 16)
                sp.dma_start(path[0:EP, :, :], A["edge_attr_8_n2"].rearrange("(p c) h -> p c h", c=C)).then_inc(loads, 16)
                for b in range(HEADS):
                    sp.dma_start(k.rel[b * HD:(b + 1) * HD, :, b * HD:(b + 1) * HD],
                                 A["L1_gnn_blocks"][:, b, :, :].rearrange("r i j -> i r j")).then_inc(loads, 16)
                sp.wait_ge(parts_ready, 1)
                for j in range(3):
                    sp.dma_start(k.bias3[j:j + 1, :, :], bparts[:, j, :, :]).then_inc(sent, 16)
                sp.wait_ge(w_kept, NT + 2)
                for g in range(G):
                    sp.dma_start(k.wb[2 * g:2 * g + 2, :, g, :], wb_row[:, :, :]).then_inc(sent, 16)
                sp.wait_ge(sent, 16 * (3 + G))

            @block.gpsimd
            def _(pool):
                pool.memset(k.ident[:, :], 0.0)
                pool.memset(k.identb[:, :], 0.0)
                pool.memset(k.before[:, :], 1.0)
                pool.memset(k.below[:, :], 0.0)
                pool.memset(k.ones[:, :], 1.0)
                pool.memset(k.onesb[:, :], 1.0)
                pool.memset(zero[:, :], 0.0)
                pool.memset(k.eps[:, :], EPS)
                pool.memset(bres[:, :, :], 0.0)
                pool.memset(brow[:, :, :], 0.0)
                pool.memset(k.rel[:, :, :], 0.0)
                pool.memset(k.wb[:, :, :, :], 0.0)
                for e in ends:
                    pool.memset(e[:, :], PAD_NODE)
                pool.memset(weight[:, :], 0.0)
                pool.memset(dist[:, :, :], 0.0)
                pool.memset(path[:, :, :], 0.0).then_inc(cleared, 1)
                pool.wait_ge(cleared, 1)
                for m in (k.ident, k.identb):
                    pool.affine_select(out=m[:, :], in_=m[:, :], compare_op=ALU.not_equal, fill=1.0, base=0,
                                       pattern=[[-1, P]], channel_multiplier=1)
                pool.affine_select(out=k.before[:, :], in_=k.before[:, :], compare_op=ALU.is_ge, fill=0.0, base=-1,
                                   pattern=[[1, P]], channel_multiplier=-1)
                pool.affine_select(out=k.below[:, :], in_=k.below[:, :], compare_op=ALU.not_equal, fill=1.0, base=-1,
                                   pattern=[[-1, P]], channel_multiplier=1)
                pool.iota(iota_i[:, :], pattern=[[1, BUCKETS]], base=0, channel_multiplier=0)
                pool.iota(dummy_i[:, :], pattern=[[0, C // STEPS], [P, STEPS]], base=DUMMY, channel_multiplier=1)
                pool.iota(fix_i[:, :], pattern=[[P, 4]], base=FIX, channel_multiplier=1).then_inc(made, 1)

            @block.scalar
            def _(act):
                act.wait_ge(cleared, 1)
                flat = lambda t, a, n: t[a:a + n, :].rearrange("(p r) d -> p (r d)", p=P)
                x_rest = flat(k.x, NODES, ROWS - NODES)
                act.dma_start(x_rest, zero[:, 0:(ROWS - NODES) // P * D]).then_inc(zeroed, 16)
                for t in (k.xn, k.h):
                    act.dma_start(flat(t, NODES, P), zero[:, 0:D]).then_inc(zeroed, 16)
                rows = -(-FIX_DUMMY // P)
                sums = flat(k.sums, 0, rows * P)
                n_sum = 0
                for j in range(0, rows, 40):
                    w = min(40, rows - j) * SUMW
                    act.dma_start(sums[:, j * SUMW:j * SUMW + w], zero[:, 0:w]).then_inc(zeroed, 16)
                    n_sum += 1
                for t, (_, dst) in enumerate(tiles):
                    act.wait_ge(w_turned, t + 1)
                    act.copy(dst, turned[t % 4][:, :]).then_inc(w_kept, 1)
                for r in range(2):
                    act.wait_ge(w_turned, NT + r + 1)
                    act.copy(wb_row[:, r, :], turned[(NT + r) % 4][0:2, :]).then_inc(w_kept, 1)
                act.wait_ge(zeroed, 16 * (3 + n_sum))

            @block.tensor
            def _(pe):
                pe.wait_ge(made, 1)
                pe.wait_ge(w_in, 16 * (NT + 4))
                for t in range(NT):
                    wait(pe, w_kept, t - 3)
                    pe.transpose(turned[t % 4][:, :], stage[:, t, :], k.ident[:, :]).then_inc(w_turned, 1)
                for r in range(2):
                    t = NT + r
                    pe.wait_ge(w_kept, t - 3)
                    pe.transpose(turned[t % 4][0:2, :], wb_col[:, r, :], k.ident[:, :]).then_inc(w_turned, 1)

            @block.vector
            def _(dve):
                link = Chain(dve, v_step)
                dve.wait_ge(loads, 16 * n_loads)
                dve.wait_ge(made, 1)
                nc.vector.tensor_copy(k.iota[:, :], iota_i[:, :])
                nc.vector.tensor_copy(k.dummy[:, :], dummy_i[:, :])
                nc.vector.tensor_copy(k.fix[:, :], fix_i[:, :])
                for j in range(3):
                    nc.vector.tensor_copy(k.rec0[:, :, j], ends[j][:, :])
                nc.vector.tensor_copy(k.rec0[:, :, WEIGHT], weight[:, :])
                nc.vector.tensor_tensor(k.rec0[:, :, ATTN:REC], dist[:, :, :], path[:, :, :], ALU.add)
                link(nc.vector.tensor_tensor(brow[:, :, :], brow[:, :, :], bres[:, :, :], ALU.add))
                for j in range(3):
                    link(nc.vector.tensor_copy(bparts[:, j, :, :], brow[:, :, :]))
                    link(nc.vector.tensor_tensor(brow[:, :, :], brow[:, :, :], bparts[:, j, :, :], ALU.subtract))
                nc.vector.tensor_copy(k.selfw[:, :], k.rel[:, RELS, :]).then_inc(parts_ready, 1)


def sort_pass(nc, k, name, rec_in, rec_table, rec_out, key, shift):
    with Phase(nc, name) as ph:
        U = 4
        key_i = ph.sb("key_i", [P, C], I32)
        digit_i = ph.sb("digit_i", [P, C], I32)
        digit = ph.sb("digit", [P, C])
        hit = ph.sb("hit", [P, U, BUCKETS], BF16)
        own = ph.sb("own", [P, BUCKETS], BF16)
        zeros = ph.sb("zeros", [P, BUCKETS])
        total = ph.sb("total", [P, BUCKETS])
        start = ph.sb("start", [P, BUCKETS])
        picked = ph.sb("picked", [P, 2, BUCKETS])
        place = ph.sb("place", [P, U, 1])
        place_i = ph.sb("place_i", [P, U, 1], I32)
        row = ph.sb("row", [P, U, REC])
        counts = ph.ps("counts", [P, BUCKETS])
        totals = ph.ps("totals", [P, BUCKETS])
        cursor = ph.ps("cursor", [P, BUCKETS])
        v_step, digits_ready = ph.sem("v_step"), ph.sem("digits_ready")
        hit_ready, counted, counts_kept = ph.sem("hit_ready"), ph.sem("counted"), ph.sem("counts_kept")
        totals_ready, start_ready = ph.sem("totals_ready"), ph.sem("start_ready")
        cursor_ready, picked_ready, place_ready = ph.sem("cursor_ready"), ph.sem("picked_ready"), ph.sem("place_ready")
        again_ready, row_ready, loaded = ph.sem("again_ready"), ph.sem("row_ready"), ph.sem("loaded")
        stored = [ph.sem(f"stored{u}") for u in range(U)]

        with nc.Block() as block:
            @block.vector
            def _(dve):
                link = Chain(dve, v_step)
                nc.vector.memset(zeros[:, :], 0.0)
                link(nc.vector.tensor_copy(key_i[:, :], rec_in[:, :, key]))
                if shift:
                    link(nc.vector.tensor_scalar(digit_i[:, :], key_i[:, :], shift, None, ALU.logical_shift_right))
                else:
                    link(nc.vector.tensor_scalar(digit_i[:, :], key_i[:, :], BUCKETS - 1, None, ALU.bitwise_and))
                link(nc.vector.tensor_copy(digit[:, :], digit_i[:, :]))

                def hits(c, u, turn):
                    wait(dve, counted, c - U + 1)
                    nc.vector.tensor_scalar(hit[:, u, :], k.iota[:, :], digit[:, ds(c)], None, ALU.is_equal)\
                        .then_inc(hit_ready, 1)

                pipeline(dve, C, [(0, hits)], U)
                dve.wait_ge(counted, C)
                nc.vector.tensor_copy(own[:, :], counts[:, :]).then_inc(counts_kept, 1)
                dve.wait_ge(totals_ready, 1)
                link(nc.vector.tensor_copy(total[:, :], totals[:, :]))
                link(nc.vector.tensor_tensor_scan(start[:, :], zeros[:, :], total[:, :], 0.0, ALU.add, ALU.add))
                nc.vector.tensor_tensor(start[:, :], start[:, :], total[:, :], ALU.subtract).then_inc(start_ready, 1)

                def hits_again(c, u, turn):
                    wait(dve, cursor_ready, c - U + 2)
                    nc.vector.tensor_scalar(hit[:, u, :], k.iota[:, :], digit[:, ds(c)], None, ALU.is_equal)\
                        .then_inc(again_ready, 1)

                def places(c, u, turn):
                    wait(dve, again_ready, c + 1)
                    wait(dve, cursor_ready, c + 1)
                    nc.vector.tensor_tensor_reduce(out=picked[:, u % 2, :], in0=cursor[:, :], in1=hit[:, u, :],
                                                   scale=1.0, scalar=0.0, op0=ALU.mult, op1=ALU.add,
                                                   accum_out=place[:, u, :]).then_inc(picked_ready, 1)

                def places_int(c, u, turn):
                    wait(dve, picked_ready, c + 1)
                    wait(dve, stored[u], 16 * turn)
                    nc.vector.tensor_copy(place_i[:, u, :], place[:, u, :]).then_inc(place_ready, 1)

                pipeline(dve, C, [(0, hits_again), (1, places), (2, places_int)], U)

            @block.tensor
            def _(pe):
                def count(c, u, turn):
                    wait(pe, hit_ready, c + 1)
                    first = isinstance(c, int) and c == 0
                    pe.matmul(counts[:, :], k.identb[:, :], hit[:, u, :], start=first, stop=False,
                              skip_group_check=True).then_inc(counted, 1)

                pipeline(pe, C, [(0, count)], U)
                pe.wait_ge(counts_kept, 1)
                pe.matmul(totals[:, :], k.onesb[:, :], own[:, :], start=True, stop=True).then_inc(totals_ready, 1)
                pe.wait_ge(start_ready, 1)
                pe.matmul(cursor[:, :], k.before[:, :], own[:, :], start=True, stop=False, skip_group_check=True)
                pe.matmul(cursor[:, :], k.ident[:, :], start[:, :], start=False, stop=False,
                          skip_group_check=True).then_inc(cursor_ready, 1)

                def advance(c, u, turn):
                    wait(pe, picked_ready, c + 1)
                    pe.matmul(cursor[:, :], k.identb[:, :], hit[:, u, :], start=False, stop=False,
                              skip_group_check=True).then_inc(cursor_ready, 1)

                pipeline(pe, C, [(0, advance)], U)

            @block.scalar
            def _(act):
                def record(c, u, turn):
                    ph.held(act, stored[u], 16 * turn)
                    act.copy(row[:, u:u + 1, :], rec_in[:, ds(c), :]).then_inc(row_ready, 1)

                pipeline(act, C, [(0, record)], U)
                for u in range(U):
                    act.wait_ge(stored[u], 16 * C // U)
                act.dma_start(rec_out[:, :, :], rec_table[:, :].rearrange("(p c) w -> p c w", c=C)).then_inc(loaded, 16)
                act.wait_ge(loaded, 16)

            @block.gpsimd
            def _(pool):
                def store(c, u, turn):
                    ph.held(pool, row_ready, c + 1)
                    ph.held(pool, place_ready, c + 1)
                    pool.indirect_dma_start(rec_table, bass.IndirectOffsetOnAxis(ap=place_i[:, u, :], axis=0),
                                            row[:, u, :], None).then_inc(stored[u], 16)

                pipeline(pool, C, [(0, store)], U)


def order_masks(nc, k, name, o):
    with Phase(nc, name) as ph:
        key = o.rec[:, :, o.key]
        f_first = ph.sb("t0", [P, C])
        t1 = ph.sb("t1", [P, C])
        t2 = ph.sb("t2", [P, C])
        kdiag = ph.sb("kdiag", [P, 2, P])
        kwide = ph.sb("kwide", [P, 2, HEADS])
        nextk = ph.sb("nextk", [P, 2])
        own = ph.sb("own", [P, 2])
        kseq = ph.sb("kseq", [HEADS, P, 2])
        ktile = ph.sb("ktile", [P, 2, 1])
        kb = ph.ps("kb", [P, 2, P])
        kn = ph.ps("kn", [P, 2])
        ks = ph.ps("ks", [HEADS, 2, P])
        v_step, keys_ready, keys_wide = ph.sem("v_step"), ph.sem("keys_ready"), ph.sem("keys_wide")

        with nc.Block() as block:
            @block.vector
            def _(dve):
                link = Chain(dve, v_step)
                k0, k1 = ktile[:, 0, :], ktile[:, 1, :]
                link(nc.vector.tensor_copy(ktile[:, 0, :], o.rec[:, 0, o.key:o.key + 1]))
                link(nc.vector.tensor_copy(ktile[:, 1, :], o.rec[:, C - 1, o.key:o.key + 1]))
                for j in range(2):
                    nc.vector.tensor_scalar(kdiag[:, j, :], k.ident[:, :], ktile[:, j, :], None, ALU.mult)
                    last = nc.vector.tensor_scalar(kwide[:, j, :], k.ones[:, 0:HEADS], ktile[:, j, :], None, ALU.mult)
                last.then_inc(keys_ready, 1)
                nc.vector.memset(o.same[:, 0:1], 0.0)
                nc.vector.memset(o.notlast[:, C - 1:C], 0.0)
                nc.vector.tensor_tensor(o.same[:, 1:C], key[:, 1:C], key[:, 0:C - 1], ALU.is_equal)
                link(nc.vector.tensor_tensor(o.notlast[:, 0:C - 1], key[:, 1:C], key[:, 0:C - 1], ALU.is_equal))
                nc.vector.tensor_scalar(o.last[:, :], o.notlast[:, :], -1.0, 1.0, ALU.mult, ALU.add)
                nc.vector.tensor_scalar(o.pen[:, :], o.same[:, :], 1.0, BIG, ALU.subtract, ALU.mult)
                nc.vector.tensor_scalar(o.first[:, :], key, k0, None, ALU.is_equal)
                link(nc.vector.tensor_scalar(t1[:, :], key, k1, None, ALU.is_equal))
                link(nc.vector.tensor_tensor(t2[:, :], t1[:, :], o.first[:, :], ALU.mult))
                link(nc.vector.tensor_tensor(o.final[:, :], t1[:, :], t2[:, :], ALU.subtract))
                link(nc.vector.tensor_tensor(t1[:, :], o.first[:, :], o.final[:, :], ALU.add))
                link(nc.vector.tensor_scalar(o.middle[:, :], t1[:, :], -1.0, 1.0, ALU.mult, ALU.add))
                link(nc.vector.tensor_tensor(t1[:, :], key, o.middle[:, :], ALU.mult))
                link(nc.vector.scalar_tensor_tensor(t2[:, :], o.first[:, :], k.fix[:, 0:1], t1[:, :], ALU.mult, ALU.add))
                link(nc.vector.scalar_tensor_tensor(t1[:, :], o.final[:, :], k.fix[:, 1:2], t2[:, :], ALU.mult, ALU.add))
                link(nc.vector.tensor_tensor(t2[:, :], t1[:, :], o.last[:, :], ALU.mult))
                link(nc.vector.tensor_tensor(t1[:, :], k.dummy[:, :], o.notlast[:, :], ALU.mult))
                link(nc.vector.tensor_tensor(o.target[:, :], t1[:, :], t2[:, :], ALU.add))
                dve.wait_ge(keys_wide, 1)
                for a in range(2):
                    for b in range(2):
                        nc.vector.tensor_scalar(o.join[:, a, b, :], kb[:, b, :], ktile[:, a, :], None, ALU.is_equal)
                nc.vector.tensor_copy(nextk[:, 0:1], k1)
                link(nc.vector.tensor_copy(nextk[:, 1:2], kn[:, 0:1]))
                nc.vector.tensor_tensor(o.split[:, :], k0, k1, ALU.not_equal)
                nc.vector.tensor_tensor(own[:, 0:1], k0, k1, ALU.not_equal)
                link(nc.vector.tensor_tensor(own[:, 1:2], k1, nextk[:, 1:2], ALU.not_equal))
                link(nc.vector.tensor_tensor(t1[:, 0:2], ktile[:, :, 0], k.fix[:, 2:4], ALU.subtract))
                link(nc.vector.tensor_tensor(t2[:, 0:2], t1[:, 0:2], own[:, :], ALU.mult))
                link(nc.vector.tensor_tensor(o.fix_target[:, :], t2[:, 0:2], k.fix[:, 2:4], ALU.add))
                for j in range(2):
                    last = nc.vector.tensor_copy(kseq[:, :, j], ks[:, j, :])
                link(last)
                seq = kseq[:, :, :].rearrange("h p j -> h (p j)")
                nc.vector.memset(o.seq_same[:, 0:1], 0.0)
                nc.vector.memset(o.seq_notlast[:, 2 * P - 1:2 * P], 0.0)
                nc.vector.tensor_tensor(o.seq_same[:, 1:2 * P], seq[:, 1:2 * P], seq[:, 0:2 * P - 1], ALU.is_equal)
                link(nc.vector.tensor_tensor(o.seq_notlast[:, 0:2 * P - 1], seq[:, 1:2 * P], seq[:, 0:2 * P - 1],
                                             ALU.is_equal))
                nc.vector.tensor_scalar(o.seq_last[:, :], o.seq_notlast[:, :], -1.0, 1.0, ALU.mult, ALU.add)
                link(nc.vector.tensor_scalar(o.seq_pen[:, :], o.seq_same[:, :], 1.0, BIG, ALU.subtract, ALU.mult))
                nc.vector.tensor_copy(o.tail[:, :, 0], o.rec[:, :, WEIGHT])
                nc.vector.memset(o.tail[:, :, 1], 1.0)
                link(nc.vector.tensor_copy(o.ends[:, :, :], o.rec[:, :, KEY_SRC:KEY_DST + 1]))

            @block.tensor
            def _(pe):
                pe.wait_ge(keys_ready, 1)
                for j in range(2):
                    pe.matmul(kb[:, j, :], k.ones[:, :], kdiag[:, j, :], start=True, stop=True)
                    pe.matmul(ks[:, j, :], kwide[:, j, :], k.ident[:, :], start=True, stop=True)
                pe.matmul(kn[:, 0:1], k.below[:, :], ktile[:, 0, :], start=True, stop=True).then_inc(keys_wide, 1)


def dense_stats(nc, ph, dve, m, s, i, rows):
    for g in range(G):
        last = nc.vector.bn_stats(m.stats[:, s, g, :], rows[:, g, :])
    last.then_inc(m.stats_done, 1)
    ph.held(dve, m.stats_done, i + 1)
    for g in range(G):
        last = nc.vector.bn_aggr(m.moments[:, s, g, :], m.stats[:, s, g, :])
    last.then_inc(m.moments_done, 1)


def row_roots(act, k, m, s, i):
    wait(act, m.moments_done, i + 1)
    act.activation(m.root[:, s, :], m.moments[:, s, :, 1], ACT.Sqrt, bias=k.eps[:, :]).then_inc(m.root_done, 1)


def row_scales(nc, dve, m, s, i):
    wait(dve, m.root_done, i + 1)
    nc.vector.reciprocal(m.scale[:, s, :], m.root[:, s, :]).then_inc(m.scale_done, 1)
    wait(dve, m.scale_done, i + 1)
    nc.vector.scalar_tensor_tensor(m.shift[:, s, :], m.moments[:, s, :, 0], -1.0, m.scale[:, s, :],
                                   ALU.mult, ALU.mult).then_inc(m.ready, 1)


def moments_of(ph, name, slots, g=G):
    m = Group()
    m.stats, m.moments = ph.sb(name + "_stats", [P, slots, g, 6]), ph.sb(name + "_moments", [P, slots, g, 2])
    m.root, m.scale = ph.sb(name + "_root", [P, slots, g]), ph.sb(name + "_scale", [P, slots, g])
    m.shift = ph.sb(name + "_shift", [P, slots, g])
    m.stats_done, m.moments_done = ph.sem(name + "_stats_done"), ph.sem(name + "_moments_done")
    m.root_done, m.scale_done, m.ready = ph.sem(name + "_root_done"), ph.sem(name + "_scale_done"), ph.sem(name + "_ready")
    return m


def first_norm(nc, k, A):
    with Phase(nc, "norm0") as ph:
        U = 8
        x = ph.sb("x", [P, U, G, D])
        h = ph.sb("h", [P, U, G, D])
        xn = ph.sb("xn", [P, U, G, D])
        xo = ph.sb("xo", [P, U, G, D])
        mx, mh = moments_of(ph, "mx", U), moments_of(ph, "mh", U)
        x_in = [ph.sem(f"x_in{u}") for u in range(U)]
        out_x = [ph.sem(f"out_x{u}") for u in range(U)]
        out_n = [ph.sem(f"out_n{u}") for u in range(U)]
        h_done, n_done, scaled, xn_ready = ph.sem("h_done"), ph.sem("n_done"), ph.sem("scaled"), ph.sem("xn_ready")
        summed, xo_ready = ph.sem("summed"), ph.sem("xo_ready")
        wide = lambda row: spread(row[:, :].rearrange("p (g d) -> p g d", g=1), 1, G)

        with nc.Block() as block:
            @block.sync
            def _(sp):
                def load(i, s, turn):
                    wait(sp, summed, i - U + 1)
                    sp.dma_start(block_tile(x, s, i), block_rows(A["x"], i)).then_inc(x_in[s], 16)

                def store(i, s, turn):
                    wait(sp, xo_ready, i + 1)
                    sp.dma_start(block_rows(k.x, i), block_tile(xo, s, i)).then_inc(out_x[s], 16)

                pipeline(sp, BLOCKS, [(0, load), (5, store)], U, TAIL)
                for s in range(U):
                    sp.wait_ge(out_x[s], 16 * len(range(s, BLOCKS, U)))

            @block.vector
            def _(dve):
                def x_stats(i, s, turn):
                    wait(dve, x_in[s], 16 * (turn + 1))
                    dense_stats(nc, ph, dve, mx, s, i, x[:, s])

                def x_scales(i, s, turn):
                    row_scales(nc, dve, mx, s, i)

                def h_scales(i, s, turn):
                    row_scales(nc, dve, mh, s, i)

                def h_stats(i, s, turn):
                    wait(dve, h_done, i + 1)
                    wait(dve, out_x[s], 16 * turn)
                    nc.vector.tensor_tensor(xo[:, s], x[:, s], h[:, s], ALU.add).then_inc(summed, 1)
                    dense_stats(nc, ph, dve, mh, s, i, h[:, s])
                    wait(dve, summed, i + 1)
                    nc.vector.tensor_tensor(xo[:, s], xo[:, s], wide(k.b_out), ALU.add).then_inc(xo_ready, 1)

                def affine(i, s, turn):
                    wait(dve, n_done, i + 1)
                    nc.vector.tensor_tensor(xn[:, s], xn[:, s], wide(k.gamma), ALU.mult).then_inc(scaled, 1)
                    wait(dve, scaled, i + 1)
                    nc.vector.tensor_tensor(xn[:, s], xn[:, s], wide(k.beta), ALU.add).then_inc(xn_ready, 1)

                pipeline(dve, BLOCKS, [(0, x_stats), (1, x_scales), (2, h_stats), (3, h_scales), (4, affine)], U, TAIL)

            @block.scalar
            def _(act):
                def relu(i, s, turn):
                    wait(act, n_done, i - U + 1)
                    wait(act, xo_ready, i - U + 1)
                    wait(act, mx.ready, i + 1)
                    for g in range(G):
                        last = act.activation(h[:, s, g, :], x[:, s, g, :], ACT.Relu,
                                              bias=mx.shift[:, s, g:g + 1], scale=mx.scale[:, s, g:g + 1])
                    last.then_inc(h_done, 1)

                def norm(i, s, turn):
                    wait(act, out_n[s], 16 * turn)
                    wait(act, mh.ready, i + 1)
                    for g in range(G):
                        last = act.activation(xn[:, s, g, :], h[:, s, g, :], ACT.Identity,
                                              bias=mh.shift[:, s, g:g + 1], scale=mh.scale[:, s, g:g + 1])
                    last.then_inc(n_done, 1)

                def x_roots(i, s, turn):
                    row_roots(act, k, mx, s, i)

                def h_roots(i, s, turn):
                    row_roots(act, k, mh, s, i)

                pipeline(act, BLOCKS, [(0, x_roots), (1, relu), (2, h_roots), (3, norm)], U, TAIL)

            @block.gpsimd
            def _(pool):
                def store(i, s, turn):
                    wait(pool, xn_ready, i + 1)
                    pool.sem_inc(ph.gate, 1)
                    pool.dma_start(block_rows(k.xn, i), block_tile(xn, s, i)).then_inc(out_n[s], 16)

                pipeline(pool, BLOCKS, [(0, store)], U, TAIL)
                for s in range(U):
                    pool.wait_ge(out_n[s], 16 * len(range(s, BLOCKS, U)))


def edge_scores(nc, k, name, o, table, L, normed):
    with Phase(nc, name) as ph:
        U = 8
        idx = ph.sb("idx", [P, U, 2], I32)
        rows = [[ph.sb(f"rows{u}{j}", [P, D]) for j in range(2)] for u in range(U)]
        act_rows = ph.sb("act_rows", [P, 2, 2, D]) if normed else None
        turned_sb = ph.sb("turned_sb", [P, 2, 2, D])
        k_sb = ph.sb("k_sb", [P, 2, D])
        prod = ph.sb("prod", [P, 2, D])
        turned = [ph.ps(f"turned{j}", [P, 2, D]) for j in range(2)]
        qvk = [ph.ps(f"qvk{j}", [P, 512]) for j in range(2)]
        idx_ready, turned_ready, turned_kept = ph.sem("idx_ready"), ph.sem("turned_ready"), ph.sem("turned_kept")
        qvk_ready, kv_kept, prod_ready, scores_done = ph.sem("qvk_ready"), ph.sem("kv_kept"), ph.sem("prod_ready"), ph.sem("scores_done")
        gathered = [ph.sem(f"gathered{u}") for u in range(U)]
        relu_done = ph.sem("relu_done")
        m = moments_of(ph, "m", 2, 2) if normed else None

        with nc.Block() as block:
            @block.gpsimd
            def _(pool):
                def gather(c, u, turn):
                    ph.held(pool, idx_ready, c + 1)
                    ph.held(pool, relu_done if normed else turned_ready, c - U + 1)
                    for j in range(2):
                        pool.indirect_dma_start(rows[u][j][:, :], None, table,
                                                bass.IndirectOffsetOnAxis(ap=idx[:, u, j:j + 1], axis=0))\
                            .then_inc(gathered[u], 16)

                pipeline(pool, C, [(0, gather)], U)

            @block.vector
            def _(dve):
                def index(c, u, turn):
                    ph.held(dve, gathered[u], 32 * turn)
                    nc.vector.tensor_copy(idx[:, u:u + 1, :], o.ends[:, ds(c), :]).then_inc(idx_ready, 1)

                def moments(c, u, turn):
                    s = u % 2
                    wait(dve, gathered[u], 32 * (turn + 1))
                    for j in range(2):
                        last = nc.vector.bn_stats(m.stats[:, s, j, :], rows[u][j][:, :])
                    last.then_inc(m.stats_done, 1)
                    ph.held(dve, m.stats_done, c + 1)
                    for j in range(2):
                        last = nc.vector.bn_aggr(m.moments[:, s, j, :], m.stats[:, s, j, :])
                    last.then_inc(m.moments_done, 1)

                def scales(c, u, turn):
                    wait(dve, relu_done, c - 1)
                    row_scales(nc, dve, m, u % 2, c)

                def product(c, u, turn):
                    s = u % 2
                    wait(dve, kv_kept, c + 1)
                    wait(dve, scores_done, c - 1)
                    nc.vector.tensor_tensor(prod[:, s, :], qvk[s][:, 0:D], k_sb[:, s, :], ALU.mult)\
                        .then_inc(prod_ready, 1)

                def head_sums(c, u, turn):
                    s = u % 2
                    ph.held(dve, prod_ready, c + 1)
                    nc.vector.tensor_reduce(k.att[:, :, ds(c)], prod[:, s, :].rearrange("p (h e) -> p h e", e=HD),
                                            axis=AXX, op=ALU.add).then_inc(scores_done, 1)

                stages = [(0, index)] + ([(4, moments), (5, scales)] if normed else [])
                stages += [(8, product), (9, head_sums)] if normed else [(6, product), (7, head_sums)]
                pipeline(dve, C, stages, U)

            @block.tensor
            def _(pe):
                def turn_rows(c, u, turn):
                    s = u % 2
                    wait(pe, turned_kept, c - 1)
                    if normed:
                        wait(pe, relu_done, c + 1)
                    else:
                        wait(pe, gathered[u], 32 * (turn + 1))
                    for j in range(2):
                        src = act_rows[:, s, j, :] if normed else rows[u][j][:, :]
                        last = pe.transpose(turned[s][:, j, :], src, k.ident[:, :])
                    last.then_inc(turned_ready, 1)

                def project(c, u, turn):
                    s = u % 2
                    wait(pe, turned_kept, c + 1)
                    wait(pe, prod_ready, c - 1)
                    pe.matmul(qvk[s][:, 0:384], k.onesb[0:3, :], k.bias3[:, L.bias, 0:384], start=True, stop=False)
                    pe.matmul(qvk[s][:, 0:256], turned_sb[:, s, 0, :], L.w[:, 0:256], start=False, stop=False)
                    pe.matmul(qvk[s][:, 256:384], turned_sb[:, s, 1, :], L.w[:, 256:384], start=False, stop=True)\
                        .then_inc(qvk_ready, 1)

                pipeline(pe, C, [(0, turn_rows), (1, project)], U)

            @block.scalar
            def _(act):
                def relu(c, u, turn):
                    s = u % 2
                    wait(act, turned_ready, c - 1)
                    wait(act, m.ready, c + 1)
                    for j in range(2):
                        last = act.activation(act_rows[:, s, j, :], rows[u][j][:, :], ACT.Relu,
                                              bias=m.shift[:, s, j:j + 1], scale=m.scale[:, s, j:j + 1])
                    last.then_inc(relu_done, 1)

                def keep_turned(c, u, turn):
                    s = u % 2
                    wait(act, turned_ready, c + 1)
                    wait(act, qvk_ready, c - 1)
                    act.copy(turned_sb[:, s, :, :], turned[s][:, :, :]).then_inc(turned_kept, 1)

                def keep_kv(c, u, turn):
                    s = u % 2
                    ph.held(act, qvk_ready, c + 1)
                    ph.held(act, prod_ready, c - 1)
                    act.copy(k_sb[:, s, :], qvk[s][:, 256:384])
                    act.copy(k.edge_v[:, ds(c), :], qvk[s][:, 128:256].rearrange("p (o d) -> p o d", o=1))\
                        .then_inc(kv_kept, 1)

                def roots(c, u, turn):
                    row_roots(act, k, m, u % 2, c)

                stages = [(0, roots), (1, relu), (2, keep_turned), (3, keep_kv)] if normed else \
                    [(1, keep_turned), (2, keep_kv)]
                pipeline(act, C, stages, U)


def segment_softmax(nc, k, name, o, scale, biased):
    with Phase(nc, name) as ph:
        a = k.att
        run = ph.sb("run", [P, HEADS, C])
        tmp = ph.sb("tmp", [P, HEADS, C])
        low = ph.sb("low", [P, 1])
        part = ph.sb("part", [P, 2, HEADS])
        total = ph.sb("total", [P, 2, HEADS])
        seq = ph.sb("seq", [HEADS, P, 2])
        seq_run = ph.sb("seq_run", [HEADS, 2 * P])
        seq_end = ph.sb("seq_end", [HEADS, 2 * P])
        seq_tot = ph.sb("seq_tot", [HEADS, 2 * P])
        seq_half = ph.sb("seq_half", [HEADS, 2, P])
        wide = ph.ps("wide", [HEADS, 2, P])
        tall = ph.ps("tall", [P, 2, HEADS])
        v_step, part_ready, wide_ready = ph.sem("v_step"), ph.sem("part_ready"), ph.sem("wide_ready")
        seq_ready, tall_ready, shifted, exps = ph.sem("seq_ready"), ph.sem("tall_ready"), ph.sem("shifted"), ph.sem("exps")
        per_head = lambda mask: spread(mask[:, :].rearrange("p (h c) -> p h c", h=1), 1, HEADS)
        V = nc.vector

        with nc.Block() as block:
            @block.vector
            def _(dve):
                link = Chain(dve, v_step)
                if biased:
                    attn = o.rec[:, :, ATTN:REC].rearrange("p c h -> p h c")
                    link(V.tensor_scalar(tmp[:, :, :], a[:, :, :], scale, None, ALU.mult))
                    link(V.tensor_tensor(a[:, :, :], tmp[:, :, :], attn, ALU.add))
                else:
                    link(V.tensor_scalar(a[:, :, :], a[:, :, :], scale, None, ALU.mult))

                def over_segments(step, state_in, state_op, value_op, start):
                    for h in range(HEADS):
                        last = V.tensor_tensor_scan(run[:, h, :], state_in[:, :], a[:, h, :], start, state_op, value_op)
                    link(last)
                    link(V.tensor_tensor(tmp[:, :, :], run[:, :, :], per_head(o.last), ALU.mult))
                    for h in range(HEADS):
                        last = V.tensor_tensor_scan(run[:, h, ::-1], o.notlast[:, ::-1], tmp[:, h, ::-1], 0.0,
                                                    ALU.mult, ALU.add)
                    link(last)
                    V.tensor_copy(part[:, 0, :], run[:, :, 0])
                    if state_op == ALU.mult:
                        last = V.tensor_scalar(part[:, 1, :], run[:, :, C - 1], o.split[:, :], None, ALU.mult)
                    else:
                        last = V.tensor_copy(part[:, 1, :], run[:, :, C - 1])
                    last.then_inc(part_ready, 1)
                    dve.wait_ge(wide_ready, step)
                    for j in range(2):
                        last = V.tensor_copy(seq[:, :, j], wide[:, j, :])
                    link(last)
                    seq_in = o.seq_pen if state_op == ALU.add else o.seq_same
                    link(V.tensor_tensor_scan(seq_run[:, :], seq_in[:, :], seq[:, :, :].rearrange("h p j -> h (p j)"),
                                              start, state_op, value_op))
                    link(V.tensor_tensor(seq_end[:, :], seq_run[:, :], o.seq_last[:, :], ALU.mult))
                    link(V.tensor_tensor_scan(seq_tot[:, ::-1], o.seq_notlast[:, ::-1], seq_end[:, ::-1], 0.0,
                                              ALU.mult, ALU.add))
                    V.tensor_copy(seq_half[:, :, :], seq_tot[:, :].rearrange("h (p j) -> h j p", j=2)).then_inc(seq_ready, 1)
                    dve.wait_ge(tall_ready, step)
                    link(V.tensor_copy(total[:, :, :], tall[:, :, :]))
                    link(V.tensor_tensor(run[:, :, :], run[:, :, :], per_head(o.middle), ALU.mult))
                    for mask, j in ((o.first, 0), (o.final, 1)):
                        for h in range(HEADS):
                            last = V.scalar_tensor_tensor(run[:, h, :], mask[:, :], total[:, j, h:h + 1], run[:, h, :],
                                                          ALU.mult, ALU.add)
                        link(last)

                over_segments(1, o.pen, ALU.add, ALU.max, -BIG)
                V.tensor_tensor(a[:, :, :], a[:, :, :], run[:, :, :], ALU.subtract).then_inc(shifted, 1)
                dve.wait_ge(exps, 1)
                over_segments(2, o.same, ALU.mult, ALU.add, 0.0)
                link(V.reciprocal(tmp[:, :, :], run[:, :, :]))
                link(V.tensor_tensor(a[:, :, :], a[:, :, :], tmp[:, :, :], ALU.mult))

            @block.scalar
            def _(act):
                act.wait_ge(shifted, 1)
                act.activation(a[:, :, :], a[:, :, :], ACT.Exp).then_inc(exps, 1)

            @block.tensor
            def _(pe):
                for step in (1, 2):
                    pe.wait_ge(part_ready, step)
                    for j in range(2):
                        last = pe.transpose(wide[:, j, :], part[:, j, :], k.ident[:, :])
                    last.then_inc(wide_ready, 1)
                    pe.wait_ge(seq_ready, step)
                    for j in range(2):
                        last = pe.transpose(tall[:, j, :], seq_half[:, j, :], k.ident[0:HEADS, 0:HEADS])
                    last.then_inc(tall_ready, 1)


def add_attention(nc, k, name, o, wo):
    with Phase(nc, name) as ph:
        U = 8
        idx = ph.sb("idx", [P, U, 1], I32)
        value = ph.sb("value", [P, U, D])
        state = ph.sb("state", [P, U, D])
        turned_sb = ph.sb("turned_sb", [P, 2, D])
        out = ph.sb("out", [P, U, D])
        turned = [ph.ps(f"turned{j}", [P, D]) for j in range(2)]
        mixed = [ph.ps(f"mixed{j}", [P, D]) for j in range(2)]
        idx_ready, value_ready, state_ready = ph.sem("idx_ready"), ph.sem("value_ready"), ph.sem("state_ready")
        turned_ready, turned_kept, mixed_ready, out_ready = ph.sem("turned_ready"), ph.sem("turned_kept"), ph.sem("mixed_ready"), ph.sem("out_ready")
        added = [ph.sem(f"added{u}") for u in range(U)]
        state_init = ph.sem("state_init")

        with nc.Block() as block:
            @block.vector
            def _(dve):
                nc.vector.memset(state[:, U - 1, :], 0.0).then_inc(state_init, 1)
                dve.wait_ge(state_init, 1)

                def weigh(c, u, turn):
                    ph.held(dve, added[u], 16 * turn)
                    nc.vector.tensor_copy(idx[:, u:u + 1, :], o.target[:, ds(c)].rearrange("p (a c) -> p a c", a=1))\
                        .then_inc(idx_ready, 1)
                    v = k.edge_v[:, ds(c), :].rearrange("p c (h e) -> p (c h) e", e=HD)
                    nc.vector.tensor_tensor(value[:, u, :].rearrange("p (h e) -> p h e", e=HD), v,
                                            spread(k.att[:, :, ds(c)], 2, HD), ALU.mult).then_inc(value_ready, 1)

                def accumulate(c, u, turn):
                    wait(dve, value_ready, c + 1)
                    wait(dve, turned_ready, c - U + 1)
                    wait(dve, state_ready, c)
                    nc.vector.scalar_tensor_tensor(state[:, u, :], state[:, (u - 1) % U, :], o.same[:, ds(c)],
                                                   value[:, u, :], ALU.mult, ALU.add).then_inc(state_ready, 1)

                pipeline(dve, C, [(0, weigh), (1, accumulate)], U)

            @block.tensor
            def _(pe):
                def turn_sums(c, u, turn):
                    wait(pe, state_ready, c + 1)
                    wait(pe, turned_kept, c - 1)
                    pe.transpose(turned[u % 2][:, :], state[:, u, :], k.ident[:, :]).then_inc(turned_ready, 1)

                def mix(c, u, turn):
                    wait(pe, turned_kept, c + 1)
                    wait(pe, out_ready, c - 1)
                    pe.matmul(mixed[u % 2][:, :], turned_sb[:, u % 2, :], wo[:, :], start=True, stop=True)\
                        .then_inc(mixed_ready, 1)

                pipeline(pe, C, [(0, turn_sums), (1, mix)], U)

            @block.scalar
            def _(act):
                def keep_turned(c, u, turn):
                    wait(act, turned_ready, c + 1)
                    wait(act, mixed_ready, c - 1)
                    act.copy(turned_sb[:, u % 2, :], turned[u % 2][:, :]).then_inc(turned_kept, 1)

                def keep_out(c, u, turn):
                    wait(act, mixed_ready, c + 1)
                    wait(act, added[u], 16 * turn)
                    act.copy(out[:, u, :], mixed[u % 2][:, :]).then_inc(out_ready, 1)

                pipeline(act, C, [(0, keep_turned), (1, keep_out)], U)

            @block.gpsimd
            def _(pool):
                def add(c, u, turn):
                    ph.held(pool, idx_ready, c + 1)
                    ph.held(pool, out_ready, c + 1)
                    pool.indirect_dma_start(k.x, bass.IndirectOffsetOnAxis(ap=idx[:, u, :], axis=0), out[:, u, :],
                                            None, compute_op=ALU.add).then_inc(added[u], 16)

                pipeline(pool, C, [(0, add)], U)
                for u in range(U):
                    pool.wait_ge(added[u], 16 * C // U)


def join_parts(nc, k, name, o, table, width, adding):
    with Phase(nc, name) as ph:
        part = ph.sb("part", [P, 2, width])
        out = [ph.sb(f"out{j}", [P, width]) for j in range(2)]
        zero = ph.sb("zero", [P, 2 * width])
        idx = ph.sb("idx", [P, 2], I32)
        total = ph.ps("total", [P, 2, 256])
        loaded, totals, ready, stored, cleared = ph.sem("loaded"), ph.sem("totals"), ph.sem("ready"), ph.sem("stored"), ph.sem("cleared")
        parts = table[FIX:FIX + 2 * P, :].rearrange("(j p) d -> p j d", p=P)

        with nc.Block() as block:
            @block.sync
            def _(sp):
                sp.dma_start(part[:, :, :], parts).then_inc(loaded, 16)
                if adding:
                    sp.wait_ge(loaded, 16)
                    sp.wait_ge(ready, 1)
                    sp.dma_start(parts, zero[:, :].rearrange("p (j d) -> p j d", j=2)).then_inc(cleared, 16)
                    sp.wait_ge(cleared, 16)

            @block.tensor
            def _(pe):
                pe.wait_ge(loaded, 16)
                for b in range(2):
                    for a in range(2):
                        last = pe.matmul(total[:, b, 0:width], o.join[:, a, b, :], part[:, a, :],
                                         start=(a == 0), stop=(a == 1))
                last.then_inc(totals, 1)

            @block.vector
            def _(dve):
                nc.vector.memset(zero[:, :], 0.0)
                nc.vector.tensor_copy(idx[:, :], o.fix_target[:, :]).then_inc(ready, 1)
                dve.wait_ge(totals, 1)
                for j in range(2):
                    nc.vector.tensor_copy(out[j][:, :], total[:, j, 0:width]).then_inc(ready, 1)

            @block.gpsimd
            def _(pool):
                pool.wait_ge(ready, 3)
                for j in range(2):
                    op = dict(compute_op=ALU.add) if adding else {}
                    pool.indirect_dma_start(table, bass.IndirectOffsetOnAxis(ap=idx[:, j:j + 1], axis=0),
                                            out[j][:, :], None, **op).then_inc(stored, 16)
                pool.wait_ge(stored, 32)


def self_relation(nc, k):
    with Phase(nc, "self") as ph:
        U = 8
        x = ph.sb("x", [P, U, G, D])
        h = ph.sb("h", [P, U, G, D])
        xo = ph.sb("xo", [P, U, G, D])
        h_t = ph.sb("h_t", [P, 2, G, D])
        m = moments_of(ph, "m", U)
        turned = [ph.ps(f"turned{j}", [P, G, D]) for j in range(2)]
        own = [ph.ps(f"own{j}", [P, G, D]) for j in range(2)]
        x_in = [ph.sem(f"x_in{u}") for u in range(U)]
        out_x = [ph.sem(f"out_x{u}") for u in range(U)]
        out_h = [ph.sem(f"out_h{u}") for u in range(U)]
        h_done, turned_ready, turned_kept, own_ready, xo_ready = (ph.sem(n) for n in ("h_done", "turned_ready", "turned_kept", "own_ready", "xo_ready"))

        with nc.Block() as block:
            @block.sync
            def _(sp):
                def load(i, s, turn):
                    wait(sp, xo_ready, i - U + 1)
                    sp.dma_start(block_tile(x, s, i), block_rows(k.x, i)).then_inc(x_in[s], 16)

                def store(i, s, turn):
                    wait(sp, h_done, i + 1)
                    sp.dma_start(block_rows(k.h, i), block_tile(h, s, i)).then_inc(out_h[s], 16)
                    wait(sp, xo_ready, i + 1)
                    sp.dma_start(block_rows(k.x, i), block_tile(xo, s, i)).then_inc(out_x[s], 16)

                pipeline(sp, BLOCKS, [(0, load), (5, store)], U, TAIL)
                for s in range(U):
                    sp.wait_ge(out_x[s], 16 * len(range(s, BLOCKS, U)))
                    sp.wait_ge(out_h[s], 16 * len(range(s, BLOCKS, U)))

            @block.vector
            def _(dve):
                def stats(i, s, turn):
                    wait(dve, x_in[s], 16 * (turn + 1))
                    dense_stats(nc, ph, dve, m, s, i, x[:, s])

                def scales(i, s, turn):
                    wait(dve, h_done, i - U + 1)
                    row_scales(nc, dve, m, s, i)

                def add(i, s, turn):
                    wait(dve, own_ready, i + 1)
                    wait(dve, out_x[s], 16 * turn)
                    nc.vector.tensor_tensor(xo[:, s], x[:, s], own[s % 2][:, :, :], ALU.add).then_inc(xo_ready, 1)

                pipeline(dve, BLOCKS, [(0, stats), (1, scales), (3, add)], U, TAIL)

            @block.scalar
            def _(act):
                def roots(i, s, turn):
                    row_roots(act, k, m, s, i)

                def relu(i, s, turn):
                    wait(act, turned_ready, i - U + 1)
                    wait(act, out_h[s], 16 * turn)
                    wait(act, m.ready, i + 1)
                    for g in range(G):
                        last = act.activation(h[:, s, g, :], x[:, s, g, :], ACT.Relu,
                                              bias=m.shift[:, s, g:g + 1], scale=m.scale[:, s, g:g + 1])
                    last.then_inc(h_done, 1)

                def keep(i, s, turn):
                    wait(act, turned_ready, i + 1)
                    wait(act, own_ready, i - 1)
                    act.copy(h_t[:, s % 2], turned[s % 2][:, :, :]).then_inc(turned_kept, 1)

                pipeline(act, BLOCKS, [(0, roots), (1, relu), (2, keep)], U, TAIL)

            @block.tensor
            def _(pe):
                def turn_rows(i, s, turn):
                    wait(pe, h_done, i + 1)
                    wait(pe, turned_kept, i - 1)
                    for g in range(G):
                        last = pe.transpose(turned[s % 2][:, g, :], h[:, s, g, :], k.ident[:, :])
                    last.then_inc(turned_ready, 1)

                def multiply(i, s, turn):
                    wait(pe, turned_kept, i + 1)
                    wait(pe, xo_ready, i - 1)
                    for g in range(G):
                        last = pe.matmul(own[s % 2][:, g, :], h_t[:, s % 2, g, :], k.selfw[:, :], start=True, stop=True)
                    last.then_inc(own_ready, 1)

                pipeline(pe, BLOCKS, [(0, turn_rows), (1, multiply)], U, TAIL)


def add_relations(nc, k, name, o, other):
    with Phase(nc, name) as ph:
        U = 8
        idx = ph.sb("idx", [P, U, 1], I32)
        idx_to = ph.sb("idx_to", [P, U, 1], I32)
        rows = [ph.sb(f"rows{u}", [P, D]) for u in range(U)]
        rel = ph.sb("rel", [P, C, RELS])
        turned_sb = ph.sb("turned_sb", [P, 2, D])
        state = ph.sb("state", [P, U, D])
        odd = ph.sb("odd", [P, 2, D])
        turned = [ph.ps(f"turned{j}", [P, D]) for j in range(2)]
        each = [ph.ps(f"each{j}", [P, RELS, D]) for j in range(2)]
        idx_ready, to_ready, turned_ready, turned_kept, each_ready = (ph.sem(n) for n in ("idx_ready", "to_ready", "turned_ready", "turned_kept", "each_ready"))
        even_step, odd_step, picked, v_step = ph.sem("even_step"), ph.sem("odd_step"), ph.sem("picked"), ph.sem("v_step")
        PICKS = RELS // 2 + 1
        gathered = [ph.sem(f"gathered{u}") for u in range(U)]
        added = [ph.sem(f"added{u}") for u in range(U)]

        with nc.Block() as block:
            @block.gpsimd
            def _(pool):
                def gather(c, u, turn):
                    ph.held(pool, idx_ready, c + 1)
                    ph.held(pool, turned_ready, c - U + 1)
                    pool.indirect_dma_start(rows[u][:, :], None, k.h,
                                            bass.IndirectOffsetOnAxis(ap=idx[:, u, :], axis=0)).then_inc(gathered[u], 16)

                def add(c, u, turn):
                    ph.held(pool, picked, c + 1)
                    ph.held(pool, to_ready, c + 1)
                    pool.indirect_dma_start(k.x, bass.IndirectOffsetOnAxis(ap=idx_to[:, u, :], axis=0), state[:, u, :],
                                            None, compute_op=ALU.add).then_inc(added[u], 16)

                pipeline(pool, C, [(0, gather), (6, add)], U)
                for u in range(U):
                    pool.wait_ge(added[u], 16 * C // U)

            @block.vector
            def _(dve):
                for r in range(RELS):
                    last = nc.vector.tensor_scalar(rel[:, :, r], o.rec[:, :, TYPE], float(r), None, ALU.is_equal)
                nc.vector.memset(state[:, U - 1, :], 0.0).then_inc(v_step, 1)
                dve.wait_ge(v_step, 1)

                def index(c, u, turn):
                    ph.held(dve, gathered[u], 16 * turn)
                    nc.vector.tensor_copy(idx[:, u:u + 1, :], o.ends[:, ds(c), other:other + 1]).then_inc(idx_ready, 1)

                def pick(c, u, turn):
                    s = u % 2
                    of = lambda r: rel[:, ds(c), r:r + 1].rearrange("p a b -> p (a b)")
                    ph.held(dve, added[u], 16 * turn)
                    nc.vector.tensor_copy(idx_to[:, u:u + 1, :], o.target[:, ds(c)].rearrange("p (a c) -> p a c", a=1))\
                        .then_inc(to_ready, 1)
                    wait(dve, each_ready, c + 1)
                    wait(dve, picked, c)
                    for r in range(0, RELS + 2, 2):
                        if r < RELS:
                            if r:
                                wait(dve, odd_step, RELS // 2 * c + r // 2)
                                nc.vector.scalar_tensor_tensor(odd[:, s, :], each[s][:, r + 1, :], of(r + 1),
                                                               odd[:, s, :], ALU.mult, ALU.add).then_inc(odd_step, 1)
                            else:
                                nc.vector.tensor_scalar(odd[:, s, :], each[s][:, 1, :], of(1), None, ALU.mult)\
                                    .then_inc(odd_step, 1)
                        if r == 0:
                            nc.vector.tensor_scalar(state[:, u, :], state[:, (u - 1) % U, :], o.same[:, ds(c)], None,
                                                    ALU.mult).then_inc(even_step, 1)
                        else:
                            wait(dve, even_step, PICKS * c + r // 2)
                            nc.vector.scalar_tensor_tensor(state[:, u, :], each[s][:, r - 2, :], of(r - 2),
                                                           state[:, u, :], ALU.mult, ALU.add).then_inc(even_step, 1)
                    wait(dve, odd_step, RELS // 2 * (c + 1))
                    wait(dve, even_step, PICKS * (c + 1))
                    nc.vector.tensor_tensor(state[:, u, :], state[:, u, :], odd[:, s, :], ALU.add).then_inc(picked, 1)

                pipeline(dve, C, [(0, index), (5, pick)], U)

            @block.scalar
            def _(act):
                def keep(c, u, turn):
                    wait(act, turned_ready, c + 1)
                    wait(act, each_ready, c - 1)
                    act.copy(turned_sb[:, u % 2, :], turned[u % 2][:, :]).then_inc(turned_kept, 1)

                pipeline(act, C, [(0, keep)], U)

            @block.tensor
            def _(pe):
                def turn_rows(c, u, turn):
                    wait(pe, gathered[u], 16 * (turn + 1))
                    wait(pe, turned_kept, c - 1)
                    pe.transpose(turned[u % 2][:, :], rows[u][:, :], k.ident[:, :]).then_inc(turned_ready, 1)

                def multiply(c, u, turn):
                    s = u % 2
                    wait(pe, turned_kept, c + 1)
                    wait(pe, picked, c - 1)
                    for j in range(2):
                        last = pe.matmul(each[s][:, 4 * j:4 * j + 4, :], turned_sb[:, s, :],
                                         k.rel[:, 4 * j:4 * j + 4, :], start=True, stop=True)
                    last.then_inc(each_ready, 1)

                pipeline(pe, C, [(0, turn_rows), (1, multiply)], U)


def last_norm(nc, k):
    with Phase(nc, "norm3") as ph:
        U = 8
        x = ph.sb("x", [P, U, G, D])
        h = ph.sb("h", [P, U, G, D])
        xb = ph.sb("xb", [P, U, G, D])
        m = moments_of(ph, "m", U)
        x_in = [ph.sem(f"x_in{u}") for u in range(U)]
        out_h = [ph.sem(f"out_h{u}") for u in range(U)]
        h_done, biased = ph.sem("h_done"), ph.sem("biased")
        bo = spread(k.bo[:, :].rearrange("p (g d) -> p g d", g=1), 1, G)

        with nc.Block() as block:
            @block.sync
            def _(sp):
                def load(i, s, turn):
                    wait(sp, biased, i - U + 1)
                    sp.dma_start(block_tile(x, s, i), block_rows(k.x, i)).then_inc(x_in[s], 16)

                def store(i, s, turn):
                    wait(sp, h_done, i + 1)
                    sp.dma_start(block_rows(k.h, i), block_tile(h, s, i)).then_inc(out_h[s], 16)

                pipeline(sp, BLOCKS, [(0, load), (5, store)], U, TAIL)
                for s in range(U):
                    sp.wait_ge(out_h[s], 16 * len(range(s, BLOCKS, U)))

            @block.vector
            def _(dve):
                def stats(i, s, turn):
                    wait(dve, x_in[s], 16 * (turn + 1))
                    wait(dve, h_done, i - U + 1)
                    nc.vector.tensor_tensor(xb[:, s], x[:, s], bo, ALU.add).then_inc(biased, 1)
                    wait(dve, biased, i + 1)
                    dense_stats(nc, ph, dve, m, s, i, xb[:, s])

                def scales(i, s, turn):
                    row_scales(nc, dve, m, s, i)

                pipeline(dve, BLOCKS, [(0, stats), (1, scales)], U, TAIL)

            @block.scalar
            def _(act):
                def roots(i, s, turn):
                    row_roots(act, k, m, s, i)

                def relu(i, s, turn):
                    wait(act, out_h[s], 16 * turn)
                    wait(act, m.ready, i + 1)
                    for g in range(G):
                        last = act.activation(h[:, s, g, :], xb[:, s, g, :], ACT.Relu,
                                              bias=m.shift[:, s, g:g + 1], scale=m.scale[:, s, g:g + 1])
                    last.then_inc(h_done, 1)

                pipeline(act, BLOCKS, [(0, roots), (1, relu)], U, TAIL)


def sum_neighbours(nc, k, name, o):
    with Phase(nc, name) as ph:
        U = 4
        idx = ph.sb("idx", [P, U, 1], I32)
        idx_to = ph.sb("idx_to", [P, U, 1], I32)
        rows = [ph.sb(f"rows{u}", [P, D]) for u in range(U)]
        state = ph.sb("state", [P, U, SUMW])
        idx_ready, to_ready, tails, summed, v_step = (ph.sem(n) for n in ("idx_ready", "to_ready", "tails", "summed", "v_step"))
        gathered = [ph.sem(f"gathered{u}") for u in range(U)]
        stored = [ph.sem(f"stored{u}") for u in range(U)]

        with nc.Block() as block:
            @block.gpsimd
            def _(pool):
                def gather(c, u, turn):
                    ph.held(pool, idx_ready, c + 1)
                    ph.held(pool, summed, c - U + 1)
                    pool.indirect_dma_start(rows[u][:, :], None, k.h,
                                            bass.IndirectOffsetOnAxis(ap=idx[:, u, :], axis=0)).then_inc(gathered[u], 16)

                def store(c, u, turn):
                    ph.held(pool, summed, c + 1)
                    ph.held(pool, to_ready, c + 1)
                    pool.indirect_dma_start(k.sums, bass.IndirectOffsetOnAxis(ap=idx_to[:, u, :], axis=0),
                                            state[:, u, :], None).then_inc(stored[u], 16)

                pipeline(pool, C, [(0, gather), (3, store)], U)
                for u in range(U):
                    pool.wait_ge(stored[u], 16 * C // U)

            @block.vector
            def _(dve):
                nc.vector.memset(state[:, U - 1, :], 0.0).then_inc(v_step, 1)
                dve.wait_ge(v_step, 1)

                def index(c, u, turn):
                    ph.held(dve, gathered[u], 16 * turn)
                    nc.vector.tensor_copy(idx[:, u:u + 1, :], o.ends[:, ds(c), 1:2]).then_inc(idx_ready, 1)

                def add(c, u, turn):
                    ph.held(dve, stored[u], 16 * turn)
                    nc.vector.tensor_copy(idx_to[:, u:u + 1, :], o.target[:, ds(c)].rearrange("p (a c) -> p a c", a=1))\
                        .then_inc(to_ready, 1)
                    ph.held(dve, summed, c)
                    same = o.same[:, ds(c)]
                    nc.vector.scalar_tensor_tensor(state[:, u, D:SUMW], state[:, (u - 1) % U, D:SUMW], same,
                                                   o.tail[:, ds(c), :].rearrange("p a b -> p (a b)"),
                                                   ALU.mult, ALU.add)
                    wait(dve, gathered[u], 16 * (turn + 1))
                    nc.vector.scalar_tensor_tensor(state[:, u, 0:D], state[:, (u - 1) % U, 0:D], same, rows[u][:, :],
                                                   ALU.mult, ALU.add).then_inc(summed, 1)

                pipeline(dve, C, [(0, index), (3, add)], U)


def update_nodes(nc, k, A, out, r):
    final = r == 1
    with Phase(nc, f"gru{r}") as ph:
        U = 8
        h = ph.sb("h", [P, U, G, D])
        su = ph.sb("su", [P, U, G, SUMW])
        x = ph.sb("x", [P, U, G, D]) if final else None
        dh = ph.sb("dh", [P, 2, G, D])
        wd_in = ph.sb("wd_in", [P, 2, G, 2])
        t_sb = ph.sb("t_sb", [P, 4, 3, G, D])
        wd_sb = ph.sb("wd_sb", [2 * G, 2, P])
        agg_sb = ph.sb("agg_sb", [P, 2, G, P])
        rz = ph.sb("rz", [P, 2, G, 2 * D])
        t1 = ph.sb("t1", [P, 2, D])
        cand = ph.sb("cand", [P, 2, G, D])
        n = ph.sb("n", [P, 2, G, D])
        change = ph.sb("change", [P, 2, G, D])
        ho = ph.sb("ho", [P, U, G, D])
        turned = [ph.ps(f"turned{j}", [P, G, P]) for j in range(3)]
        wd = ph.ps("wd", [2 * G, P])
        agg = ph.ps("agg", [P, G, P])
        gate = [ph.ps(f"gate{j}", [P, 512]) for j in range(2)]
        h_in = [ph.sem(f"h_in{u}") for u in range(U)]
        h_out = [ph.sem(f"h_out{u}") for u in range(U)]
        scaled, turned_ready, turned_kept, agg_ready, agg_kept = (ph.sem(s) for s in ("scaled", "turned_ready", "turned_kept", "agg_ready", "agg_kept"))
        gate_ready, rz_ready, gated, cand_ready, n_ready = (ph.sem(s) for s in ("gate_ready", "rz_ready", "gated", "cand_ready", "n_ready"))
        changed, weighed, blended, x_sum, block_done = (ph.sem(s) for s in ("changed", "weighed", "blended", "x_sum", "block_done"))
        bo = spread(k.bo[:, :].rearrange("p (g d) -> p g d", g=1), 1, G)
        loads = 3 if final else 2

        with nc.Block() as block:
            @block.sync
            def _(sp):
                def load(i, s, turn):
                    wait(sp, block_done, i - U + 1)
                    sp.dma_start(block_tile(h, s, i), block_rows(k.h, i)).then_inc(h_in[s], 16)
                    sp.dma_start(block_tile(su, s, i), block_rows(k.sums, i, SUMW)).then_inc(h_in[s], 16)
                    if final:
                        sp.dma_start(block_tile(x, s, i), block_rows(k.x, i)).then_inc(h_in[s], 16)

                def store(i, s, turn):
                    wait(sp, block_done, i + 1)
                    sp.dma_start(block_rows(out if final else k.h, i), block_tile(ho, s, i)).then_inc(h_out[s], 16)

                pipeline(sp, BLOCKS, [(0, load), (7, store)], U, TAIL)
                for s in range(U):
                    sp.wait_ge(h_out[s], 16 * len(range(s, BLOCKS, U)))

            @block.vector
            def _(dve):
                def degree(i, s, turn):
                    wait(dve, h_in[s], 16 * loads * (turn + 1))
                    wait(dve, turned_ready, i - 1)
                    nc.vector.tensor_copy(wd_in[:, s % 2], su[:, s, :, D:SUMW])
                    nc.vector.tensor_tensor(dh[:, s % 2], h[:, s], spread(su[:, s, :, D + 1:D + 2], 2, D), ALU.mult)\
                        .then_inc(scaled, 1)

                def candidate(i, s, turn):
                    b = s % 2

                    for g in range(G):
                        wait(dve, rz_ready, i * G + g + 1)
                        nc.vector.tensor_tensor(t1[:, g % 2, :], gate[g % 2][:, 384:512], rz[:, b, g, 0:D], ALU.mult)\
                            .then_inc(gated, 1)
                        wait(dve, gated, i * G + g + 1)
                        nc.vector.tensor_tensor(cand[:, b, g, :], gate[g % 2][:, 256:384], t1[:, g % 2, :], ALU.add)\
                            .then_inc(cand_ready, 1)

                def blend(i, s, turn):
                    b = s % 2
                    wait(dve, n_ready, i + 1)
                    nc.vector.tensor_tensor(change[:, b], h[:, s], n[:, b], ALU.subtract).then_inc(changed, 1)
                    wait(dve, changed, i + 1)
                    nc.vector.tensor_tensor(change[:, b], change[:, b], rz[:, b, :, D:2 * D], ALU.mult).then_inc(weighed, 1)
                    wait(dve, h_out[s], 16 * turn)
                    if final:
                        nc.vector.tensor_tensor(x[:, s], x[:, s], bo, ALU.add).then_inc(x_sum, 1)
                        wait(dve, weighed, i + 1)
                        nc.vector.tensor_tensor(ho[:, s], change[:, b], n[:, b], ALU.add).then_inc(blended, 1)
                        wait(dve, x_sum, i + 1)
                        wait(dve, blended, i + 1)
                        nc.vector.tensor_tensor(ho[:, s], ho[:, s], x[:, s], ALU.add).then_inc(block_done, 1)
                    else:
                        wait(dve, weighed, i + 1)
                        nc.vector.tensor_tensor(ho[:, s], change[:, b], n[:, b], ALU.add).then_inc(block_done, 1)

                pipeline(dve, BLOCKS, [(0, degree), (3, candidate), (4, blend)], U, TAIL)

            @block.tensor
            def _(pe):
                def turn_rows(i, s, turn):
                    wait(pe, scaled, i + 1)
                    wait(pe, turned_kept, i)
                    for g in range(G):
                        pe.transpose(turned[0][:, g, :], su[:, s, g, 0:D], k.ident[:, :])
                        pe.transpose(turned[1][:, g, :], dh[:, s % 2, g, :], k.ident[:, :])
                        pe.transpose(turned[2][:, g, :], h[:, s, g, :], k.ident[:, :])
                    pe.transpose(wd[:, :], wd_in[:, s % 2, :, :], k.ident[:, :]).then_inc(turned_ready, 1)

                def aggregate(i, s, turn):
                    wait(pe, turned_kept, i + 1)
                    wait(pe, agg_kept, i)
                    pe.matmul(agg[:, :, :], k.msg[:, r, 0, :], t_sb[:, s % 4, 0, :, :], start=True, stop=False)
                    pe.matmul(agg[:, :, :], k.msg[:, r, 1, :], t_sb[:, s % 4, 1, :, :], start=False, stop=False)
                    for g in range(G):
                        last = pe.matmul(agg[:, g, :], k.wb[:, r, g, :], wd_sb[:, s % 2, :], start=False, stop=(g == G - 1))
                    last.then_inc(agg_ready, 1)

                def gates(i, s, turn):
                    wait(pe, agg_kept, i + 1)
                    for g in range(G):
                        j, q = g % 2, i * G + g
                        wait(pe, cand_ready, q - 1)
                        pe.matmul(gate[j][:, :], k.onesb[0:3, :], k.bias3[:, 2 + r, :], start=True, stop=False)
                        pe.matmul(gate[j][:, 0:384], agg_sb[:, s % 2, g, :], k.wih[:, r, :], start=False, stop=False)
                        pe.matmul(gate[j][:, 0:256], t_sb[:, s % 4, 2, g, :], k.whh[:, r, 0:256], start=False, stop=False)
                        pe.matmul(gate[j][:, 384:512], t_sb[:, s % 4, 2, g, :], k.whh[:, r, 256:384], start=False,
                                  stop=True).then_inc(gate_ready, 1)

                pipeline(pe, BLOCKS, [(1, turn_rows), (2, aggregate), (3, gates)], U, TAIL)

            @block.scalar
            def _(act):
                def keep(i, s, turn):
                    wait(act, turned_ready, i + 1)
                    wait(act, gate_ready, G * (i - 3))
                    wait(act, agg_ready, i - 1)
                    act.copy(t_sb[:, s % 4, 0], turned[0][:, :, :])
                    act.copy(t_sb[:, s % 4, 1], turned[1][:, :, :])
                    act.copy(wd_sb[:, s % 2, :], wd[:, :])
                    act.copy(t_sb[:, s % 4, 2], turned[2][:, :, :]).then_inc(turned_kept, 1)

                def keep_agg(i, s, turn):
                    wait(act, agg_ready, i + 1)
                    wait(act, gate_ready, G * (i - 1))
                    act.copy(agg_sb[:, s % 2], agg[:, :, :]).then_inc(agg_kept, 1)

                def gates(i, s, turn):
                    wait(act, weighed, i - 1)
                    for g in range(G):
                        wait(act, gate_ready, i * G + g + 1)
                        act.activation(rz[:, s % 2, g, :], gate[g % 2][:, 0:256], ACT.Sigmoid).then_inc(rz_ready, 1)
                    wait(act, cand_ready, G * (i + 1))
                    wait(act, block_done, i - 1)
                    act.activation(n[:, s % 2], cand[:, s % 2], ACT.Tanh).then_inc(n_ready, 1)

                pipeline(act, BLOCKS, [(1, keep), (2, keep_agg), (3, gates)], U, TAIL)


def build(nc, A, out):
    k = Group()
    sb = lambda name, shape, dt=F32: nc.alloc_sbuf_tensor(name, shape, dt)
    table = lambda name, rows, width: nc.dram_tensor(name, (rows, width), F32, kind="Internal").ap()
    k.x, k.h, k.xn = table("x_rows", ROWS, D), table("h_rows", NODES + P, D), table("xn_rows", NODES + P, D)
    k.sums = table("sum_rows", ROWS, SUMW)
    k.edge_table = [table(f"edge_rows{j}", P * C, REC) for j in range(4)]
    k.ident, k.identb = sb("ident", [P, P]), sb("identb", [P, P], BF16)
    k.before, k.below = sb("before", [P, P], BF16), sb("below", [P, P])
    k.ones, k.onesb = sb("ones", [P, P]), sb("onesb", [P, P], BF16)
    k.iota, k.dummy, k.fix = sb("iota", [P, BUCKETS], BF16), sb("dummy_rows", [P, C]), sb("fix", [P, 4])
    k.l0, k.l2 = Group(), Group()
    k.l0.w, k.l0.wo, k.l0.bias = sb("w0", [P, 384]), sb("wo0", [P, D]), 0
    k.l2.w, k.l2.wo, k.l2.bias = sb("w2", [P, 384]), sb("wo2", [P, D]), 1
    k.rel, k.selfw = sb("rel", [P, RELS + 1, D]), sb("selfw", [P, D])
    k.msg, k.wb = sb("msg", [P, 2, 2, D]), sb("wb", [2 * G, 2, G, D])
    k.wih, k.whh = sb("wih", [P, 2, 384]), sb("whh", [P, 2, 384])
    k.bias3 = sb("bias3", [3, 4, 512], BF16)
    k.gamma, k.beta, k.b_out, k.bo = (sb(n, [P, D]) for n in ("gamma", "beta", "b_out", "bo"))
    k.eps = sb("eps", [P, 1])

    def order(name, key):
        mask = lambda n: sb(f"{name}_{n}", [P, C])
        seq = lambda n: sb(f"{name}_{n}", [HEADS, 2 * P])
        o = Group()
        o.key, o.rec = key, sb(f"{name}_rec", [P, C, REC])
        o.ends, o.tail = sb(f"{name}_ends", [P, C, 2], I32), sb(f"{name}_tail", [P, C, 2])
        o.target, o.fix_target = sb(f"{name}_target", [P, C], I32), sb(f"{name}_fix", [P, 2], I32)
        o.split, o.join = sb(f"{name}_split", [P, 1]), sb(f"{name}_join", [P, 2, 2, P])
        o.same, o.notlast, o.last, o.pen = mask("same"), mask("notlast"), mask("last"), mask("pen")
        o.first, o.final, o.middle = mask("first"), mask("final"), mask("middle")
        o.seq_same, o.seq_pen = seq("seq_same"), seq("seq_pen")
        o.seq_last, o.seq_notlast = seq("seq_last"), seq("seq_notlast")
        return o

    by_src, by_dst = order("src", KEY_SRC), order("dst", KEY_DST)

    with nc.sbuf_tensor("rec0", [P, C, REC], F32) as k.rec0, nc.sbuf_tensor("rec_mid", [P, C, REC], F32) as rec_mid:
        prepare(nc, k, A)
        for j, (name, o) in enumerate((("sort_src", by_src), ("sort_dst", by_dst))):
            sort_pass(nc, k, name + "_low", k.rec0, k.edge_table[2 * j], rec_mid, o.key, 0)
            sort_pass(nc, k, name + "_high", rec_mid, k.edge_table[2 * j + 1], o.rec, o.key, 8)
            order_masks(nc, k, name + "_masks", o)
    first_norm(nc, k, A)

    k.att = sb("att", [P, HEADS, C])
    with nc.sbuf_tensor("edge_v0", [P, C, D], F32) as k.edge_v:
        edge_scores(nc, k, "score0", by_dst, k.xn, k.l0, False)
        segment_softmax(nc, k, "soft0", by_dst, float(D) ** -0.5, True)
        add_attention(nc, k, "att0", by_dst, k.l0.wo)
    join_parts(nc, k, "join0", by_dst, k.x, D, True)
    self_relation(nc, k)
    add_relations(nc, k, "rel_dst", by_dst, 0)
    join_parts(nc, k, "join1", by_dst, k.x, D, True)
    add_relations(nc, k, "rel_src", by_src, 1)
    join_parts(nc, k, "join2", by_src, k.x, D, True)
    with nc.sbuf_tensor("edge_v2", [P, C, D], F32) as k.edge_v:
        edge_scores(nc, k, "score2", by_dst, k.x, k.l2, True)
        segment_softmax(nc, k, "soft2", by_dst, float(HD) ** -0.5, False)
        add_attention(nc, k, "att2", by_dst, k.l2.wo)
    join_parts(nc, k, "join3", by_dst, k.x, D, True)
    last_norm(nc, k)
    for r in range(2):
        sum_neighbours(nc, k, f"sum{r}", by_src)
        join_parts(nc, k, f"joins{r}", by_src, k.sums, SUMW, False)
        update_nodes(nc, k, A, out, r)


INPUTS = ["x", "src", "dst", "edge_attr_8", "edge_attr_8_n2", "edge_type_8", "edge_weight1", "L0_gnn_gamma",
          "L0_gnn_beta", "L0_gnn_W_qkv", "L0_gnn_b_qkv", "L0_gnn_W_out", "L0_gnn_b_out", "L1_gnn_blocks",
          "L2_gnn_Wq", "L2_gnn_bq", "L2_gnn_Wk", "L2_gnn_bk", "L2_gnn_Wv", "L2_gnn_bv", "L2_gnn_Wo", "L2_gnn_bo",
          "L3_gnn_msg_W", "L3_gnn_msg_b", "L3_gnn_gru_Wih", "L3_gnn_gru_Whh", "L3_gnn_gru_bih", "L3_gnn_gru_bhh"]


def kernel(**inputs):
    import concourse.bacc as bacc
    from concourse.bass_utils import run_bass_kernel_spmd

    nc = bacc.Bacc("TRN2", target_bir_lowering=False, num_devices=1)
    arrays, args = {}, {}
    for name in INPUTS:
        a = np.ascontiguousarray(inputs[name])
        arrays[f"in_{name}"] = a
        args[name] = nc.dram_tensor(f"in_{name}", a.shape, mybir.dt.from_np(a.dtype), kind="ExternalInput").ap()
    out = nc.dram_tensor("out_x", (NODES, D), F32, kind="ExternalOutput").ap()
    build(nc, args, out)
    r = run_bass_kernel_spmd(nc, [arrays], core_ids=[0])
    return r.results[0]["out_x"]
```

```python
from contextlib import ExitStack

import numpy as np
import concourse.bass as bass
from concourse import mybir
from concourse.alu_op_type import AluOpType as ALU

F32, BF16, I32 = mybir.dt.float32, mybir.dt.bfloat16, mybir.dt.int32
F32R = mybir.dt.float32r
ACT = mybir.ActivationFunctionType
AXX = mybir.AxisListType.X

NODES, EDGES, D, HEADS = 50000, 25000, 128, 8
HD = D // HEADS
P = 128
RELS = 8
EPS = 1e-5
BIG = 1e30
UPPER = -4096

C = EDGES // 125
EP = EDGES // C
REC = 4 + HEADS
KEY_SRC, KEY_DST, TYPE, WEIGHT, ATTN = 0, 1, 2, 3, 4
BUCKETS = 256

PAD_NODE = NODES
FIX = NODES + P
FIX_DUMMY = FIX + 2 * P
DUMMY = FIX_DUMMY + 2 * P
STEPS = 8
ROWS = DUMMY + P * STEPS
SUMW = D + 2

G = 4
BLOCK = P * G
BLOCKS = -(-NODES // BLOCK)
TAIL = BLOCKS - 1
TAIL_P = (NODES - TAIL * BLOCK) // G


class Group:
    pass


def ds(i, n=1):
    return bass.ds(i, n)


def wait(eng, sem, value):
    if not isinstance(value, int) or value > 0:
        eng.wait_ge(sem, value)


def spread(ap, axis, n):
    shape = list(ap.shape)
    shape[axis] = n
    return ap.broadcast_to(shape)


class Phase:

    def __init__(self, nc, name):
        self.nc, self.name, self.stack = nc, name, ExitStack()

    def __enter__(self):
        self.stack.enter_context(self.nc.cleanup_on_exit())
        self.gate = self.sem("gate")
        return self

    def __exit__(self, *said):
        self.stack.__exit__(*said)
        self.nc.all_engine_barrier()

    def sb(self, name, shape, dt=F32):
        return self.nc.alloc_sbuf_tensor(f"{self.name}_{name}", shape, dt)

    def ps(self, name, shape):
        parts, free = shape[0], shape[1:]
        size = int(np.prod(free))
        whole = self.nc.alloc_psum_tensor(f"{self.name}_{name}", [P, -(-size // 512) * 512], F32)
        used = whole[0:parts, 0:size]
        return used if len(free) == 1 else used.rearrange("p (a b) -> p a b", b=free[-1])

    def sem(self, name):
        return self.nc.alloc_semaphore(f"{self.name}_{name}")

    def held(self, eng, sem, value):
        wait(eng, sem, value)
        if not isinstance(value, int):
            eng.sem_inc(self.gate, 1)


def pipeline(eng, n, stages, unroll, alike=None):
    last = max(lag for lag, _ in stages)
    first = -(-(last + unroll) // unroll) * unroll
    turns = ((alike or n) - first) // unroll

    def tick(t):
        for lag, stage in stages:
            if 0 <= t - lag < n:
                stage(t - lag, (t - lag) % unroll, (t - lag) // unroll)

    for t in range(first):
        tick(t)
    with eng.Fori(0, turns) as turn:
        for u in range(unroll):
            for lag, stage in stages:
                at = first + u - lag
                stage(turn * unroll + at, at % unroll, turn + at // unroll)
    for t in range(first + turns * unroll, n + last):
        tick(t)


class Chain:

    def __init__(self, eng, sem):
        self.eng, self.sem, self.n = eng, sem, 0

    def __call__(self, instruction):
        self.n += 1
        instruction.then_inc(self.sem, 1)
        self.eng.wait_ge(self.sem, self.n)


def block_rows(table, i, width=D, at=0, rows=NODES):
    if isinstance(i, int) and i == TAIL:
        return table[TAIL * BLOCK:NODES, :].rearrange("(p a g) d -> p a (g d)", g=G, a=1)
    whole = table[0:TAIL * BLOCK, :].rearrange("(i p g) d -> p i (g d)", p=P, g=G)
    return whole[:, ds(i), :]


def block_tile(tile, s, i):
    n = TAIL_P if isinstance(i, int) and i == TAIL else P
    return tile[0:n, s:s + 1, :, :].rearrange("p s g d -> p s (g d)")


def split_upper(nc, upper, x):
    return nc.vector.tensor_scalar(upper.bitcast(I32), x.bitcast(I32), UPPER, None, ALU.bitwise_and)


def clear_rows_behind(k, eng, zero, cleared):
    flat = lambda t, a, n: t[a:a + n, :].rearrange("(p r) d -> p (r d)", p=P)
    for t, n in ((k.x, ROWS - NODES), (k.xn, P), (k.h, P), (k.sums, ROWS - NODES)):
        width = n // P * (SUMW if t is k.sums else D)
        eng.dma_start(flat(t, NODES, n), zero[:, 0:width]).then_inc(cleared, 16)
    return 4


def prepare(nc, k, A):
    with Phase(nc, "prep") as ph:
        NT = 24
        stage = ph.sb("stage", [P, NT, D])
        wb_col = ph.sb("wb_col", [P, 2, 2])
        iota_i = ph.sb("iota_i", [P, BUCKETS], I32)
        dummy_i = ph.sb("dummy_i", [P, C], I32)
        fix_i = ph.sb("fix_i", [P, 4], I32)
        ends = [ph.sb(f"end{j}", [P, C], I32) for j in range(3)]
        dist = ph.sb("dist", [P, C, HEADS])
        path = ph.sb("path", [P, C, HEADS])
        weight = ph.sb("weight", [P, C])
        wb_row = ph.sb("wb_row", [2, 2, D])
        brow = ph.sb("brow", [1, 4, 512])
        bres = ph.sb("bres", [1, 4, 512])
        bparts = ph.sb("bparts", [1, 3, 4, 512], BF16)
        gb_col = ph.sb("gb_col", [P, 2])
        folded = ph.ps("folded", [1, 384])
        turned = [ph.ps(f"turned{j}", [P, D]) for j in range(4)]
        loads, cleared, made, sent = ph.sem("loads"), ph.sem("cleared"), ph.sem("made"), ph.sem("sent")
        w_in, w_turned, w_kept, v_step = ph.sem("w_in"), ph.sem("w_turned"), ph.sem("w_kept"), ph.sem("v_step")
        parts_ready, fold_ready = ph.sem("parts_ready"), ph.sem("fold_ready")

        tiles = [(A["L0_gnn_W_qkv"][j * D:(j + 1) * D, :], k.l0.w[:, o:o + D]) for j, o in ((0, 0), (1, 256), (2, 128))]
        tiles += [(A["L0_gnn_W_out"], k.l0.wo[:, :])]
        tiles += [(w, k.l2.w[:, o:o + D]) for w, o in ((A["L2_gnn_Wq"], 0), (A["L2_gnn_Wk"], 256), (A["L2_gnn_Wv"], 128))]
        tiles += [(A["L2_gnn_Wo"], k.l2.wo[:, :])]
        for r in range(2):
            tiles += [(A["L3_gnn_msg_W"][r, :, j * D:(j + 1) * D], k.msg[:, r, j, :]) for j in range(2)]
            tiles += [(A["L3_gnn_gru_Wih"][r, j * D:(j + 1) * D, :], k.wih[:, r, o:o + D]) for j, o in ((0, D), (1, 2 * D), (2, 0))]
            tiles += [(A["L3_gnn_gru_Whh"][r, j * D:(j + 1) * D, :], k.whh[:, r, j * D:(j + 1) * D]) for j in range(3)]
        assert len(tiles) == NT
        row = lambda a: a.rearrange("(o n) -> o n", o=1)
        n_loads = 6 + 8 + 2 + 3 + 3 + HEADS
        with nc.Block() as block:
            @block.sync
            def _(sp):
                for t, (src, _) in enumerate(tiles):
                    sp.dma_start(stage[:, t, :], src).then_inc(w_in, 16)
                with nc.allow_non_contiguous_dma(reason="columns of 128 single elements, once"):
                    for r in range(2):
                        sp.dma_start(wb_col[:, r, 0:1], A["L3_gnn_msg_W"][r, :, 2 * D:2 * D + 1]).then_inc(w_in, 16)
                        sp.dma_start(wb_col[:, r, 1:2], A["L3_gnn_msg_b"][r, :].rearrange("(n o) -> n o", o=1)).then_inc(w_in, 16)
                    for j, src in enumerate((A["L0_gnn_gamma"], A["L0_gnn_beta"])):
                        sp.dma_start(gb_col[:, j:j + 1], src.rearrange("(n o) -> n o", o=1)).then_inc(w_in, 16)
                sp.wait_ge(cleared, 1)
                for dst, src in (
                    (brow[:, 0, 0:D], row(A["L0_gnn_b_qkv"][0:D])), (brow[:, 0, 256:384], row(A["L0_gnn_b_qkv"][D:2 * D])),
                    (brow[:, 0, D:256], row(A["L0_gnn_b_qkv"][2 * D:3 * D])),
                    (brow[:, 1, 0:D], row(A["L2_gnn_bq"])), (brow[:, 1, 256:384], row(A["L2_gnn_bk"])),
                    (brow[:, 1, D:256], row(A["L2_gnn_bv"])),
                ):
                    sp.dma_start(dst, src).then_inc(loads, 16)
                for r in range(2):
                    sp.dma_start(brow[:, 2 + r, 0:D], A["L3_gnn_gru_bih"][r:r + 1, 2 * D:3 * D]).then_inc(loads, 16)
                    sp.dma_start(brow[:, 2 + r, D:384], A["L3_gnn_gru_bih"][r:r + 1, 0:2 * D]).then_inc(loads, 16)
                    sp.dma_start(brow[:, 2 + r, 384:512], A["L3_gnn_gru_bhh"][r:r + 1, 2 * D:3 * D]).then_inc(loads, 16)
                    sp.dma_start(bres[:, 2 + r, D:384], A["L3_gnn_gru_bhh"][r:r + 1, 0:2 * D]).then_inc(loads, 16)
                for dst, src in ((k.b_out, A["L0_gnn_b_out"]), (k.bo, A["L2_gnn_bo"])):
                    sp.dma_start(dst[:, :], spread(row(src), 0, P)).then_inc(loads, 16)
                for j, src in enumerate((A["src"], A["dst"], A["edge_type_8"])):
                    sp.dma_start(ends[j][0:EP, :], src.rearrange("(p c) -> p c", c=C)).then_inc(loads, 16)
                sp.dma_start(weight[0:EP, :], A["edge_weight1"].rearrange("(p c) o -> p (c o)", c=C)).then_inc(loads, 16)
                sp.dma_start(dist[0:EP, :, :], A["edge_attr_8"].rearrange("(p c) h -> p c h", c=C)).then_inc(loads, 16)
                sp.dma_start(path[0:EP, :, :], A["edge_attr_8_n2"].rearrange("(p c) h -> p c h", c=C)).then_inc(loads, 16)
                for b in range(HEADS):
                    sp.dma_start(k.rel[b * HD:(b + 1) * HD, :, b * HD:(b + 1) * HD],
                                 A["L1_gnn_blocks"][:, b, :, :].rearrange("r i j -> i r j")).then_inc(loads, 16)
                sp.wait_ge(parts_ready, 1)
                for j in range(3):
                    sp.dma_start(k.bias3[j:j + 1, :, :], bparts[:, j, :, :]).then_inc(sent, 16)
                sp.wait_ge(w_kept, NT + 2)
                for g in range(G):
                    sp.dma_start(k.wb[2 * g:2 * g + 2, :, g, :], wb_row[:, :, :]).then_inc(sent, 16)
                sp.wait_ge(sent, 16 * (3 + G))

            @block.gpsimd
            def _(pool):
                pool.memset(k.ident[:, :], 0.0)
                pool.memset(k.identb[:, :], 0.0)
                pool.memset(k.before[:, :], 1.0)
                pool.memset(k.below[:, :], 0.0)
                pool.memset(k.ones[:, :], 1.0)
                pool.memset(k.onesb[:, :], 1.0)
                pool.memset(k.eps[:, :], EPS)
                pool.memset(bres[:, :, :], 0.0)
                pool.memset(brow[:, :, :], 0.0)
                pool.memset(k.rel[:, :, :], 0.0)
                pool.memset(k.wb[:, :, :, :], 0.0)
                for e in ends:
                    pool.memset(e[:, :], PAD_NODE)
                pool.memset(weight[:, :], 0.0)
                pool.memset(dist[:, :, :], 0.0)
                pool.memset(path[:, :, :], 0.0).then_inc(cleared, 1)
                pool.wait_ge(cleared, 1)
                for m in (k.ident, k.identb):
                    pool.affine_select(out=m[:, :], in_=m[:, :], compare_op=ALU.not_equal, fill=1.0, base=0,
                                       pattern=[[-1, P]], channel_multiplier=1)
                pool.affine_select(out=k.before[:, :], in_=k.before[:, :], compare_op=ALU.is_ge, fill=0.0, base=-1,
                                   pattern=[[1, P]], channel_multiplier=-1)
                pool.affine_select(out=k.below[:, :], in_=k.below[:, :], compare_op=ALU.not_equal, fill=1.0, base=-1,
                                   pattern=[[-1, P]], channel_multiplier=1)
                pool.iota(iota_i[:, :], pattern=[[1, BUCKETS]], base=0, channel_multiplier=0)
                pool.iota(dummy_i[:, :], pattern=[[0, C // STEPS], [P, STEPS]], base=DUMMY, channel_multiplier=1)
                pool.iota(fix_i[:, :], pattern=[[P, 4]], base=FIX, channel_multiplier=1).then_inc(made, 1)

            @block.scalar
            def _(act):
                for t, (_, dst) in enumerate(tiles):
                    act.wait_ge(w_turned, t + 1)
                    act.copy(dst, turned[t % 4][:, :]).then_inc(w_kept, 1)
                for r in range(2):
                    act.wait_ge(w_turned, NT + r + 1)
                    act.copy(wb_row[:, r, :], turned[(NT + r) % 4][0:2, :]).then_inc(w_kept, 1)
                act.wait_ge(fold_ready, 1)
                act.activation(k.l0.w[:, :], k.l0.w[:, :], ACT.Copy, scale=gb_col[:, 0:1]).then_inc(w_kept, 1)
                act.wait_ge(w_kept, NT + 3)

            @block.tensor
            def _(pe):
                pe.wait_ge(made, 1)
                pe.wait_ge(w_in, 16 * (NT + 6))
                for t in range(NT):
                    wait(pe, w_kept, t - 3)
                    pe.transpose(turned[t % 4][:, :], stage[:, t, :], k.ident[:, :]).then_inc(w_turned, 1)
                for r in range(2):
                    t = NT + r
                    pe.wait_ge(w_kept, t - 3)
                    pe.transpose(turned[t % 4][0:2, :], wb_col[:, r, :], k.ident[:, :]).then_inc(w_turned, 1)
                pe.wait_ge(w_kept, NT + 2)
                pe.matmul(folded[:, :], gb_col[:, 1:2], k.l0.w[:, :], start=True, stop=True).then_inc(fold_ready, 1)

            @block.vector
            def _(dve):
                link = Chain(dve, v_step)
                dve.wait_ge(loads, 16 * n_loads)
                dve.wait_ge(made, 1)
                nc.vector.tensor_copy(k.iota[:, :], iota_i[:, :])
                nc.vector.tensor_copy(k.dummy[:, :], dummy_i[:, :])
                nc.vector.tensor_copy(k.fix[:, :], fix_i[:, :])
                for j in range(3):
                    nc.vector.tensor_copy(k.rec0[:, :, j], ends[j][:, :])
                nc.vector.tensor_copy(k.rec0[:, :, WEIGHT], weight[:, :])
                nc.vector.tensor_tensor(k.rec0[:, :, ATTN:REC], dist[:, :, :], path[:, :, :], ALU.add)
                dve.wait_ge(fold_ready, 1)
                link(nc.vector.tensor_tensor(brow[:, 0, 0:384], brow[:, 0, 0:384], folded[:, :], ALU.add))
                link(nc.vector.tensor_tensor(brow[:, :, :], brow[:, :, :], bres[:, :, :], ALU.add))
                for j in range(3):
                    link(nc.vector.tensor_copy(bparts[:, j, :, :], brow[:, :, :]))
                    link(nc.vector.tensor_tensor(brow[:, :, :], brow[:, :, :], bparts[:, j, :, :], ALU.subtract))
                nc.vector.tensor_copy(k.selfw[:, :], k.rel[:, RELS, :]).then_inc(parts_ready, 1)


def take_digits(nc, link, p, key_i, digit_i):
    link(nc.vector.tensor_copy(key_i[:, :], p.rec_in[:, :, p.key]))
    if p.shift:
        link(nc.vector.tensor_scalar(digit_i[:, :], key_i[:, :], p.shift, None, ALU.logical_shift_right))
    else:
        link(nc.vector.tensor_scalar(digit_i[:, :], key_i[:, :], BUCKETS - 1, None, ALU.bitwise_and))
    link(nc.vector.tensor_copy(p.digit[:, :], digit_i[:, :]))


def count_digits(nc, k, name, p):
    with Phase(nc, name) as ph:
        U = 8
        key_i, digit_i = ph.sb("key_i", [P, C], I32), ph.sb("digit_i", [P, C], I32)
        hit = ph.sb("hit", [P, U, BUCKETS], BF16)
        counts = ph.ps("counts", [P, BUCKETS])
        v_step, hit_ready, counted = ph.sem("v_step"), ph.sem("hit_ready"), ph.sem("counted")

        with nc.Block() as block:
            @block.vector
            def _(dve):
                take_digits(nc, Chain(dve, v_step), p, key_i, digit_i)

                def hits(c, u, turn):
                    wait(dve, counted, c - U + 1)
                    nc.vector.tensor_scalar(hit[:, u, :], k.iota[:, :], p.digit[:, ds(c)], None, ALU.is_equal)\
                        .then_inc(hit_ready, 1)

                pipeline(dve, C, [(0, hits)], U)
                dve.wait_ge(counted, C)
                nc.vector.tensor_copy(p.own[:, :], counts[:, :])

            @block.tensor
            def _(pe):
                def count(c, u, turn):
                    wait(pe, hit_ready, c + 1)
                    pe.matmul(counts[:, :], k.identb[:, :], hit[:, u, :], start=isinstance(c, int) and c == 0,
                              stop=False, skip_group_check=True).then_inc(counted, 1)

                pipeline(pe, C, [(0, count)], U)


def sort_pass(nc, k, name, p, following=None):
    with Phase(nc, name) as ph:
        U = 8
        hit = ph.sb("hit", [P, U, BUCKETS], BF16)
        zeros = ph.sb("zeros", [P, BUCKETS])
        total = ph.sb("total", [P, BUCKETS])
        start = ph.sb("start", [P, BUCKETS])
        picked = ph.sb("picked", [P, 2, BUCKETS])
        place = ph.sb("place", [P, U, 1])
        place_i = ph.sb("place_i", [P, U, 1], I32)
        row = ph.sb("row", [P, U, REC])
        totals = ph.ps("totals", [P, BUCKETS])
        cursor = ph.ps("cursor", [P, BUCKETS])
        v_step, totals_ready, start_ready = ph.sem("v_step"), ph.sem("totals_ready"), ph.sem("start_ready")
        hit_ready, cursor_ready, picked_ready, place_ready = (ph.sem(s) for s in ("hit_ready", "cursor_ready", "picked_ready", "place_ready"))
        row_ready, loaded = ph.sem("row_ready"), ph.sem("loaded")
        stored = [ph.sem(f"stored{u}") for u in range(U)]
        if following:
            key_i, digit_i = ph.sb("key_i", [P, C], I32), ph.sb("digit_i", [P, C], I32)
            hit_f = ph.sb("hit_f", [P, U, BUCKETS], BF16)
            counts_f = ph.ps("counts_f", [P, BUCKETS])
            hit_f_ready, counted_f = ph.sem("hit_f_ready"), ph.sem("counted_f")

        with nc.Block() as block:
            @block.vector
            def _(dve):
                link = Chain(dve, v_step)
                nc.vector.memset(zeros[:, :], 0.0)
                dve.wait_ge(totals_ready, 1)
                link(nc.vector.tensor_copy(total[:, :], totals[:, :]))
                link(nc.vector.tensor_tensor_scan(start[:, :], zeros[:, :], total[:, :], 0.0, ALU.add, ALU.add))
                nc.vector.tensor_tensor(start[:, :], start[:, :], total[:, :], ALU.subtract).then_inc(start_ready, 1)
                if following:
                    take_digits(nc, link, following, key_i, digit_i)

                def hits(c, u, turn):
                    wait(dve, cursor_ready, c - U + 2)
                    nc.vector.tensor_scalar(hit[:, u, :], k.iota[:, :], p.digit[:, ds(c)], None, ALU.is_equal)\
                        .then_inc(hit_ready, 1)

                def places(c, u, turn):
                    wait(dve, hit_ready, c + 1)
                    wait(dve, cursor_ready, c + 1)
                    nc.vector.tensor_tensor_reduce(out=picked[:, u % 2, :], in0=cursor[:, :], in1=hit[:, u, :],
                                                   scale=1.0, scalar=0.0, op0=ALU.mult, op1=ALU.add,
                                                   accum_out=place[:, u, :]).then_inc(picked_ready, 1)

                def places_int(c, u, turn):
                    wait(dve, picked_ready, c + 1)
                    wait(dve, stored[u], 16 * turn)
                    nc.vector.tensor_copy(place_i[:, u, :], place[:, u, :]).then_inc(place_ready, 1)

                def hits_following(c, u, turn):
                    wait(dve, counted_f, c - U + 1)
                    nc.vector.tensor_scalar(hit_f[:, u, :], k.iota[:, :], following.digit[:, ds(c)], None,
                                            ALU.is_equal).then_inc(hit_f_ready, 1)

                stages = [(0, hits), (1, places)] + ([(0, hits_following)] if following else []) + [(2, places_int)]
                pipeline(dve, C, stages, U)
                if following:
                    dve.wait_ge(counted_f, C)
                    nc.vector.tensor_copy(following.own[:, :], counts_f[:, :])

            @block.tensor
            def _(pe):
                pe.matmul(totals[:, :], k.onesb[:, :], p.own[:, :], start=True, stop=True).then_inc(totals_ready, 1)
                pe.wait_ge(start_ready, 1)
                pe.matmul(cursor[:, :], k.before[:, :], p.own[:, :], start=True, stop=False, skip_group_check=True)
                pe.matmul(cursor[:, :], k.ident[:, :], start[:, :], start=False, stop=False,
                          skip_group_check=True).then_inc(cursor_ready, 1)

                def advance(c, u, turn):
                    wait(pe, picked_ready, c + 1)
                    pe.matmul(cursor[:, :], k.identb[:, :], hit[:, u, :], start=False, stop=False,
                              skip_group_check=True).then_inc(cursor_ready, 1)

                def count_following(c, u, turn):
                    wait(pe, hit_f_ready, c + 1)
                    pe.matmul(counts_f[:, :], k.identb[:, :], hit_f[:, u, :], start=isinstance(c, int) and c == 0,
                              stop=False, skip_group_check=True).then_inc(counted_f, 1)

                pipeline(pe, C, [(0, advance)] + ([(0, count_following)] if following else []), U)

            @block.scalar
            def _(act):
                def record(c, u, turn):
                    ph.held(act, stored[u], 16 * turn)
                    act.copy(row[:, u:u + 1, :], p.rec_in[:, ds(c), :]).then_inc(row_ready, 1)

                pipeline(act, C, [(0, record)], U)
                for u in range(U):
                    act.wait_ge(stored[u], 16 * C // U)
                act.dma_start(p.rec_out[:, :, :], p.table[:, :].rearrange("(p c) w -> p c w", c=C)).then_inc(loaded, 16)
                act.wait_ge(loaded, 16)

            @block.gpsimd
            def _(pool):
                def store(c, u, turn):
                    ph.held(pool, row_ready, c + 1)
                    ph.held(pool, place_ready, c + 1)
                    pool.indirect_dma_start(p.table, bass.IndirectOffsetOnAxis(ap=place_i[:, u, :], axis=0),
                                            row[:, u, :], None).then_inc(stored[u], 16)

                pipeline(pool, C, [(0, store)], U)


def order_masks(nc, k, name, o):
    with Phase(nc, name) as ph:
        key = o.rec[:, :, o.key]
        f_first = ph.sb("t0", [P, C])
        t1 = ph.sb("t1", [P, C])
        t2 = ph.sb("t2", [P, C])
        kdiag = ph.sb("kdiag", [P, 2, P])
        kwide = ph.sb("kwide", [P, 2, HEADS])
        nextk = ph.sb("nextk", [P, 2])
        own = ph.sb("own", [P, 2])
        kseq = ph.sb("kseq", [HEADS, P, 2])
        ktile = ph.sb("ktile", [P, 2, 1])
        kb = ph.ps("kb", [P, 2, P])
        kn = ph.ps("kn", [P, 2])
        ks = ph.ps("ks", [HEADS, 2, P])
        v_step, keys_ready, keys_wide = ph.sem("v_step"), ph.sem("keys_ready"), ph.sem("keys_wide")

        with nc.Block() as block:
            @block.vector
            def _(dve):
                link = Chain(dve, v_step)
                k0, k1 = ktile[:, 0, :], ktile[:, 1, :]
                link(nc.vector.tensor_copy(ktile[:, 0, :], o.rec[:, 0, o.key:o.key + 1]))
                link(nc.vector.tensor_copy(ktile[:, 1, :], o.rec[:, C - 1, o.key:o.key + 1]))
                for j in range(2):
                    nc.vector.tensor_scalar(kdiag[:, j, :], k.ident[:, :], ktile[:, j, :], None, ALU.mult)
                    last = nc.vector.tensor_scalar(kwide[:, j, :], k.ones[:, 0:HEADS], ktile[:, j, :], None, ALU.mult)
                last.then_inc(keys_ready, 1)
                nc.vector.memset(o.same[:, 0:1], 0.0)
                nc.vector.memset(o.notlast[:, C - 1:C], 0.0)
                nc.vector.tensor_tensor(o.same[:, 1:C], key[:, 1:C], key[:, 0:C - 1], ALU.is_equal)
                link(nc.vector.tensor_tensor(o.notlast[:, 0:C - 1], key[:, 1:C], key[:, 0:C - 1], ALU.is_equal))
                nc.vector.tensor_scalar(o.last[:, :], o.notlast[:, :], -1.0, 1.0, ALU.mult, ALU.add)
                nc.vector.tensor_scalar(o.pen[:, :], o.same[:, :], 1.0, BIG, ALU.subtract, ALU.mult)
                nc.vector.tensor_scalar(o.first[:, :], key, k0, None, ALU.is_equal)
                link(nc.vector.tensor_scalar(t1[:, :], key, k1, None, ALU.is_equal))
                link(nc.vector.tensor_tensor(t2[:, :], t1[:, :], o.first[:, :], ALU.mult))
                link(nc.vector.tensor_tensor(o.final[:, :], t1[:, :], t2[:, :], ALU.subtract))
                link(nc.vector.tensor_tensor(t1[:, :], o.first[:, :], o.final[:, :], ALU.add))
                link(nc.vector.tensor_scalar(o.middle[:, :], t1[:, :], -1.0, 1.0, ALU.mult, ALU.add))
                link(nc.vector.tensor_tensor(t1[:, :], key, o.middle[:, :], ALU.mult))
                link(nc.vector.scalar_tensor_tensor(t2[:, :], o.first[:, :], k.fix[:, 0:1], t1[:, :], ALU.mult, ALU.add))
                link(nc.vector.scalar_tensor_tensor(t1[:, :], o.final[:, :], k.fix[:, 1:2], t2[:, :], ALU.mult, ALU.add))
                link(nc.vector.tensor_tensor(t2[:, :], t1[:, :], o.last[:, :], ALU.mult))
                link(nc.vector.tensor_tensor(t1[:, :], k.dummy[:, :], o.notlast[:, :], ALU.mult))
                link(nc.vector.tensor_tensor(o.target[:, :], t1[:, :], t2[:, :], ALU.add))
                dve.wait_ge(keys_wide, 1)
                for a in range(2):
                    for b in range(2):
                        nc.vector.tensor_scalar(o.join[:, a, b, :], kb[:, b, :], ktile[:, a, :], None, ALU.is_equal)
                nc.vector.tensor_copy(nextk[:, 0:1], k1)
                link(nc.vector.tensor_copy(nextk[:, 1:2], kn[:, 0:1]))
                nc.vector.tensor_tensor(o.split[:, :], k0, k1, ALU.not_equal)
                nc.vector.tensor_tensor(own[:, 0:1], k0, k1, ALU.not_equal)
                link(nc.vector.tensor_tensor(own[:, 1:2], k1, nextk[:, 1:2], ALU.not_equal))
                link(nc.vector.tensor_tensor(t1[:, 0:2], ktile[:, :, 0], k.fix[:, 2:4], ALU.subtract))
                link(nc.vector.tensor_tensor(t2[:, 0:2], t1[:, 0:2], own[:, :], ALU.mult))
                link(nc.vector.tensor_tensor(o.fix_target[:, :], t2[:, 0:2], k.fix[:, 2:4], ALU.add))
                for j in range(2):
                    last = nc.vector.tensor_copy(kseq[:, :, j], ks[:, j, :])
                link(last)
                seq = kseq[:, :, :].rearrange("h p j -> h (p j)")
                nc.vector.memset(o.seq_same[:, 0:1], 0.0)
                nc.vector.memset(o.seq_notlast[:, 2 * P - 1:2 * P], 0.0)
                nc.vector.tensor_tensor(o.seq_same[:, 1:2 * P], seq[:, 1:2 * P], seq[:, 0:2 * P - 1], ALU.is_equal)
                link(nc.vector.tensor_tensor(o.seq_notlast[:, 0:2 * P - 1], seq[:, 1:2 * P], seq[:, 0:2 * P - 1],
                                             ALU.is_equal))
                nc.vector.tensor_scalar(o.seq_last[:, :], o.seq_notlast[:, :], -1.0, 1.0, ALU.mult, ALU.add)
                link(nc.vector.tensor_scalar(o.seq_pen[:, :], o.seq_same[:, :], 1.0, BIG, ALU.subtract, ALU.mult))
                nc.vector.tensor_copy(o.tail[:, :, 0], o.rec[:, :, WEIGHT])
                nc.vector.memset(o.tail[:, :, 1], 1.0)
                link(nc.vector.tensor_copy(o.ends[:, :, :], o.rec[:, :, KEY_SRC:KEY_DST + 1]))

            @block.tensor
            def _(pe):
                pe.wait_ge(keys_ready, 1)
                for j in range(2):
                    pe.matmul(kb[:, j, :], k.ones[:, :], kdiag[:, j, :], start=True, stop=True)
                    pe.matmul(ks[:, j, :], kwide[:, j, :], k.ident[:, :], start=True, stop=True)
                pe.matmul(kn[:, 0:1], k.below[:, :], ktile[:, 0, :], start=True, stop=True).then_inc(keys_wide, 1)


def dense_stats(nc, ph, dve, m, s, i, rows):
    for g in range(G):
        last = nc.vector.bn_stats(m.stats[:, s, g, :], rows[:, g, :])
    last.then_inc(m.stats_done, 1)
    ph.held(dve, m.stats_done, i + 1)
    for g in range(G):
        last = nc.vector.bn_aggr(m.moments[:, s, g, :], m.stats[:, s, g, :])
    last.then_inc(m.moments_done, 1)


def row_roots(act, k, m, s, i):
    wait(act, m.moments_done, i + 1)
    act.activation(m.root[:, s, :], m.moments[:, s, :, 1], ACT.Sqrt, bias=k.eps[:, :]).then_inc(m.root_done, 1)


def row_scales(nc, dve, m, s, i):
    wait(dve, m.root_done, i + 1)
    nc.vector.reciprocal(m.scale[:, s, :], m.root[:, s, :]).then_inc(m.scale_done, 1)
    wait(dve, m.scale_done, i + 1)
    nc.vector.scalar_tensor_tensor(m.shift[:, s, :], m.moments[:, s, :, 0], -1.0, m.scale[:, s, :],
                                   ALU.mult, ALU.mult).then_inc(m.ready, 1)


def moments_of(ph, name, slots, g=G):
    m = Group()
    m.stats, m.moments = ph.sb(name + "_stats", [P, slots, g, 6]), ph.sb(name + "_moments", [P, slots, g, 2])
    m.root, m.scale = ph.sb(name + "_root", [P, slots, g]), ph.sb(name + "_scale", [P, slots, g])
    m.shift = ph.sb(name + "_shift", [P, slots, g])
    m.stats_done, m.moments_done = ph.sem(name + "_stats_done"), ph.sem(name + "_moments_done")
    m.root_done, m.scale_done, m.ready = ph.sem(name + "_root_done"), ph.sem(name + "_scale_done"), ph.sem(name + "_ready")
    return m


def first_norm(nc, k, A):
    with Phase(nc, "norm0") as ph:
        U = 8
        x = ph.sb("x", [P, U, G, D])
        h = ph.sb("h", [P, U, G, D])
        xn = ph.sb("xn", [P, U, G, D])
        xo = ph.sb("xo", [P, U, G, D])
        zero = ph.sb("zero", [P, 1, (ROWS - NODES) // P * SUMW])
        zero_ready, cleared = ph.sem("zero_ready"), ph.sem("cleared")
        mx, mh = moments_of(ph, "mx", U), moments_of(ph, "mh", U)
        x_in = [ph.sem(f"x_in{u}") for u in range(U)]
        out_x = [ph.sem(f"out_x{u}") for u in range(U)]
        out_n = [ph.sem(f"out_n{u}") for u in range(U)]
        h_done, n_done, biased, xo_ready = ph.sem("h_done"), ph.sem("n_done"), ph.sem("biased"), ph.sem("xo_ready")
        n_done_v = ph.sem("n_done_v")
        OWN = G - 2
        b_out = spread(k.b_out[:, :].rearrange("p (g d) -> p g d", g=1), 1, G)

        with nc.Block() as block:
            @block.sync
            def _(sp):
                def load(i, s, turn):
                    wait(sp, h_done, i - U + 1)
                    wait(sp, biased, i - U + 1)
                    sp.dma_start(block_tile(x, s, i), block_rows(A["x"], i)).then_inc(x_in[s], 16)

                def store(i, s, turn):
                    wait(sp, xo_ready, i + 1)
                    sp.dma_start(block_rows(k.x, i), block_tile(xo, s, i)).then_inc(out_x[s], 16)

                def store_norm(i, s, turn):
                    wait(sp, n_done, i + 1)
                    wait(sp, n_done_v, i + 1)
                    sp.dma_start(block_rows(k.xn, i), block_tile(xn, s, i)).then_inc(out_n[s], 16)

                def clear_sums(i, s, turn):
                    n = TAIL_P if isinstance(i, int) and i == TAIL else P
                    sp.dma_start(block_rows(k.sums, i, SUMW), zero[0:n, :, 0:G * SUMW]).then_inc(cleared, 16)

                sp.wait_ge(zero_ready, 1)
                behind = clear_rows_behind(k, sp, zero[:, 0, :], cleared)

                pipeline(sp, BLOCKS, [(0, load), (6, store), (9, store_norm), (3, clear_sums)], U, TAIL)
                for s in range(U):
                    sp.wait_ge(out_x[s], 16 * len(range(s, BLOCKS, U)))
                    sp.wait_ge(out_n[s], 16 * len(range(s, BLOCKS, U)))
                sp.wait_ge(cleared, 16 * (BLOCKS + behind))

            @block.vector
            def _(dve):
                def x_stats(i, s, turn):
                    wait(dve, x_in[s], 16 * (turn + 1))
                    dense_stats(nc, ph, dve, mx, s, i, x[:, s])

                def x_scales(i, s, turn):
                    row_scales(nc, dve, mx, s, i)

                def h_scales(i, s, turn):
                    row_scales(nc, dve, mh, s, i)

                def h_stats(i, s, turn):
                    wait(dve, h_done, i + 1)
                    dense_stats(nc, ph, dve, mh, s, i, h[:, s])

                def norm(i, s, turn):
                    wait(dve, mh.ready, i + 1)
                    wait(dve, out_n[s], 16 * turn)
                    for g in range(OWN, G):
                        last = nc.vector.tensor_scalar(xn[:, s, g, :], h[:, s, g, :], mh.scale[:, s, g:g + 1],
                                                       mh.shift[:, s, g:g + 1], ALU.mult, ALU.add)
                    last.then_inc(n_done_v, 1)

                pipeline(dve, BLOCKS, [(0, x_stats), (1, x_scales), (3, h_stats), (4, h_scales), (5, norm)], U, TAIL)

            @block.scalar
            def _(act):
                def relu(i, s, turn):
                    wait(act, n_done, i - U + 1)
                    wait(act, n_done_v, i - U + 1)
                    wait(act, xo_ready, i - U + 1)
                    wait(act, mx.ready, i + 1)
                    for g in range(G):
                        last = act.activation(h[:, s, g, :], x[:, s, g, :], ACT.Relu,
                                              bias=mx.shift[:, s, g:g + 1], scale=mx.scale[:, s, g:g + 1])
                    last.then_inc(h_done, 1)

                def norm(i, s, turn):
                    wait(act, out_n[s], 16 * turn)
                    wait(act, mh.ready, i + 1)
                    for g in range(OWN):
                        last = act.activation(xn[:, s, g, :], h[:, s, g, :], ACT.Identity,
                                              bias=mh.shift[:, s, g:g + 1], scale=mh.scale[:, s, g:g + 1])
                    last.then_inc(n_done, 1)

                def x_roots(i, s, turn):
                    row_roots(act, k, mx, s, i)

                def h_roots(i, s, turn):
                    row_roots(act, k, mh, s, i)

                pipeline(act, BLOCKS, [(0, x_roots), (1, relu), (3, h_roots), (4, norm)], U, TAIL)

            @block.gpsimd
            def _(pool):
                pool.memset(zero[:, :, :], 0.0).then_inc(zero_ready, 1)

                def bias(i, s, turn):
                    wait(pool, x_in[s], 16 * (turn + 1))
                    wait(pool, out_x[s], 16 * turn)
                    nc.gpsimd.tensor_tensor(xo[:, s], x[:, s], b_out, ALU.add).then_inc(biased, 1)

                def add_h(i, s, turn):
                    wait(pool, h_done, i + 1)
                    wait(pool, biased, i + 1)
                    nc.gpsimd.tensor_tensor(xo[:, s], xo[:, s], h[:, s], ALU.add).then_inc(xo_ready, 1)

                pipeline(pool, BLOCKS, [(0, bias), (2, add_h)], U, TAIL)


def edge_scores(nc, k, name, o, table, L, normed):
    with Phase(nc, name) as ph:
        U = 8
        idx = ph.sb("idx", [P, U, 2], I32)
        rows = [[ph.sb(f"rows{u}{j}", [P, D]) for j in range(2)] for u in range(U)]
        act_rows = ph.sb("act_rows", [P, 2, 2, D]) if normed else None
        turned_sb = ph.sb("turned_sb", [P, 2, 2, D])
        k_sb = ph.sb("k_sb", [P, 2, D])
        prod = ph.sb("prod", [P, 2, D])
        turned = [ph.ps(f"turned{j}", [P, 2, D]) for j in range(2)]
        qvk = [ph.ps(f"qvk{j}", [P, 512]) for j in range(2)]
        idx_ready, turned_ready, turned_kept = ph.sem("idx_ready"), ph.sem("turned_ready"), ph.sem("turned_kept")
        qvk_ready, kv_kept, prod_ready, scores_done = ph.sem("qvk_ready"), ph.sem("kv_kept"), ph.sem("prod_ready"), ph.sem("scores_done")
        gathered = [ph.sem(f"gathered{u}") for u in range(U)]
        relu_done = ph.sem("relu_done")
        m = moments_of(ph, "m", 2, 2) if normed else None

        with nc.Block() as block:
            @block.gpsimd
            def _(pool):
                def gather(c, u, turn):
                    ph.held(pool, idx_ready, c + 1)
                    ph.held(pool, relu_done if normed else turned_ready, c - U + 1)
                    for j in range(2):
                        pool.indirect_dma_start(rows[u][j][:, :], None, table,
                                                bass.IndirectOffsetOnAxis(ap=idx[:, u, j:j + 1], axis=0))\
                            .then_inc(gathered[u], 16)

                pipeline(pool, C, [(0, gather)], U)

            @block.vector
            def _(dve):
                def index(c, u, turn):
                    ph.held(dve, gathered[u], 32 * turn)
                    nc.vector.tensor_copy(idx[:, u:u + 1, :], o.ends[:, ds(c), :]).then_inc(idx_ready, 1)

                def moments(c, u, turn):
                    s = u % 2
                    wait(dve, gathered[u], 32 * (turn + 1))
                    for j in range(2):
                        last = nc.vector.bn_stats(m.stats[:, s, j, :], rows[u][j][:, :])
                    last.then_inc(m.stats_done, 1)
                    ph.held(dve, m.stats_done, c + 1)
                    for j in range(2):
                        last = nc.vector.bn_aggr(m.moments[:, s, j, :], m.stats[:, s, j, :])
                    last.then_inc(m.moments_done, 1)

                def scales(c, u, turn):
                    wait(dve, relu_done, c - 1)
                    row_scales(nc, dve, m, u % 2, c)

                def product(c, u, turn):
                    s = u % 2
                    wait(dve, kv_kept, c + 1)
                    wait(dve, scores_done, c - 1)
                    nc.vector.tensor_tensor(prod[:, s, :], qvk[s][:, 0:D], k_sb[:, s, :], ALU.mult)\
                        .then_inc(prod_ready, 1)

                def head_sums(c, u, turn):
                    s = u % 2
                    ph.held(dve, prod_ready, c + 1)
                    nc.vector.tensor_reduce(k.att[:, :, ds(c)], prod[:, s, :].rearrange("p (h e) -> p h e", e=HD),
                                            axis=AXX, op=ALU.add).then_inc(scores_done, 1)

                stages = [(0, index)] + ([(4, moments), (5, scales)] if normed else [])
                stages += [(8, product), (9, head_sums)] if normed else [(6, product), (7, head_sums)]
                pipeline(dve, C, stages, U)

            @block.tensor
            def _(pe):
                def turn_rows(c, u, turn):
                    s = u % 2
                    wait(pe, turned_kept, c - 1)
                    if normed:
                        wait(pe, relu_done, c + 1)
                    else:
                        wait(pe, gathered[u], 32 * (turn + 1))
                    for j in range(2):
                        src = act_rows[:, s, j, :] if normed else rows[u][j][:, :]
                        last = pe.transpose(turned[s][:, j, :], src, k.ident[:, :])
                    last.then_inc(turned_ready, 1)

                def project(c, u, turn):
                    s = u % 2
                    wait(pe, turned_kept, c + 1)
                    wait(pe, prod_ready, c - 1)
                    pe.matmul(qvk[s][:, 0:384], k.onesb[0:3, :], k.bias3[:, L.bias, 0:384], start=True, stop=False)
                    pe.matmul(qvk[s][:, 0:256], turned_sb[:, s, 0, :], L.w[:, 0:256], start=False, stop=False)
                    pe.matmul(qvk[s][:, 256:384], turned_sb[:, s, 1, :], L.w[:, 256:384], start=False, stop=True)\
                        .then_inc(qvk_ready, 1)

                pipeline(pe, C, [(0, turn_rows), (1, project)], U)

            @block.scalar
            def _(act):
                def relu(c, u, turn):
                    s = u % 2
                    wait(act, turned_ready, c - 1)
                    wait(act, m.ready, c + 1)
                    for j in range(2):
                        last = act.activation(act_rows[:, s, j, :], rows[u][j][:, :], ACT.Relu,
                                              bias=m.shift[:, s, j:j + 1], scale=m.scale[:, s, j:j + 1])
                    last.then_inc(relu_done, 1)

                def keep_turned(c, u, turn):
                    s = u % 2
                    wait(act, turned_ready, c + 1)
                    wait(act, qvk_ready, c - 1)
                    act.copy(turned_sb[:, s, :, :], turned[s][:, :, :]).then_inc(turned_kept, 1)

                def keep_kv(c, u, turn):
                    s = u % 2
                    ph.held(act, qvk_ready, c + 1)
                    ph.held(act, prod_ready, c - 1)
                    act.copy(k_sb[:, s, :], qvk[s][:, 256:384])
                    act.copy(k.edge_v[:, ds(c), :], qvk[s][:, 128:256].rearrange("p (o d) -> p o d", o=1))\
                        .then_inc(kv_kept, 1)

                def roots(c, u, turn):
                    row_roots(act, k, m, u % 2, c)

                stages = [(0, roots), (1, relu), (2, keep_turned), (3, keep_kv)] if normed else \
                    [(1, keep_turned), (2, keep_kv)]
                pipeline(act, C, stages, U)


def segment_softmax(nc, k, name, o, scale, biased):
    with Phase(nc, name) as ph:
        a = k.att
        run = ph.sb("run", [P, HEADS, C])
        tmp = ph.sb("tmp", [P, HEADS, C])
        low = ph.sb("low", [P, 1])
        part = ph.sb("part", [P, 2, HEADS])
        total = ph.sb("total", [P, 2, HEADS])
        seq = ph.sb("seq", [HEADS, P, 2])
        seq_run = ph.sb("seq_run", [HEADS, 2 * P])
        seq_end = ph.sb("seq_end", [HEADS, 2 * P])
        seq_tot = ph.sb("seq_tot", [HEADS, 2 * P])
        seq_half = ph.sb("seq_half", [HEADS, 2, P])
        wide = ph.ps("wide", [HEADS, 2, P])
        tall = ph.ps("tall", [P, 2, HEADS])
        v_step, part_ready, wide_ready = ph.sem("v_step"), ph.sem("part_ready"), ph.sem("wide_ready")
        seq_ready, tall_ready, shifted, exps = ph.sem("seq_ready"), ph.sem("tall_ready"), ph.sem("shifted"), ph.sem("exps")
        per_head = lambda mask: spread(mask[:, :].rearrange("p (h c) -> p h c", h=1), 1, HEADS)
        V = nc.vector

        with nc.Block() as block:
            @block.vector
            def _(dve):
                link = Chain(dve, v_step)
                if biased:
                    attn = o.rec[:, :, ATTN:REC].rearrange("p c h -> p h c")
                    link(V.tensor_scalar(tmp[:, :, :], a[:, :, :], scale, None, ALU.mult))
                    link(V.tensor_tensor(a[:, :, :], tmp[:, :, :], attn, ALU.add))
                else:
                    link(V.tensor_scalar(a[:, :, :], a[:, :, :], scale, None, ALU.mult))

                def over_segments(step, state_in, state_op, value_op, start):
                    for h in range(HEADS):
                        last = V.tensor_tensor_scan(run[:, h, :], state_in[:, :], a[:, h, :], start, state_op, value_op)
                    link(last)
                    link(V.tensor_tensor(tmp[:, :, :], run[:, :, :], per_head(o.last), ALU.mult))
                    for h in range(HEADS):
                        last = V.tensor_tensor_scan(run[:, h, ::-1], o.notlast[:, ::-1], tmp[:, h, ::-1], 0.0,
                                                    ALU.mult, ALU.add)
                    link(last)
                    V.tensor_copy(part[:, 0, :], run[:, :, 0])
                    if state_op == ALU.mult:
                        last = V.tensor_scalar(part[:, 1, :], run[:, :, C - 1], o.split[:, :], None, ALU.mult)
                    else:
                        last = V.tensor_copy(part[:, 1, :], run[:, :, C - 1])
                    last.then_inc(part_ready, 1)
                    dve.wait_ge(wide_ready, step)
                    for j in range(2):
                        last = V.tensor_copy(seq[:, :, j], wide[:, j, :])
                    link(last)
                    seq_in = o.seq_pen if state_op == ALU.add else o.seq_same
                    link(V.tensor_tensor_scan(seq_run[:, :], seq_in[:, :], seq[:, :, :].rearrange("h p j -> h (p j)"),
                                              start, state_op, value_op))
                    link(V.tensor_tensor(seq_end[:, :], seq_run[:, :], o.seq_last[:, :], ALU.mult))
                    link(V.tensor_tensor_scan(seq_tot[:, ::-1], o.seq_notlast[:, ::-1], seq_end[:, ::-1], 0.0,
                                              ALU.mult, ALU.add))
                    V.tensor_copy(seq_half[:, :, :], seq_tot[:, :].rearrange("h (p j) -> h j p", j=2)).then_inc(seq_ready, 1)
                    dve.wait_ge(tall_ready, step)
                    link(V.tensor_copy(total[:, :, :], tall[:, :, :]))
                    link(V.tensor_tensor(run[:, :, :], run[:, :, :], per_head(o.middle), ALU.mult))
                    for mask, j in ((o.first, 0), (o.final, 1)):
                        for h in range(HEADS):
                            last = V.scalar_tensor_tensor(run[:, h, :], mask[:, :], total[:, j, h:h + 1], run[:, h, :],
                                                          ALU.mult, ALU.add)
                        link(last)

                over_segments(1, o.pen, ALU.add, ALU.max, -BIG)
                V.tensor_tensor(a[:, :, :], a[:, :, :], run[:, :, :], ALU.subtract).then_inc(shifted, 1)
                dve.wait_ge(exps, 1)
                over_segments(2, o.same, ALU.mult, ALU.add, 0.0)
                link(V.reciprocal(tmp[:, :, :], run[:, :, :]))
                link(V.tensor_tensor(a[:, :, :], a[:, :, :], tmp[:, :, :], ALU.mult))

            @block.scalar
            def _(act):
                act.wait_ge(shifted, 1)
                act.activation(a[:, :, :], a[:, :, :], ACT.Exp).then_inc(exps, 1)

            @block.tensor
            def _(pe):
                for step in (1, 2):
                    pe.wait_ge(part_ready, step)
                    for j in range(2):
                        last = pe.transpose(wide[:, j, :], part[:, j, :], k.ident[:, :])
                    last.then_inc(wide_ready, 1)
                    pe.wait_ge(seq_ready, step)
                    for j in range(2):
                        last = pe.transpose(tall[:, j, :], seq_half[:, j, :], k.ident[0:HEADS, 0:HEADS])
                    last.then_inc(tall_ready, 1)


def add_attention(nc, k, name, o, wo):
    with Phase(nc, name) as ph:
        U = 8
        idx = ph.sb("idx", [P, U, 1], I32)
        value = ph.sb("value", [P, U, D])
        state = ph.sb("state", [P, U, D])
        turned_sb = ph.sb("turned_sb", [P, 2, D])
        out = ph.sb("out", [P, U, D])
        turned = [ph.ps(f"turned{j}", [P, D]) for j in range(2)]
        mixed = [ph.ps(f"mixed{j}", [P, D]) for j in range(2)]
        idx_ready, value_ready, state_ready = ph.sem("idx_ready"), ph.sem("value_ready"), ph.sem("state_ready")
        turned_ready, turned_kept, mixed_ready, out_ready = ph.sem("turned_ready"), ph.sem("turned_kept"), ph.sem("mixed_ready"), ph.sem("out_ready")
        added = [ph.sem(f"added{u}") for u in range(U)]
        state_init = ph.sem("state_init")

        with nc.Block() as block:
            @block.vector
            def _(dve):
                nc.vector.memset(state[:, U - 1, :], 0.0).then_inc(state_init, 1)
                dve.wait_ge(state_init, 1)

                def weigh(c, u, turn):
                    ph.held(dve, added[u], 16 * turn)
                    nc.vector.tensor_copy(idx[:, u:u + 1, :], o.target[:, ds(c)].rearrange("p (a c) -> p a c", a=1))\
                        .then_inc(idx_ready, 1)
                    v = k.edge_v[:, ds(c), :].rearrange("p c (h e) -> p (c h) e", e=HD)
                    nc.vector.tensor_tensor(value[:, u, :].rearrange("p (h e) -> p h e", e=HD), v,
                                            spread(k.att[:, :, ds(c)], 2, HD), ALU.mult).then_inc(value_ready, 1)

                def accumulate(c, u, turn):
                    wait(dve, value_ready, c + 1)
                    wait(dve, turned_ready, c - U + 1)
                    wait(dve, state_ready, c)
                    nc.vector.scalar_tensor_tensor(state[:, u, :], state[:, (u - 1) % U, :], o.same[:, ds(c)],
                                                   value[:, u, :], ALU.mult, ALU.add).then_inc(state_ready, 1)

                pipeline(dve, C, [(0, weigh), (1, accumulate)], U)

            @block.tensor
            def _(pe):
                def turn_sums(c, u, turn):
                    wait(pe, state_ready, c + 1)
                    wait(pe, turned_kept, c - 1)
                    pe.transpose(turned[u % 2][:, :], state[:, u, :], k.ident[:, :]).then_inc(turned_ready, 1)

                def mix(c, u, turn):
                    wait(pe, turned_kept, c + 1)
                    wait(pe, out_ready, c - 1)
                    pe.matmul(mixed[u % 2][:, :], turned_sb[:, u % 2, :], wo[:, :], start=True, stop=True)\
                        .then_inc(mixed_ready, 1)

                pipeline(pe, C, [(0, turn_sums), (1, mix)], U)

            @block.scalar
            def _(act):
                def keep_turned(c, u, turn):
                    wait(act, turned_ready, c + 1)
                    wait(act, mixed_ready, c - 1)
                    act.copy(turned_sb[:, u % 2, :], turned[u % 2][:, :]).then_inc(turned_kept, 1)

                def keep_out(c, u, turn):
                    wait(act, mixed_ready, c + 1)
                    wait(act, added[u], 16 * turn)
                    act.copy(out[:, u, :], mixed[u % 2][:, :]).then_inc(out_ready, 1)

                pipeline(act, C, [(0, keep_turned), (1, keep_out)], U)

            @block.gpsimd
            def _(pool):
                def add(c, u, turn):
                    ph.held(pool, idx_ready, c + 1)
                    ph.held(pool, out_ready, c + 1)
                    pool.indirect_dma_start(k.x, bass.IndirectOffsetOnAxis(ap=idx[:, u, :], axis=0), out[:, u, :],
                                            None, compute_op=ALU.add).then_inc(added[u], 16)

                pipeline(pool, C, [(0, add)], U)
                for u in range(U):
                    pool.wait_ge(added[u], 16 * C // U)


def join_parts(nc, k, name, o, table, width, adding):
    with Phase(nc, name) as ph:
        part = ph.sb("part", [P, 2, width])
        out = [ph.sb(f"out{j}", [P, width]) for j in range(2)]
        zero = ph.sb("zero", [P, 2 * width])
        idx = ph.sb("idx", [P, 2], I32)
        total = ph.ps("total", [P, 2, 256])
        loaded, totals, ready, stored, cleared = ph.sem("loaded"), ph.sem("totals"), ph.sem("ready"), ph.sem("stored"), ph.sem("cleared")
        parts = table[FIX:FIX + 2 * P, :].rearrange("(j p) d -> p j d", p=P)

        with nc.Block() as block:
            @block.sync
            def _(sp):
                sp.dma_start(part[:, :, :], parts).then_inc(loaded, 16)
                if adding:
                    sp.wait_ge(loaded, 16)
                    sp.wait_ge(ready, 1)
                    sp.dma_start(parts, zero[:, :].rearrange("p (j d) -> p j d", j=2)).then_inc(cleared, 16)
                    sp.wait_ge(cleared, 16)

            @block.tensor
            def _(pe):
                pe.wait_ge(loaded, 16)
                for b in range(2):
                    for a in range(2):
                        last = pe.matmul(total[:, b, 0:width], o.join[:, a, b, :], part[:, a, :],
                                         start=(a == 0), stop=(a == 1))
                last.then_inc(totals, 1)

            @block.vector
            def _(dve):
                nc.vector.memset(zero[:, :], 0.0)
                nc.vector.tensor_copy(idx[:, :], o.fix_target[:, :]).then_inc(ready, 1)
                dve.wait_ge(totals, 1)
                for j in range(2):
                    nc.vector.tensor_copy(out[j][:, :], total[:, j, 0:width]).then_inc(ready, 1)

            @block.gpsimd
            def _(pool):
                pool.wait_ge(ready, 3)
                for j in range(2):
                    op = dict(compute_op=ALU.add) if adding else {}
                    pool.indirect_dma_start(table, bass.IndirectOffsetOnAxis(ap=idx[:, j:j + 1], axis=0),
                                            out[j][:, :], None, **op).then_inc(stored, 16)
                pool.wait_ge(stored, 32)


def self_relation(nc, k):
    with Phase(nc, "self") as ph:
        U = 8
        x = ph.sb("x", [P, U, G, D])
        h = ph.sb("h", [P, U, G, D])
        xo = ph.sb("xo", [P, U, G, D])
        h_t = ph.sb("h_t", [P, 2, G, D])
        m = moments_of(ph, "m", U)
        turned = [ph.ps(f"turned{j}", [P, G, D]) for j in range(2)]
        own = [ph.ps(f"own{j}", [P, G, D]) for j in range(2)]
        x_in = [ph.sem(f"x_in{u}") for u in range(U)]
        out_x = [ph.sem(f"out_x{u}") for u in range(U)]
        out_h = [ph.sem(f"out_h{u}") for u in range(U)]
        h_done, turned_ready, turned_kept, own_ready, xo_ready = (ph.sem(n) for n in ("h_done", "turned_ready", "turned_kept", "own_ready", "xo_ready"))

        with nc.Block() as block:
            @block.sync
            def _(sp):
                def load(i, s, turn):
                    wait(sp, xo_ready, i - U + 1)
                    sp.dma_start(block_tile(x, s, i), block_rows(k.x, i)).then_inc(x_in[s], 16)

                def store(i, s, turn):
                    wait(sp, h_done, i + 1)
                    sp.dma_start(block_rows(k.h, i), block_tile(h, s, i)).then_inc(out_h[s], 16)
                    wait(sp, xo_ready, i + 1)
                    sp.dma_start(block_rows(k.x, i), block_tile(xo, s, i)).then_inc(out_x[s], 16)

                pipeline(sp, BLOCKS, [(0, load), (5, store)], U, TAIL)
                for s in range(U):
                    sp.wait_ge(out_x[s], 16 * len(range(s, BLOCKS, U)))
                    sp.wait_ge(out_h[s], 16 * len(range(s, BLOCKS, U)))

            @block.vector
            def _(dve):
                def stats(i, s, turn):
                    wait(dve, x_in[s], 16 * (turn + 1))
                    dense_stats(nc, ph, dve, m, s, i, x[:, s])

                def scales(i, s, turn):
                    wait(dve, h_done, i - U + 1)
                    row_scales(nc, dve, m, s, i)

                def add(i, s, turn):
                    wait(dve, own_ready, i + 1)
                    wait(dve, out_x[s], 16 * turn)
                    nc.vector.tensor_tensor(xo[:, s], x[:, s], own[s % 2][:, :, :], ALU.add).then_inc(xo_ready, 1)

                pipeline(dve, BLOCKS, [(0, stats), (1, scales), (3, add)], U, TAIL)

            @block.scalar
            def _(act):
                def roots(i, s, turn):
                    row_roots(act, k, m, s, i)

                def relu(i, s, turn):
                    wait(act, turned_ready, i - U + 1)
                    wait(act, out_h[s], 16 * turn)
                    wait(act, m.ready, i + 1)
                    for g in range(G):
                        last = act.activation(h[:, s, g, :], x[:, s, g, :], ACT.Relu,
                                              bias=m.shift[:, s, g:g + 1], scale=m.scale[:, s, g:g + 1])
                    last.then_inc(h_done, 1)

                def keep(i, s, turn):
                    wait(act, turned_ready, i + 1)
                    wait(act, own_ready, i - 1)
                    act.copy(h_t[:, s % 2], turned[s % 2][:, :, :]).then_inc(turned_kept, 1)

                pipeline(act, BLOCKS, [(0, roots), (1, relu), (2, keep)], U, TAIL)

            @block.tensor
            def _(pe):
                def turn_rows(i, s, turn):
                    wait(pe, h_done, i + 1)
                    wait(pe, turned_kept, i - 1)
                    for g in range(G):
                        last = pe.transpose(turned[s % 2][:, g, :], h[:, s, g, :], k.ident[:, :])
                    last.then_inc(turned_ready, 1)

                def multiply(i, s, turn):
                    wait(pe, turned_kept, i + 1)
                    wait(pe, xo_ready, i - 1)
                    for g in range(G):
                        last = pe.matmul(own[s % 2][:, g, :], h_t[:, s % 2, g, :], k.selfw[:, :], start=True, stop=True)
                    last.then_inc(own_ready, 1)

                pipeline(pe, BLOCKS, [(0, turn_rows), (1, multiply)], U, TAIL)


def add_relations(nc, k, name, o, other):
    with Phase(nc, name) as ph:
        U = 8
        HALF = RELS // 2
        idx = ph.sb("idx", [P, U, 1], I32)
        idx_to = ph.sb("idx_to", [P, U, 1], I32)
        rows = [ph.sb(f"rows{u}", [P, D]) for u in range(U)]
        rel = ph.sb("rel", [P, C, RELS])
        turned_sb = ph.sb("turned_sb", [P, 2, D])
        masked = ph.sb("masked", [P, 2, HALF, D])
        pairs = ph.sb("pairs", [P, 2, 2, D])
        chosen = ph.sb("chosen", [P, 4, D])
        state = ph.sb("state", [P, U, D])
        turned = [ph.ps(f"turned{j}", [P, D]) for j in range(2)]
        low = [ph.ps(f"low{j}", [P, HALF, D]) for j in range(2)]
        high = [ph.ps(f"high{j}", [P, HALF, D]) for j in range(2)]
        idx_ready, to_ready, turned_ready, turned_kept, low_ready, high_ready = (
            ph.sem(n) for n in ("idx_ready", "to_ready", "turned_ready", "turned_kept", "low_ready", "high_ready"))
        masks_made, masked_ready, paired, carried, low_step, picked = (ph.sem(n) for n in ("masks_made", "masked_ready", "paired", "carried", "low_step", "picked"))
        gathered = [ph.sem(f"gathered{u}") for u in range(U)]
        added = [ph.sem(f"added{u}") for u in range(U)]
        of = lambda c, r: rel[:, ds(c), r:r + 1].rearrange("p a b -> p (a b)")

        with nc.Block() as block:
            @block.gpsimd
            def _(pool):
                def gather(c, u, turn):
                    ph.held(pool, idx_ready, c + 1)
                    ph.held(pool, turned_ready, c - U + 1)
                    pool.indirect_dma_start(rows[u][:, :], None, k.h,
                                            bass.IndirectOffsetOnAxis(ap=idx[:, u, :], axis=0)).then_inc(gathered[u], 16)

                def add(c, u, turn):
                    ph.held(pool, picked, c + 1)
                    ph.held(pool, to_ready, c + 1)
                    pool.indirect_dma_start(k.x, bass.IndirectOffsetOnAxis(ap=idx_to[:, u, :], axis=0), state[:, u, :],
                                            None, compute_op=ALU.add).then_inc(added[u], 16)

                pipeline(pool, C, [(0, gather), (7, add)], U)
                for u in range(U):
                    pool.wait_ge(added[u], 16 * C // U)

            @block.vector
            def _(dve):
                for r in range(RELS):
                    last = nc.vector.tensor_scalar(rel[:, :, r], o.rec[:, :, TYPE], float(r), None, ALU.is_equal)
                nc.vector.memset(state[:, U - 1, :], 0.0).then_inc(masks_made, 1)
                dve.wait_ge(masks_made, 1)

                def choose(r):
                    def step(c, u, turn):
                        s = u % 2
                        if r == 0:
                            wait(dve, low_ready, c + 1)
                            nc.vector.tensor_scalar(chosen[:, u % 4, :], low[s][:, 0, :], of(c, 0), None, ALU.mult)\
                                .then_inc(low_step, 1)
                        else:
                            wait(dve, low_step, HALF * c + r)
                            nc.vector.scalar_tensor_tensor(chosen[:, u % 4, :], low[s][:, r, :], of(c, r), chosen[:, u % 4, :],
                                                           ALU.mult, ALU.add).then_inc(low_step, 1)
                    return step

                def pair_up(c, u, turn):
                    s = u % 2
                    wait(dve, masked_ready, c + 1)
                    nc.vector.tensor_tensor(pairs[:, s], masked[:, s, 0:2, :], masked[:, s, 2:4, :], ALU.add)\
                        .then_inc(paired, 1)

                def carry(c, u, turn):
                    wait(dve, picked, c)
                    wait(dve, paired, c + 1)
                    wait(dve, added[u], 16 * turn)
                    nc.vector.scalar_tensor_tensor(state[:, u, :], state[:, (u - 1) % U, :], o.same[:, ds(c)],
                                                   pairs[:, u % 2, 0, :], ALU.mult, ALU.add).then_inc(carried, 1)

                def add_pair(c, u, turn):
                    wait(dve, carried, 2 * c + 1)
                    nc.vector.tensor_tensor(state[:, u, :], state[:, u, :], pairs[:, u % 2, 1, :], ALU.add)\
                        .then_inc(carried, 1)

                def add_chosen(c, u, turn):
                    wait(dve, carried, 2 * c + 2)
                    wait(dve, low_step, HALF * (c + 1))
                    nc.vector.tensor_tensor(state[:, u, :], state[:, u, :], chosen[:, u % 4, :], ALU.add)\
                        .then_inc(picked, 1)

                pipeline(dve, C, [(0, choose(0)), (1, pair_up), (0, choose(1)), (1, carry), (0, choose(2)),
                                  (1, add_pair), (0, choose(3)), (1, add_chosen)], U)

            @block.scalar
            def _(act):
                act.wait_ge(masks_made, 1)

                def index(c, u, turn):
                    ph.held(act, gathered[u], 16 * turn)
                    act.copy(idx[:, u:u + 1, :], o.ends[:, ds(c), other:other + 1]).then_inc(idx_ready, 1)

                def keep(c, u, turn):
                    wait(act, turned_ready, c + 1)
                    wait(act, low_ready, c - 1)
                    act.copy(turned_sb[:, u % 2, :], turned[u % 2][:, :]).then_inc(turned_kept, 1)

                def mask_high(c, u, turn):
                    ph.held(act, added[u], 16 * turn)
                    act.copy(idx_to[:, u:u + 1, :], o.target[:, ds(c)].rearrange("p (a c) -> p a c", a=1))\
                        .then_inc(to_ready, 1)
                    ph.held(act, high_ready, c + 1)
                    ph.held(act, paired, c - 1)
                    for r in range(HALF):
                        last = act.activation(masked[:, u % 2, r, :], high[u % 2][:, r, :], ACT.Copy, scale=of(c, HALF + r))
                    last.then_inc(masked_ready, 1)

                pipeline(act, C, [(0, index), (4, keep), (5, mask_high)], U)

            @block.tensor
            def _(pe):
                def turn_rows(c, u, turn):
                    wait(pe, gathered[u], 16 * (turn + 1))
                    wait(pe, turned_kept, c - 1)
                    pe.transpose(turned[u % 2][:, :], rows[u][:, :], k.ident[:, :]).then_inc(turned_ready, 1)

                def multiply(c, u, turn):
                    s = u % 2
                    wait(pe, turned_kept, c + 1)
                    wait(pe, masked_ready, c - 1)
                    pe.matmul(high[s][:, :, :], turned_sb[:, s, :], k.rel[:, HALF:RELS, :], start=True, stop=True)\
                        .then_inc(high_ready, 1)
                    wait(pe, low_step, HALF * (c - 1))
                    pe.matmul(low[s][:, :, :], turned_sb[:, s, :], k.rel[:, 0:HALF, :], start=True, stop=True)\
                        .then_inc(low_ready, 1)

                pipeline(pe, C, [(0, turn_rows), (1, multiply)], U)


def last_norm(nc, k):
    with Phase(nc, "norm3") as ph:
        U = 8
        x = ph.sb("x", [P, U, G, D])
        h = ph.sb("h", [P, U, G, D])
        xb = ph.sb("xb", [P, U, G, D])
        m = moments_of(ph, "m", U)
        x_in = [ph.sem(f"x_in{u}") for u in range(U)]
        out_h = [ph.sem(f"out_h{u}") for u in range(U)]
        h_done, biased = ph.sem("h_done"), ph.sem("biased")
        bo = spread(k.bo[:, :].rearrange("p (g d) -> p g d", g=1), 1, G)

        with nc.Block() as block:
            @block.sync
            def _(sp):
                def load(i, s, turn):
                    wait(sp, biased, i - U + 1)
                    sp.dma_start(block_tile(x, s, i), block_rows(k.x, i)).then_inc(x_in[s], 16)

                def store(i, s, turn):
                    wait(sp, h_done, i + 1)
                    sp.dma_start(block_rows(k.h, i), block_tile(h, s, i)).then_inc(out_h[s], 16)

                pipeline(sp, BLOCKS, [(0, load), (5, store)], U, TAIL)
                for s in range(U):
                    sp.wait_ge(out_h[s], 16 * len(range(s, BLOCKS, U)))

            @block.vector
            def _(dve):
                def stats(i, s, turn):
                    wait(dve, x_in[s], 16 * (turn + 1))
                    wait(dve, h_done, i - U + 1)
                    nc.vector.tensor_tensor(xb[:, s], x[:, s], bo, ALU.add).then_inc(biased, 1)
                    wait(dve, biased, i + 1)
                    dense_stats(nc, ph, dve, m, s, i, xb[:, s])

                def scales(i, s, turn):
                    row_scales(nc, dve, m, s, i)

                pipeline(dve, BLOCKS, [(0, stats), (1, scales)], U, TAIL)

            @block.scalar
            def _(act):
                def roots(i, s, turn):
                    row_roots(act, k, m, s, i)

                def relu(i, s, turn):
                    wait(act, out_h[s], 16 * turn)
                    wait(act, m.ready, i + 1)
                    for g in range(G):
                        last = act.activation(h[:, s, g, :], xb[:, s, g, :], ACT.Relu,
                                              bias=m.shift[:, s, g:g + 1], scale=m.scale[:, s, g:g + 1])
                    last.then_inc(h_done, 1)

                pipeline(act, BLOCKS, [(0, roots), (1, relu)], U, TAIL)


def sum_neighbours(nc, k, name, o):
    with Phase(nc, name) as ph:
        U = 4
        idx = ph.sb("idx", [P, U, 1], I32)
        idx_to = ph.sb("idx_to", [P, U, 1], I32)
        rows = [ph.sb(f"rows{u}", [P, D]) for u in range(U)]
        state = ph.sb("state", [P, U, SUMW])
        idx_ready, to_ready, tails, summed, v_step = (ph.sem(n) for n in ("idx_ready", "to_ready", "tails", "summed", "v_step"))
        gathered = [ph.sem(f"gathered{u}") for u in range(U)]
        stored = [ph.sem(f"stored{u}") for u in range(U)]

        with nc.Block() as block:
            @block.gpsimd
            def _(pool):
                def gather(c, u, turn):
                    ph.held(pool, idx_ready, c + 1)
                    ph.held(pool, summed, c - U + 1)
                    pool.indirect_dma_start(rows[u][:, :], None, k.h,
                                            bass.IndirectOffsetOnAxis(ap=idx[:, u, :], axis=0)).then_inc(gathered[u], 16)

                def store(c, u, turn):
                    ph.held(pool, summed, c + 1)
                    ph.held(pool, to_ready, c + 1)
                    pool.indirect_dma_start(k.sums, bass.IndirectOffsetOnAxis(ap=idx_to[:, u, :], axis=0),
                                            state[:, u, :], None).then_inc(stored[u], 16)

                pipeline(pool, C, [(0, gather), (3, store)], U)
                for u in range(U):
                    pool.wait_ge(stored[u], 16 * C // U)

            @block.vector
            def _(dve):
                nc.vector.memset(state[:, U - 1, :], 0.0).then_inc(v_step, 1)
                dve.wait_ge(v_step, 1)

                def index(c, u, turn):
                    ph.held(dve, gathered[u], 16 * turn)
                    nc.vector.tensor_copy(idx[:, u:u + 1, :], o.ends[:, ds(c), 1:2]).then_inc(idx_ready, 1)

                def add(c, u, turn):
                    ph.held(dve, stored[u], 16 * turn)
                    nc.vector.tensor_copy(idx_to[:, u:u + 1, :], o.target[:, ds(c)].rearrange("p (a c) -> p a c", a=1))\
                        .then_inc(to_ready, 1)
                    ph.held(dve, summed, c)
                    same = o.same[:, ds(c)]
                    nc.vector.scalar_tensor_tensor(state[:, u, D:SUMW], state[:, (u - 1) % U, D:SUMW], same,
                                                   o.tail[:, ds(c), :].rearrange("p a b -> p (a b)"),
                                                   ALU.mult, ALU.add)
                    wait(dve, gathered[u], 16 * (turn + 1))
                    nc.vector.scalar_tensor_tensor(state[:, u, 0:D], state[:, (u - 1) % U, 0:D], same, rows[u][:, :],
                                                   ALU.mult, ALU.add).then_inc(summed, 1)

                pipeline(dve, C, [(0, index), (3, add)], U)


def update_nodes(nc, k, A, out, r):
    final = r == 1
    with Phase(nc, f"gru{r}") as ph:
        U = 8
        h = ph.sb("h", [P, U, G, D])
        su = ph.sb("su", [P, U, G, SUMW])
        x = ph.sb("x", [P, U, G, D]) if final else None
        dh = ph.sb("dh", [P, 2, G, D])
        wd_in = ph.sb("wd_in", [P, 2, G, 2])
        t_sb = ph.sb("t_sb", [P, 2, 2, G, D])
        h_sb = ph.sb("h_sb", [P, 4, 2, G, D], F32R)
        wih, whh = ph.sb("wih", [P, 2, 384], F32R), ph.sb("whh", [P, 2, 384], F32R)
        w_up = ph.sb("w_up", [P, 2, 384])
        h_up, agg_up = ph.sb("h_up", [P, G, D]), ph.sb("agg_up", [P, G, P])
        wd_sb = ph.sb("wd_sb", [2 * G, 2, P])
        agg_sb = ph.sb("agg_sb", [P, 2, 2, G, P], F32R)
        rz = ph.sb("rz", [P, 2, G, 2 * D])
        t1 = ph.sb("t1", [P, 2, D])
        cand = ph.sb("cand", [P, 2, G, D])
        n = ph.sb("n", [P, 2, G, D])
        change = ph.sb("change", [P, 2, G, D])
        ho = ph.sb("ho", [P, U, G, D])
        turned = [ph.ps(f"turned{j}", [P, G, P]) for j in range(3)]
        wd = ph.ps("wd", [2 * G, P])
        agg = ph.ps("agg", [P, G, P])
        gate = [ph.ps(f"gate{j}", [P, 512]) for j in range(2)]
        h_in = [ph.sem(f"h_in{u}") for u in range(U)]
        h_out = [ph.sem(f"h_out{u}") for u in range(U)]
        scaled, turned_ready, turned_kept, agg_ready = (ph.sem(s) for s in ("scaled", "turned_ready", "turned_kept", "agg_ready"))
        pairs_ready, h_upper, h_lower, h_kept, agg_upper, agg_lower, agg_kept, summed = (
            ph.sem(s) for s in ("pairs_ready", "h_upper", "h_lower", "h_kept", "agg_upper", "agg_lower", "agg_kept", "summed"))
        w_split = ph.sem("w_split")
        gate_ready, rz_ready, gated, cand_ready, n_ready = (ph.sem(s) for s in ("gate_ready", "rz_ready", "gated", "cand_ready", "n_ready"))
        changed, weighed, x_biased, block_done = (ph.sem(s) for s in ("changed", "weighed", "x_biased", "block_done"))
        bo = spread(k.bo[:, :].rearrange("p (g d) -> p g d", g=1), 1, G)
        loads = 3 if final else 2

        with nc.Block() as block:
            @block.sync
            def _(sp):
                def load(i, s, turn):
                    wait(sp, block_done, i - U + 1)
                    sp.dma_start(block_tile(h, s, i), block_rows(k.h, i)).then_inc(h_in[s], 16)
                    sp.dma_start(block_tile(su, s, i), block_rows(k.sums, i, SUMW)).then_inc(h_in[s], 16)
                    if final:
                        sp.dma_start(block_tile(x, s, i), block_rows(k.x, i)).then_inc(h_in[s], 16)

                def store(i, s, turn):
                    wait(sp, block_done, i + 1)
                    sp.dma_start(block_rows(out if final else k.h, i), block_tile(ho, s, i)).then_inc(h_out[s], 16)

                pipeline(sp, BLOCKS, [(0, load), (7, store)], U, TAIL)
                for s in range(U):
                    sp.wait_ge(h_out[s], 16 * len(range(s, BLOCKS, U)))

            @block.vector
            def _(dve):
                link = Chain(dve, w_split)
                for j, (parts, w) in enumerate(((wih, k.wih), (whh, k.whh))):
                    link(split_upper(nc, w_up[:, j, :], w[:, r, :]))
                    link(nc.vector.tensor_copy(parts[:, 0, :], w_up[:, j, :]))
                    link(nc.vector.tensor_tensor(parts[:, 1, :], w[:, r, :], w_up[:, j, :], ALU.subtract))

                def split_h(i, s, turn):
                    wait(dve, turned_ready, i + 1)
                    wait(dve, gate_ready, G * (i - 3))
                    wait(dve, h_kept, i)
                    split_upper(nc, h_up[:, :, :], turned[2][:, :, :]).then_inc(h_upper, 1)
                    wait(dve, h_upper, i + 1)
                    nc.vector.tensor_tensor(h_sb[:, s % 4, 1], turned[2][:, :, :], h_up[:, :, :], ALU.subtract)\
                        .then_inc(h_lower, 1)

                def split_agg(i, s, turn):
                    wait(dve, agg_ready, i + 1)
                    wait(dve, gate_ready, G * (i - 1))
                    wait(dve, agg_kept, i)
                    split_upper(nc, agg_up[:, :, :], agg[:, :, :]).then_inc(agg_upper, 1)
                    wait(dve, agg_upper, i + 1)
                    nc.vector.tensor_tensor(agg_sb[:, s % 2, 1], agg[:, :, :], agg_up[:, :, :], ALU.subtract)\
                        .then_inc(agg_lower, 1)

                def candidate(g):
                    def step(i, s, turn):
                        b = s % 2
                        wait(dve, rz_ready, i * G + g + 1)
                        nc.vector.tensor_tensor(t1[:, g % 2, :], gate[g % 2][:, 384:512], rz[:, b, g, 0:D], ALU.mult)\
                            .then_inc(gated, 1)
                        wait(dve, gated, i * G + g + 1)
                        nc.vector.tensor_tensor(cand[:, b, g, :], gate[g % 2][:, 0:128], t1[:, g % 2, :], ALU.add)\
                            .then_inc(cand_ready, 1)
                    return step

                def subtract(i, s, turn):
                    wait(dve, n_ready, i + 1)
                    nc.vector.tensor_tensor(change[:, s % 2], h[:, s], n[:, s % 2], ALU.subtract).then_inc(changed, 1)

                def add_x(i, s, turn):
                    wait(dve, x_biased, i + 1)
                    nc.vector.tensor_tensor(x[:, s], x[:, s], n[:, s % 2], ALU.add).then_inc(summed, 1)

                def weigh(i, s, turn):
                    b = s % 2
                    wait(dve, changed, i + 1)
                    nc.vector.tensor_tensor(change[:, b], change[:, b], rz[:, b, :, D:2 * D], ALU.mult).then_inc(weighed, 1)

                def add(i, s, turn):
                    b = s % 2
                    wait(dve, h_out[s], 16 * turn)
                    if final:
                        wait(dve, summed, i + 1)
                    wait(dve, weighed, i + 1)
                    nc.vector.tensor_tensor(ho[:, s], change[:, b], x[:, s] if final else n[:, b], ALU.add)\
                        .then_inc(block_done, 1)

                stages = [(1, split_h), (2, split_agg), (3, candidate(0)), (4, subtract), (3, candidate(1))]
                stages += [(4, add_x)] if final else []
                stages += [(3, candidate(2)), (4, weigh), (3, candidate(3)), (4, add)]
                pipeline(dve, BLOCKS, stages, U, TAIL)

            @block.gpsimd
            def _(pool):
                def scale_rows(i, s, turn):
                    wait(pool, h_in[s], 16 * loads * (turn + 1))
                    wait(pool, turned_ready, i - 1)
                    nc.gpsimd.tensor_tensor(dh[:, s % 2], h[:, s], spread(su[:, s, :, D + 1:D + 2], 2, D), ALU.mult)\
                        .then_inc(scaled, 1)
                    if final:
                        nc.gpsimd.tensor_tensor(x[:, s], x[:, s], bo, ALU.add).then_inc(x_biased, 1)

                pipeline(pool, BLOCKS, [(0, scale_rows)], U, TAIL)

            @block.tensor
            def _(pe):
                pe.wait_ge(w_split, 6)

                def turn_rows(i, s, turn):
                    wait(pe, scaled, i + 1)
                    wait(pe, pairs_ready, i + 1)
                    wait(pe, turned_kept, i)
                    wait(pe, h_lower, i)
                    for g in range(G):
                        pe.transpose(turned[0][:, g, :], su[:, s, g, 0:D], k.ident[:, :])
                        pe.transpose(turned[1][:, g, :], dh[:, s % 2, g, :], k.ident[:, :])
                        pe.transpose(turned[2][:, g, :], h[:, s, g, :], k.ident[:, :])
                    pe.transpose(wd[:, :], wd_in[:, s % 2, :, :], k.ident[:, :]).then_inc(turned_ready, 1)

                def aggregate(i, s, turn):
                    wait(pe, turned_kept, i + 1)
                    wait(pe, agg_lower, i)
                    pe.matmul(agg[:, :, :], k.msg[:, r, 0, :], t_sb[:, s % 2, 0, :, :], start=True, stop=False)
                    pe.matmul(agg[:, :, :], k.msg[:, r, 1, :], t_sb[:, s % 2, 1, :, :], start=False, stop=False)
                    for g in range(G):
                        last = pe.matmul(agg[:, g, :], k.wb[:, r, g, :], wd_sb[:, s % 2, :], start=False, stop=(g == G - 1))
                    last.then_inc(agg_ready, 1)

                def gates(i, s, turn):
                    wait(pe, agg_lower, i + 1)
                    wait(pe, agg_kept, i + 1)
                    wait(pe, h_lower, i + 1)
                    wait(pe, h_kept, i + 1)
                    for g in range(G):
                        j, q = g % 2, i * G + g
                        wait(pe, cand_ready, q - 1)
                        pe.matmul(gate[j][:, :], k.onesb[0:3, :], k.bias3[:, 2 + r, :], start=True, stop=False)
                        for part, w in ((0, 0), (1, 0), (0, 1)):
                            sums = agg_sb[:, s % 2, part, g, :]
                            rows = h_sb[:, s % 4, part, g, :]
                            pe.matmul(gate[j][:, 0:384], sums, wih[:, w, :], start=False, stop=False)
                            last = pe.matmul(gate[j][:, 128:512], rows, whh[:, w, :], start=False, stop=(w == 1))
                        last.then_inc(gate_ready, 1)

                pipeline(pe, BLOCKS, [(1, turn_rows), (2, aggregate), (3, gates)], U, TAIL)

            @block.scalar
            def _(act):
                def pairs(i, s, turn):
                    wait(act, h_in[s], 16 * loads * (turn + 1))
                    wait(act, turned_ready, i - 1)
                    act.copy(wd_in[:, s % 2], su[:, s, :, D:SUMW]).then_inc(pairs_ready, 1)

                def keep(i, s, turn):
                    wait(act, turned_ready, i + 1)
                    wait(act, agg_ready, i - 1)
                    act.copy(t_sb[:, s % 2, 0], turned[0][:, :, :])
                    act.copy(t_sb[:, s % 2, 1], turned[1][:, :, :])
                    act.copy(wd_sb[:, s % 2, :], wd[:, :]).then_inc(turned_kept, 1)

                def keep_h(i, s, turn):
                    wait(act, h_upper, i + 1)
                    wait(act, gate_ready, G * (i - 3))
                    act.copy(h_sb[:, s % 4, 0], h_up[:, :, :]).then_inc(h_kept, 1)

                def keep_agg(i, s, turn):
                    wait(act, agg_upper, i + 1)
                    wait(act, gate_ready, G * (i - 1))
                    act.copy(agg_sb[:, s % 2, 0], agg_up[:, :, :]).then_inc(agg_kept, 1)

                def gates(i, s, turn):
                    wait(act, weighed, i - 1)
                    for g in range(G):
                        wait(act, gate_ready, i * G + g + 1)
                        act.activation(rz[:, s % 2, g, :], gate[g % 2][:, 128:384], ACT.Sigmoid).then_inc(rz_ready, 1)
                    wait(act, cand_ready, G * (i + 1))
                    wait(act, block_done, i - 1)
                    act.activation(n[:, s % 2], cand[:, s % 2], ACT.Tanh).then_inc(n_ready, 1)

                pipeline(act, BLOCKS, [(0, pairs), (1, keep), (1, keep_h), (2, keep_agg), (3, gates)], U, TAIL)


def build(nc, A, out):
    k = Group()
    sb = lambda name, shape, dt=F32: nc.alloc_sbuf_tensor(name, shape, dt)
    table = lambda name, rows, width: nc.dram_tensor(name, (rows, width), F32, kind="Internal").ap()
    k.x, k.h, k.xn = table("x_rows", ROWS, D), table("h_rows", NODES + P, D), table("xn_rows", NODES + P, D)
    k.sums = table("sum_rows", ROWS, SUMW)
    k.edge_table = [table(f"edge_rows{j}", P * C, REC) for j in range(4)]
    k.ident, k.identb = sb("ident", [P, P]), sb("identb", [P, P], BF16)
    k.before, k.below = sb("before", [P, P], BF16), sb("below", [P, P])
    k.ones, k.onesb = sb("ones", [P, P]), sb("onesb", [P, P], BF16)
    k.iota, k.dummy, k.fix = sb("iota", [P, BUCKETS], BF16), sb("dummy_rows", [P, C]), sb("fix", [P, 4])
    k.l0, k.l2 = Group(), Group()
    k.l0.w, k.l0.wo, k.l0.bias = sb("w0", [P, 384]), sb("wo0", [P, D]), 0
    k.l2.w, k.l2.wo, k.l2.bias = sb("w2", [P, 384]), sb("wo2", [P, D]), 1
    k.rel, k.selfw = sb("rel", [P, RELS + 1, D]), sb("selfw", [P, D])
    k.msg, k.wb = sb("msg", [P, 2, 2, D]), sb("wb", [2 * G, 2, G, D])
    k.wih, k.whh = sb("wih", [P, 2, 384]), sb("whh", [P, 2, 384])
    k.bias3 = sb("bias3", [3, 4, 512], BF16)
    k.b_out, k.bo = sb("b_out", [P, D]), sb("bo", [P, D])
    k.eps = sb("eps", [P, 1])

    def order(sb, name, key):
        mask = lambda n: sb(f"{name}_{n}", [P, C])
        seq = lambda n: sb(f"{name}_{n}", [HEADS, 2 * P])
        o = Group()
        o.key, o.rec = key, sb(f"{name}_rec", [P, C, REC])
        o.ends, o.tail = sb(f"{name}_ends", [P, C, 2], I32), sb(f"{name}_tail", [P, C, 2])
        o.target, o.fix_target = sb(f"{name}_target", [P, C], I32), sb(f"{name}_fix", [P, 2], I32)
        o.split, o.join = sb(f"{name}_split", [P, 1]), sb(f"{name}_join", [P, 2, 2, P])
        o.same, o.notlast, o.last, o.pen = mask("same"), mask("notlast"), mask("last"), mask("pen")
        o.first, o.final, o.middle = mask("first"), mask("final"), mask("middle")
        o.seq_same, o.seq_pen = seq("seq_same"), seq("seq_pen")
        o.seq_last, o.seq_notlast = seq("seq_last"), seq("seq_notlast")
        return o

    by_src = order(sb, "src", KEY_SRC)
    graph = ExitStack()
    held = lambda name, shape, dt=F32: graph.enter_context(nc.sbuf_tensor(name, shape, dt))
    by_dst = order(held, "dst", KEY_DST)

    with ExitStack() as sorting:
        for_sorting = lambda name, shape, dt=F32: sorting.enter_context(nc.sbuf_tensor(name, shape, dt))
        k.rec0 = for_sorting("rec0", [P, C, REC])
        prepare(nc, k, A)
        passes = []
        for shift in (0, 8):
            for j, o in enumerate((by_src, by_dst)):
                p = Group()
                p.key, p.shift = o.key, shift
                p.rec_in = passes[j].rec_out if shift else k.rec0
                p.table = k.edge_table[len(passes)]
                p.rec_out = o.rec if shift else for_sorting(f"rec_mid{j}", [P, C, REC])
                p.digit, p.own = for_sorting(f"digit{j}{shift}", [P, C]), for_sorting(f"own{j}{shift}", [P, BUCKETS], BF16)
                passes.append(p)
        count_digits(nc, k, "count", passes[0])
        for j, p in enumerate(passes):
            sort_pass(nc, k, f"sort{j}", p, passes[j + 1] if j < 3 else None)
    order_masks(nc, k, "src_masks", by_src)
    order_masks(nc, k, "dst_masks", by_dst)
    first_norm(nc, k, A)

    k.att = held("att", [P, HEADS, C])
    with nc.sbuf_tensor("edge_v0", [P, C, D], F32) as k.edge_v:
        edge_scores(nc, k, "score0", by_dst, k.xn, k.l0, False)
        segment_softmax(nc, k, "soft0", by_dst, float(D) ** -0.5, True)
        add_attention(nc, k, "att0", by_dst, k.l0.wo)
    join_parts(nc, k, "join0", by_dst, k.x, D, True)
    self_relation(nc, k)
    add_relations(nc, k, "rel_dst", by_dst, 0)
    join_parts(nc, k, "join1", by_dst, k.x, D, True)
    add_relations(nc, k, "rel_src", by_src, 1)
    join_parts(nc, k, "join2", by_src, k.x, D, True)
    with nc.sbuf_tensor("edge_v2", [P, C, D], F32) as k.edge_v:
        edge_scores(nc, k, "score2", by_dst, k.x, k.l2, True)
        segment_softmax(nc, k, "soft2", by_dst, float(HD) ** -0.5, False)
        add_attention(nc, k, "att2", by_dst, k.l2.wo)
    join_parts(nc, k, "join3", by_dst, k.x, D, True)
    graph.close()
    last_norm(nc, k)
    for r in range(2):
        sum_neighbours(nc, k, f"sum{r}", by_src)
        join_parts(nc, k, f"joins{r}", by_src, k.sums, SUMW, False)
        update_nodes(nc, k, A, out, r)


INPUTS = ["x", "src", "dst", "edge_attr_8", "edge_attr_8_n2", "edge_type_8", "edge_weight1", "L0_gnn_gamma",
          "L0_gnn_beta", "L0_gnn_W_qkv", "L0_gnn_b_qkv", "L0_gnn_W_out", "L0_gnn_b_out", "L1_gnn_blocks",
          "L2_gnn_Wq", "L2_gnn_bq", "L2_gnn_Wk", "L2_gnn_bk", "L2_gnn_Wv", "L2_gnn_bv", "L2_gnn_Wo", "L2_gnn_bo",
          "L3_gnn_msg_W", "L3_gnn_msg_b", "L3_gnn_gru_Wih", "L3_gnn_gru_Whh", "L3_gnn_gru_bih", "L3_gnn_gru_bhh"]


def kernel(**inputs):
    import concourse.bacc as bacc
    from concourse.bass_utils import run_bass_kernel_spmd

    nc = bacc.Bacc("TRN2", target_bir_lowering=False, num_devices=1)
    arrays, args = {}, {}
    for name in INPUTS:
        a = np.ascontiguousarray(inputs[name])
        arrays[f"in_{name}"] = a
        args[name] = nc.dram_tensor(f"in_{name}", a.shape, mybir.dt.from_np(a.dtype), kind="ExternalInput").ap()
    out = nc.dram_tensor("out_x", (NODES, D), F32, kind="ExternalOutput").ap()
    build(nc, args, out)
    r = run_bass_kernel_spmd(nc, [arrays], core_ids=[0])
    return r.results[0]["out_x"]
```
